# Optimizing a Trainium2 kernel written in Bass

```python
import numpy as np
import jax
import jax.numpy as jnp

def _softmax(x, axis=-1):
    return jax.nn.softmax(x, axis=axis)

def _gelu(x):
    return jax.nn.gelu(x, approximate=True)

def _silu(x):
    return jax.nn.silu(x)

def _sigmoid(x):
    return jax.nn.sigmoid(x)

def _layernorm(x, axis=-1, eps=1e-05):
    m = jnp.mean(x, axis=axis, keepdims=True)
    v = jnp.var(x, axis=axis, keepdims=True)
    return (x - m) / jnp.sqrt(v + eps)

def _scatter_add(tgt, idx, src, axis=0):
    return tgt.at[idx].add(src)

def _segment_sum(src, seg, n):
    return jax.ops.segment_sum(src, seg, n)
kernel_name = 'mk_adaln_d1_jaxref_r4_122d72'

def setup_inputs(seed: int=0):
    np.random.seed(seed)
    _w = jnp.asarray

    def _L0_attn_setup():
        import jax, jax.numpy as jnp
        import numpy as np
        EMBED_DIM = 256
        NUM_HEADS = 16
        DEPTH = 12
        HEAD_DIM = EMBED_DIM // NUM_HEADS // 2
        LAMBDA_INIT = float(0.8 - 0.6 * np.exp(-0.3 * DEPTH))
        B, T = (2, 512)
        key = jax.random.key(seed)
        ks = jax.random.split(key, 10)
        s = 0.02
        return {'query': jax.random.normal(ks[0], (B, T, EMBED_DIM), jnp.float32), 'Wq': jax.random.normal(ks[1], (EMBED_DIM, EMBED_DIM), jnp.float32) * s, 'Wk': jax.random.normal(ks[2], (EMBED_DIM, EMBED_DIM), jnp.float32) * s, 'Wv': jax.random.normal(ks[3], (EMBED_DIM, EMBED_DIM), jnp.float32) * s, 'Wo': jax.random.normal(ks[4], (EMBED_DIM, EMBED_DIM), jnp.float32) * s, 'lambda_q1': jax.random.normal(ks[5], (HEAD_DIM,), jnp.float32) * 0.1, 'lambda_k1': jax.random.normal(ks[6], (HEAD_DIM,), jnp.float32) * 0.1, 'lambda_q2': jax.random.normal(ks[7], (HEAD_DIM,), jnp.float32) * 0.1, 'lambda_k2': jax.random.normal(ks[8], (HEAD_DIM,), jnp.float32) * 0.1, 'subln_w': jnp.ones((2 * HEAD_DIM,), jnp.float32)}
    _L0_attn_in = _L0_attn_setup()

    def _L0_ffn_setup():
        import jax, jax.numpy as jnp
        import numpy as np
        B, T, D, E, H, K = (4, 512, 256, 8, 512, 2)
        key = jax.random.key(seed)
        k0, k1, k2, k3 = jax.random.split(key, 4)
        x = jax.random.normal(k0, (B, T, D), dtype=jnp.float32)
        router_w = jax.random.normal(k1, (E, D), dtype=jnp.float32) * D ** (-0.5)
        w1 = jax.random.normal(k2, (E, D, H), dtype=jnp.float32) * D ** (-0.5)
        w2 = jax.random.normal(k3, (E, H, D), dtype=jnp.float32) * H ** (-0.5)
        return {'x': x, 'router_w': router_w, 'w1': w1, 'w2': w2}
    _L0_ffn_in = _L0_ffn_setup()
    _L0_c = _w((lambda *s: np.random.randn(*s).astype(np.float32) * 0.05)(4, 256))
    _L0_wmod = _w((lambda *s: np.random.randn(*s).astype(np.float32) * 0.05)(256, 6 * 256) * 256 ** (-0.5))
    _d = {'L0_attn_query': _L0_attn_in['query'], 'L0_attn_Wq': _L0_attn_in['Wq'], 'L0_attn_Wk': _L0_attn_in['Wk'], 'L0_attn_Wv': _L0_attn_in['Wv'], 'L0_attn_Wo': _L0_attn_in['Wo'], 'L0_attn_lambda_q1': _L0_attn_in['lambda_q1'], 'L0_attn_lambda_k1': _L0_attn_in['lambda_k1'], 'L0_attn_lambda_q2': _L0_attn_in['lambda_q2'], 'L0_attn_lambda_k2': _L0_attn_in['lambda_k2'], 'L0_attn_subln_w': _L0_attn_in['subln_w'], 'L0_ffn_router_w': _L0_ffn_in['router_w'], 'L0_ffn_w1': _L0_ffn_in['w1'], 'L0_ffn_w2': _L0_ffn_in['w2'], 'L0_c': _L0_c, 'L0_wmod': _L0_wmod}
    _x0 = _d['L0_attn_query']
    _d['L0_attn_query'] = jax.random.normal(jax.random.fold_in(jax.random.key(seed), 1), (4, 1024, 256), dtype=_x0.dtype)
    del _x0
    return _d

def reference(L0_attn_query, L0_attn_Wq, L0_attn_Wk, L0_attn_Wv, L0_attn_Wo, L0_attn_lambda_q1, L0_attn_lambda_k1, L0_attn_lambda_q2, L0_attn_lambda_k2, L0_attn_subln_w, L0_ffn_router_w, L0_ffn_w1, L0_ffn_w2, L0_c, L0_wmod):

    def _L0_attn_ref(query, Wq, Wk, Wv, Wo, lambda_q1, lambda_k1, lambda_q2, lambda_k2, subln_w):
        import jax, jax.numpy as jnp
        import numpy as np
        EMBED_DIM = 256
        NUM_HEADS = 16
        DEPTH = 12
        HEAD_DIM = EMBED_DIM // NUM_HEADS // 2
        LAMBDA_INIT = float(0.8 - 0.6 * np.exp(-0.3 * DEPTH))
        B, T = (2, 512)
        Bsz, Tt, E = query.shape
        H, hd = (NUM_HEADS, HEAD_DIM)
        scaling = hd ** (-0.5)
        q = jnp.einsum('bte,fe->btf', query, Wq).reshape(Bsz, Tt, 2 * H, hd).transpose(0, 2, 1, 3)
        k = jnp.einsum('bse,fe->bsf', query, Wk).reshape(Bsz, Tt, 2 * H, hd).transpose(0, 2, 1, 3)
        v = jnp.einsum('bse,fe->bsf', query, Wv).reshape(Bsz, Tt, H, 2 * hd).transpose(0, 2, 1, 3)
        q = q * scaling
        scores = jnp.einsum('bhtd,bhsd->bhts', q, k)
        attn_w = jax.nn.softmax(scores.astype(jnp.float32), axis=-1).astype(q.dtype)
        lam1 = jnp.exp(jnp.sum(lambda_q1 * lambda_k1))
        lam2 = jnp.exp(jnp.sum(lambda_q2 * lambda_k2))
        lam = lam1 - lam2 + LAMBDA_INIT
        aw = attn_w.reshape(Bsz, H, 2, Tt, Tt)
        aw = aw[:, :, 0] - lam * aw[:, :, 1]
        attn = jnp.einsum('bhts,bhsd->bhtd', aw, v)
        x32 = attn.astype(jnp.float32)
        normed = (x32 * jax.lax.rsqrt(jnp.mean(x32 * x32, axis=-1, keepdims=True) + 1e-05)).astype(attn.dtype)
        attn = normed * subln_w
        attn = attn * (1.0 - LAMBDA_INIT)
        out = attn.transpose(0, 2, 1, 3).reshape(Bsz, Tt, H * 2 * hd)
        return jnp.einsum('bte,fe->btf', out, Wo)

    def _L0_ffn_ref(x, router_w, w1, w2):
        import jax, jax.numpy as jnp
        import numpy as np
        B, T, D, E, H, K = (4, 512, 256, 8, 512, 2)
        Bb, Tt, Dd = x.shape
        N = Bb * Tt
        logits = jnp.einsum('btd,ed->bte', x, router_w)
        top_vals, top_idx = jax.lax.top_k(logits, K)
        top_w = jax.nn.softmax(top_vals, axis=-1)
        xf = x.reshape(N, Dd)
        h = jnp.einsum('nd,edh->enh', xf, w1)
        h = jnp.square(jax.nn.relu(h))
        y = jnp.einsum('enh,ehd->end', h, w2)
        idx_f = top_idx.reshape(N, K)
        w_f = top_w.reshape(N, K)
        y_sel = y[idx_f, jnp.arange(N)[:, None]]
        out = jnp.einsum('nk,nkd->nd', w_f, y_sel)
        return out.reshape(Bb, Tt, Dd)
    x = L0_attn_query
    mod = (_silu(L0_c) @ L0_wmod).reshape(L0_c.shape[0], 6, 1, -1)
    sa, ca, ga, sb, cb, gb = (mod[:, 0], mod[:, 1], mod[:, 2], mod[:, 3], mod[:, 4], mod[:, 5])
    ga = (2 * (ga >= 0) - 1) * jnp.maximum(jnp.abs(ga), 0.25)
    gb = (2 * (gb >= 0) - 1) * jnp.maximum(jnp.abs(gb), 0.25)
    h = _layernorm(x, axis=-1) * (1 + ca) + sa
    x = x + ga * _L0_attn_ref(h, L0_attn_Wq, L0_attn_Wk, L0_attn_Wv, L0_attn_Wo, L0_attn_lambda_q1, L0_attn_lambda_k1, L0_attn_lambda_q2, L0_attn_lambda_k2, L0_attn_subln_w)
    h = _layernorm(x, axis=-1) * (1 + cb) + sb
    x = x + gb * _L0_ffn_ref(h, L0_ffn_router_w, L0_ffn_w1, L0_ffn_w2)
    return x

_drawn_inputs = setup_inputs


def setup_inputs(seed=0):
    import zlib

    import numpy as np

    out = dict(_drawn_inputs(seed))
    spreads = {'L0_attn_subln_w': (1.0, 0.6)}
    factors = {'L0_attn_Wq': 2.776,
     'L0_attn_lambda_q1': 200.0,
     'L0_attn_lambda_k1': 8.0,
     'L0_attn_lambda_q2': 56.616,
     'L0_attn_lambda_k2': 54.752}
    for name, (base, spread) in spreads.items():
        noise = np.random.default_rng([zlib.crc32(name.encode()), seed]).standard_normal(out[name].shape)
        drawn = base * np.exp(spread * noise) if base else spread * noise
        out[name] = jnp.asarray(drawn.astype(out[name].dtype))
    for name, factor in factors.items():
        out[name] = (out[name] * factor).astype(out[name].dtype)
    return out
```

```python
from contextlib import ExitStack

import numpy as np
import concourse.bass as bass
from concourse import mybir

FP32 = mybir.dt.float32
BF16 = mybir.dt.bfloat16
U32 = mybir.dt.uint32
ALU = mybir.AluOpType
ACT = mybir.ActivationFunctionType
AX = mybir.AxisListType

P = 128
B, T, E = 4, 1024, 256
HEADS, HD = 16, 8
NEXP, HID = 8, 512
LAMBDA_INIT = float(0.8 - 0.6 * np.exp(-0.3 * 12))
EPS = 1e-5
RANGE = 2.0 ** 61
CE = E // P
CH = HID // P
BLK = 512
TT = BLK // P
ST = T // P
QUADS = B * HEADS // 2
QB = HEADS // 2
VW = 32
Q_PART = (0, 0, 0, 1, 1, 2)
K_PART = (0, 1, 2, 0, 1, 0)
SROWS = HD * len(Q_PART)
MROW = 64
NBUF = 4
LOAD_INC = 16 * 4


class Steps:

    def __init__(self, eng, sem, base=0):
        self.eng, self.sem, self.base, self.n = eng, sem, base, 0

    def done(self, ins):
        self.n += 1
        ins.then_inc(self.sem, 1)
        self.eng.wait_ge(self.sem, self.base + self.n)


def build(nc, x, wq, wk, wv, wo, lq1, lk1, lq2, lk2, subln, router, w1, w2, cond, wmod, out):
    top = ExitStack()
    with top:
        def sb(ctx, name, shape, dt=FP32):
            return ctx.enter_context(nc.sbuf_tensor(name, shape, dt))

        def pb(ctx, name, shape, dt=FP32):
            return ctx.enter_context(nc.psum_tensor(name, shape, dt))

        def sem(ctx, name):
            return ctx.enter_context(nc.semaphore(name))

        qd = nc.dram_tensor("q_stack", (QUADS, 4, SROWS, T), BF16, kind="Internal").ap()
        kd = nc.dram_tensor("k_stack", (QUADS, 4, SROWS, T), BF16, kind="Internal").ap()
        vd = nc.dram_tensor("v_quads", (QUADS, P, ST, 2 * VW), FP32, kind="Internal").ap()
        od = nc.dram_tensor("o_quads", (QUADS, P, T), FP32, kind="Internal").ap()
        modd = nc.dram_tensor("mod_rows", (B, 6 * E), FP32, kind="Internal").ap()

        ident = sb(top, "ident", [P, P])
        wT = {n: sb(top, f"{n}_T", [P, CE, E]) for n in ("wq", "wk", "wv", "wo")}
        rT = sb(top, "router_T", [P, CE, NEXP])
        lam_sign = sb(top, "lam_sign", [P, 2])
        subw = sb(top, "subw", [P, 16])
        neg_half = sb(top, "neg_half", [P, HEADS * TT])
        w1s = sb(top, "w1s", [P, NEXP, CE, HID])
        w2s = sb(top, "w2s", [P, NEXP, CH, E])
        w_loaded = sem(top, "w_loaded")

        setup(nc, top, sb, pb, sem, locals())
        project(nc, sb, pb, sem, locals())
        attend(nc, sb, pb, sem, locals())
        mix(nc, sb, pb, sem, locals())


def setup(nc, top, sb, pb, sem, g):
    with ExitStack() as c:
        wnat = {n: sb(c, f"{n}_nat", [P, CE, E]) for n in ("wq", "wk", "wv", "wo")}
        cT = sb(c, "cT", [P, CE, B])
        cexp = sb(c, "cexp", [P, CE, B])
        cden = sb(c, "cden", [P, CE, B])
        crec = sb(c, "crec", [P, CE, B])
        sT = sb(c, "sT", [P, CE, B])
        wm = sb(c, "wm", [P, CE, 6 * E])
        lv = sb(c, "lv", [P, 4, HD])
        lp = sb(c, "lp", [P, 2, HD])
        ls = sb(c, "ls", [P, 2])
        le = sb(c, "le", [P, 2])
        ld = sb(c, "ld", [P, 1])
        subn = sb(c, "subn", [P, 16])
        mod = sb(c, "mod", [B, 6 * E])
        gsign = sb(c, "gsign", [B, 2, E])
        gabs = sb(c, "gabs", [B, 2, E])
        wps = [pb(c, f"wps{i}", [P, CE, E]) for i in range(4)]
        mps = [pb(c, f"mps{i}", [P, 512]) for i in range(3)]
        w_in, c_in, s_id0, s_id = sem(c, "w_in"), sem(c, "c_in"), sem(c, "ident_zero"), sem(c, "ident_ready")
        mod_in, lam_in, small_in = sem(c, "mod_in"), sem(c, "lam_in"), sem(c, "small_in")
        w_turned, w_kept, e_ready, s_ready = sem(c, "w_turned"), sem(c, "w_kept"), sem(c, "e_ready"), sem(c, "s_ready")
        l_sum, l_exp, mod_ps, mod_ready, mod_out = (sem(c, n) for n in ("l_sum", "l_exp", "mod_ps", "mod_ready", "mod_out"))
        v_step = sem(c, "setup_v_step")
        block = c.enter_context(nc.Block())
        names = ("wq", "wk", "wv", "wo")

        @block.sync
        def _(sp):
            for ce in range(CE):
                sp.dma_start(cT[:, ce, :], g["cond"][:, ce * P:(ce + 1) * P].rearrange("b p -> p b"), allow_slow_non_contiguous=True).then_inc(c_in, 16)
            for n in names:
                sp.dma_start(wnat[n][:], g[n].rearrange("(c p) e -> p c e", p=P)).then_inc(w_in, 16)
            sp.dma_start(wm[:], g["wmod"].rearrange("(c p) n -> p c n", p=P)).then_inc(mod_in, 16)
            for i, v in enumerate(("lq1", "lk1", "lq2", "lk2")):
                sp.dma_start(lv[:, i, :], g[v].rearrange("(a n) -> a n", a=1).broadcast_to((P, HD))).then_inc(lam_in, 16)
            sp.dma_start(subn[:], g["subln"].rearrange("(a n) -> a n", a=1).broadcast_to((P, 16))).then_inc(lam_in, 16)
            for ce in range(CE):
                sp.dma_start(g["rT"][:, ce, :], g["router"][:, ce * P:(ce + 1) * P].rearrange("n p -> p n"), allow_slow_non_contiguous=True).then_inc(small_in, 16)
            sp.wait_ge(mod_ready, 1)
            sp.dma_start(g["modd"], mod[:]).then_inc(mod_out, 16)
            sp.wait_ge(mod_out, 16)
            sp.wait_ge(small_in, 16 * CE)

        @block.gpsimd
        def _(pool):
            pool.memset(g["ident"][:], 0.0).then_inc(s_id0, 1)
            pool.memset(g["neg_half"][:], -0.5)
            pool.wait_ge(s_id0, 1)
            pool.affine_select(out=g["ident"][:], in_=g["ident"][:], compare_op=ALU.not_equal, fill=1.0,
                               base=0, pattern=[[-1, P]], channel_multiplier=1).then_inc(s_id, 1)

        @block.tensor
        def _(pe):
            pe.wait_ge(s_id, 1)
            pe.wait_ge(w_in, 64)
            for i, n in enumerate(names):
                for ce in range(CE):
                    for cf in range(CE):
                        last = pe.transpose(wps[i][:, ce, cf * P:(cf + 1) * P], wnat[n][:, cf, ce * P:(ce + 1) * P], g["ident"][:])
                last.then_inc(w_turned, 1)
            pe.wait_ge(s_ready, 1)
            pe.wait_ge(mod_in, 16)
            for k in range(3):
                for ce in range(CE):
                    last = pe.matmul(mps[k][0:B, :], sT[:, ce, :], wm[:, ce, k * 512:(k + 1) * 512], start=(ce == 0), stop=(ce == CE - 1))
            last.then_inc(mod_ps, 1)

        @block.scalar
        def _(act):
            act.wait_ge(c_in, 16 * CE)
            act.activation(cexp[:], cT[:], ACT.Exp, scale=-1.0).then_inc(e_ready, 1)
            act.wait_ge(l_sum, 1)
            act.activation(le[:], ls[:], ACT.Exp).then_inc(l_exp, 1)

        @block.vector
        def _(dve):
            st = Steps(dve, v_step)
            dve.wait_ge(e_ready, 1)
            st.done(dve.tensor_scalar(cden[:], cexp[:], 1.0, None, ALU.add))
            st.done(dve.reciprocal(crec[:], cden[:]))
            dve.wait_ge(c_in, 16 * CE)
            dve.tensor_tensor(sT[:], cT[:], crec[:], ALU.mult).then_inc(s_ready, 1)
            dve.wait_ge(lam_in, 80)
            for i in range(2):
                st.done(dve.tensor_tensor(lp[:, i, :], lv[:, 2 * i, :], lv[:, 2 * i + 1, :], ALU.mult))
            dve.reduce_sum(ls[:], lp[:], axis=AX.X).then_inc(l_sum, 1)
            dve.tensor_scalar(g["subw"][:], subn[:], 1.0 - LAMBDA_INIT, 0.5, ALU.mult, ALU.mult)
            dve.memset(g["lam_sign"][:, 0:1], 1.0)
            dve.wait_ge(l_exp, 1)
            st.done(dve.tensor_tensor(ld[:], le[:, 1:2], le[:, 0:1], ALU.subtract))
            dve.tensor_scalar(g["lam_sign"][:, 1:2], ld[:], -LAMBDA_INIT, None, ALU.add)
            for i, n in enumerate(names):
                dve.wait_ge(w_turned, i + 1)
                dve.tensor_copy(g["wT"][n][:], wps[i][:]).then_inc(w_kept, 1)
            dve.wait_ge(mod_ps, 1)
            for k in range(3):
                st.done(dve.tensor_copy(mod[:, k * 512:(k + 1) * 512], mps[k][0:B, :]))
            m6 = mod[:].rearrange("b (a k e) -> b a k e", a=2, k=3)
            st.done(dve.tensor_scalar(m6[:, :, 1, :], m6[:, :, 1, :], 1.0, None, ALU.add))
            st.done(dve.tensor_scalar(gsign[:], m6[:, :, 2, :], 0.0, 2.0, ALU.is_ge, ALU.mult))
            st.done(dve.scalar_tensor_tensor(gabs[:], m6[:, :, 2, :], -1.0, m6[:, :, 2, :], ALU.mult, ALU.max))
            st.done(dve.tensor_scalar(gabs[:], gabs[:], 0.25, None, ALU.max))
            st.done(dve.tensor_scalar(gsign[:], gsign[:], -1.0, None, ALU.add))
            dve.tensor_tensor(m6[:, :, 2, :], gsign[:], gabs[:], ALU.mult).then_inc(mod_ready, 1)


def project(nc, sb, pb, sem, g):
    with ExitStack() as c:
        xs = [sb(c, f"p_x{r}", [P, TT, E]) for r in range(2)]
        modb = sb(c, "p_modb", [P, 6, E])
        stats = sb(c, "p_stats", [P, TT, 6])
        mv = sb(c, "p_mv", [P, TT, 2])
        vare = sb(c, "p_vare", [P, TT])
        rstd = sb(c, "p_rstd", [P, TT])
        carry = sb(c, "p_carry", [P, 1])
        xn = sb(c, "p_xn", [P, TT, E])
        hm = sb(c, "p_hm", [P, TT, E])
        h = sb(c, "p_h", [P, TT, E])
        hT = sb(c, "p_hT", [P, CE, BLK])
        qf = sb(c, "p_qf", [P, 4, BLK])
        res = sb(c, "p_res", [P, BLK])
        parts = [sb(c, f"p_parts{r}", [P, 4, 3, BLK], BF16) for r in range(2)]
        vaug = [sb(c, f"p_vaug{r}", [P, TT, HEADS, VW]) for r in range(2)]
        hps = pb(c, "p_hps", [P, CE, BLK])
        fps = [pb(c, f"p_fps{i}", [P, BLK]) for i in range(4)]
        vps = pb(c, "p_vps", [P, TT, E])
        x_in = [sem(c, f"p_x_in{r}") for r in range(2)]
        stored = [sem(c, f"p_stored{r}") for r in range(2)]
        modb_in, var_ready, rstd_ready, h_ready = (sem(c, f"p_{n}") for n in ("modb_in", "var_ready", "rstd_ready", "h_ready"))
        v_init, hps_ready, hT_ready, f_ready, v_ready = (sem(c, f"p_{n}") for n in ("v_init", "hps_ready", "hT_ready", "f_ready", "v_ready"))
        q1_ready, split_done, v_kept, v_step, g_step = (sem(c, f"p_{n}") for n in ("q1_ready", "split_done", "v_kept", "v_step", "g_step"))
        block = c.enter_context(nc.Block())
        V_STEPS = 2 * (2 + TT + 1 + 8)
        STORES = 16 * (24 + TT)
        xv = g["x"].rearrange("b (u t p) e -> b u p t e", u=2, p=P)

        @block.sync
        def _(sp):
            for n in range(NEXP):
                sp.dma_start(g["w1s"][:, n], g["w1"][n].rearrange("(c p) h -> p c h", p=P)).then_inc(g["w_loaded"], 16)
                sp.dma_start(g["w2s"][:, n], g["w2"][n].rearrange("(c p) h -> p c h", p=P)).then_inc(g["w_loaded"], 16)
            with sp.Fori(0, B) as it:
                sp.wait_ge(h_ready, 2 * it)
                sp.dma_start(modb[:].rearrange("p k e -> p (k e)"), g["modd"][bass.ds(it, 1), :].broadcast_to((P, 6 * E))).then_inc(modb_in, 16)
                for r in range(2):
                    sp.dma_start(xs[r][:], xv[bass.ds(it, 1), r].rearrange("a p t e -> (a p) t e")).then_inc(x_in[r], 16)
                for r in range(2):
                    for i in range(4):
                        dst = g["qd"] if i < 2 else g["kd"]
                        dv = dst.rearrange("(b q) f (g d) t -> b (q f) g d t", b=B, g=6)
                        for n, part in enumerate(Q_PART if i < 2 else K_PART):
                            if n == 0:
                                sp.wait_ge(split_done, 8 * it + 4 * r + i + 1)
                            sp.dma_start(dv[bass.ds(it, 1), (i % 2) * 16:(i % 2) * 16 + 16, n, :, r * BLK:(r + 1) * BLK].rearrange("a f d t -> (a f) d t"),
                                         parts[r][:, i, part, :]).then_inc(stored[r], 16)
                    sp.wait_ge(v_kept, 2 * it + r + 1)
                    vv = g["vd"].rearrange("(b q) p s c -> b p q s c", b=B)
                    for t in range(TT):
                        sp.dma_start(vv[bass.ds(it, 1), :, :, r * TT + t, :].rearrange("a p q c -> (a p) q c"),
                                     vaug[r][:, t].rearrange("p (q h) c -> p q (h c)", h=2)).then_inc(stored[r], 16)
            for r in range(2):
                sp.wait_ge(stored[r], B * STORES)

        @block.gpsimd
        def _(pool):
            for r in range(2):
                pool.memset(vaug[r][:], 0.0).then_inc(g_step, 1)
            pool.wait_ge(g_step, 2)
            for r in range(2):
                pool.memset(vaug[r][:, :, :, 16:17], 1.0).then_inc(v_init, 1)
            with pool.Fori(0, B) as it:
                for r in range(2):
                    pool.wait_ge(var_ready, 2 * it + r + 1)
                    pool.tensor_tensor(rstd[:], vare[:], g["neg_half"][:, 0:TT], ALU.pow).then_inc(rstd_ready, 1)

        @block.vector
        def _(dve):
            with dve.Fori(0, B) as it:
                st = Steps(dve, v_step, V_STEPS * it)
                for r in range(2):
                    dve.wait_ge(x_in[r], 16 * (it + 1))
                    for t in range(TT):
                        ins = dve.bn_stats(stats[:, t, :], xs[r][:, t, :])
                    st.done(ins)
                    dve.memset(carry[:], 0.0)
                    for t in range(TT):
                        ins = dve.bn_aggr(mv[:, t, :], stats[:, t, :])
                    st.done(ins)
                    dve.tensor_scalar(vare[:], mv[:, :, 1], EPS, None, ALU.add).then_inc(var_ready, 1)
                    dve.wait_ge(rstd_ready, 2 * it + r + 1)
                    dve.wait_ge(var_ready, 2 * it + r + 1)
                    for t in range(TT):
                        st.done(dve.tensor_scalar(xn[:, t, :], xs[r][:, t, :], mv[:, t, 0:1], rstd[:, t:t + 1], ALU.subtract, ALU.mult))
                    dve.wait_ge(modb_in, 16 * (it + 1))
                    st.done(dve.tensor_tensor(hm[:], xn[:], modb[:, 1:2, :].broadcast_to((P, TT, E)), ALU.mult))
                    dve.wait_ge(hps_ready, 2 * it + r)
                    dve.tensor_tensor(h[:], hm[:], modb[:, 0:1, :].broadcast_to((P, TT, E)), ALU.add).then_inc(h_ready, 1)
                    for i in range(4):
                        dve.wait_ge(q1_ready, 8 * it + 4 * r + i + 1)
                        st.done(dve.tensor_tensor(res[:], qf[:, i, :], parts[r][:, i, 0, :], ALU.subtract))
                        st.done(dve.tensor_copy(parts[r][:, i, 1, :], res[:]))
                        dve.tensor_tensor(parts[r][:, i, 2, :], res[:], parts[r][:, i, 1, :], ALU.subtract).then_inc(split_done, 1)
                        dve.wait_ge(split_done, 8 * it + 4 * r + i + 1)
                assert st.n == V_STEPS, st.n

        @block.tensor
        def _(pe):
            with pe.Fori(0, B) as it:
                for r in range(2):
                    pe.wait_ge(h_ready, 2 * it + r + 1)
                    pe.wait_ge(hT_ready, 2 * it + r)
                    for ce in range(CE):
                        for t in range(TT):
                            last = pe.transpose(hps[:, ce, t * P:(t + 1) * P], h[:, t, ce * P:(ce + 1) * P], g["ident"][:])
                    last.then_inc(hps_ready, 1)
                    pe.wait_ge(hT_ready, 2 * it + r + 1)
                    pe.wait_ge(q1_ready, 8 * it + 4 * r)
                    for i in range(4):
                        w = g["wT"]["wq" if i < 2 else "wk"]
                        for ce in range(CE):
                            last = pe.matmul(fps[i][:], w[:, ce, (i % 2) * P:(i % 2 + 1) * P], hT[:, ce, :], start=(ce == 0), stop=(ce == CE - 1))
                        last.then_inc(f_ready, 1)
                    pe.wait_ge(v_kept, 2 * it + r)
                    for t in range(TT):
                        for ce in range(CE):
                            last = pe.matmul(vps[:, t, :], hT[:, ce, t * P:(t + 1) * P], g["wT"]["wv"][:, ce, :], start=(ce == 0), stop=(ce == CE - 1))
                    last.then_inc(v_ready, 1)

        @block.scalar
        def _(act):
            act.wait_ge(v_init, 2)
            with act.Fori(0, B) as it:
                for r in range(2):
                    act.wait_ge(hps_ready, 2 * it + r + 1)
                    act.wait_ge(v_ready, 2 * it + r)
                    act.activation(hT[:], hps[:], ACT.Copy).then_inc(hT_ready, 1)
                    act.wait_ge(stored[r], STORES * it)
                    for i in range(4):
                        act.wait_ge(f_ready, 8 * it + 4 * r + i + 1)
                        act.wait_ge(split_done, 8 * it + 4 * r)
                        scale = HD ** -0.5 if i < 2 else 1.0
                        act.activation(qf[:, i, :], fps[i][:], ACT.Copy, scale=scale)
                        act.activation(parts[r][:, i, 0, :], fps[i][:], ACT.Copy, scale=scale).then_inc(q1_ready, 1)
                    act.wait_ge(v_ready, 2 * it + r + 1)
                    act.activation(vaug[r][:, :, :, 0:16], vps[:].rearrange("p t (h c) -> p t h c", c=16), ACT.Copy).then_inc(v_kept, 1)


def attend(nc, sb, pb, sem, g):
    with ExitStack() as c:
        qs = [sb(c, f"a_q{r}", [P, 4, T], BF16) for r in range(NBUF)]
        ks = [sb(c, f"a_k{r}", [P, 4, T], BF16) for r in range(NBUF)]
        vs = [sb(c, f"a_v{r}", [P, ST, 2 * VW]) for r in range(NBUF)]
        probs = [sb(c, f"a_p{r}", [P, 4, T]) for r in range(2)]
        zrow = sb(c, "a_zrow", [3, T], BF16)
        negmax = [sb(c, f"a_negmax{r}", [P, 32]) for r in range(2)]
        mrow = sb(c, "a_mrow", [32, P])
        mres = sb(c, "a_mres", [32, P])
        mparts = sb(c, "a_mparts", [32, 3, P], BF16)
        oT = sb(c, "a_oT", [P, T])
        mps = [pb(c, f"a_mps{r}", [P, T]) for r in range(2)]
        eps = [pb(c, f"a_eps{r}", [P, BLK]) for r in range(2)]
        ops = [pb(c, f"a_ops{r}", [P, BLK]) for r in range(2)]
        loaded = [sem(c, f"a_loaded{r}") for r in range(NBUF)]
        zeroed, ones_set = sem(c, "a_zeroed"), sem(c, "a_ones_set")
        mscore = [sem(c, f"a_mscore{r}") for r in range(2)]
        mtaken = [sem(c, f"a_mtaken{r}") for r in range(2)]
        mstep, msplit, mplaced = sem(c, "a_mstep"), sem(c, "a_msplit"), sem(c, "a_mplaced")
        escore = [sem(c, f"a_escore{r}") for r in range(2)]
        edone = [sem(c, f"a_edone{r}") for r in range(2)]
        pv = [[sem(c, f"a_pv{s}{r}") for r in range(2)] for s in range(2)]
        okept, ostored = sem(c, "a_okept"), sem(c, "a_ostored")
        block = c.enter_context(nc.Block())

        def at(p, a, k=0):
            it, r = p
            return it * (4 * a) + (r * a + k)

        def after(p, n=1):
            return p[0], p[1] + n

        def slot(p, idx):
            it, r = p
            k = 65 + 33 * r + idx
            return k % 2, it * 66 + k // 2

        def slots(k):
            return [("item", 0, 0), ("turn", 0, 1)] if k == 0 else [("item", k, k + 1)]

        @block.sync
        def _(sp):
            def load(r, p):
                q4 = g["qd"][p].rearrange("a f s t -> s (a f) t") if not isinstance(p, int) else g["qd"][p].rearrange("f s t -> s f t")
                k4 = g["kd"][p].rearrange("a f s t -> s (a f) t") if not isinstance(p, int) else g["kd"][p].rearrange("f s t -> s f t")
                v4 = g["vd"][p].rearrange("a p s c -> (a p) s c") if not isinstance(p, int) else g["vd"][p]
                sp.dma_start(ks[r][0:SROWS], k4).then_inc(loaded[r], 16)
                sp.dma_start(qs[r][0:SROWS], q4).then_inc(loaded[r], 16)
                sp.dma_start(qs[r][MROW:MROW + 3], zrow[:].rearrange("p (a t) -> p a t", a=1).broadcast_to((3, 4, T))).then_inc(loaded[r], 16)
                sp.dma_start(vs[r][:], v4).then_inc(loaded[r], 16)

            def place(r, count):
                sp.wait_ge(msplit, count)
                for j in range(3):
                    sp.dma_start(qs[r][MROW + j:MROW + j + 1].rearrange("a f (t c) -> a (f t) c", c=P), mparts[:, j, :]).then_inc(mplaced, 16)

            def store(p, index):
                sp.wait_ge(okept, at(p, 2, 2))
                sp.dma_start(g["od"][index].rearrange("a p t -> (a p) t") if not isinstance(index, int) else g["od"][index], oT[:]).then_inc(ostored, 16)

            sp.wait_ge(zeroed, 2 * NBUF + 1)
            for q in range(3):
                load(q, q)
            place(0, 1)
            place(1, 2)
            load(3, 3)

            def period(p, quad, places, loads):
                it, r = p
                if places:
                    place((r + 2) % NBUF, at(p, 1, 3))
                store(p, quad(0))
                if loads:
                    sp.wait_ge(pv[1][1], at(p, 4, 4))
                    load(r, quad(4))

            with sp.Fori(0, QUADS // 4 - 1) as it:
                for r in range(4):
                    period((it, r), lambda n: bass.ds(it * 4 + (r + n), 1), True, True)
            for r in range(4):
                period((QUADS // 4 - 1, r), lambda n: QUADS - 4 + r + n, r < 2, False)
            sp.wait_ge(ostored, 16 * QUADS)

        @block.gpsimd
        def _(pool):
            pool.memset(zrow[:], 0.0).then_inc(zeroed, 1)
            for r in range(NBUF):
                pool.memset(qs[r][:], 0.0).then_inc(zeroed, 1)
                pool.memset(ks[r][:], 0.0).then_inc(zeroed, 1)
            pool.wait_ge(zeroed, 2 * NBUF + 1)
            for r in range(NBUF):
                pool.memset(ks[r][MROW:MROW + 3], 1.0).then_inc(ones_set, 1)

        @block.tensor
        def _(pe):
            def item(buf, uses, r, k):
                f, t = k // ST, k % ST
                pe.wait_ge(mtaken[buf], uses)
                for hlf in range(2):
                    last = pe.matmul(mps[buf][:, hlf * BLK:(hlf + 1) * BLK], qs[r][:, f, t * P:(t + 1) * P],
                                     ks[r][:, f, hlf * BLK:(hlf + 1) * BLK], start=True, stop=True)
                last.then_inc(mscore[buf], 1)

            def turn(buf, uses, par):
                pe.wait_ge(mtaken[buf], uses)
                pe.matmul(mps[buf][0:32, 0:P], negmax[par][:], g["ident"][:], start=True, stop=True).then_inc(mscore[buf], 1)

            def max_step(p, k, items, turns):
                r = p[1]
                for kind, k, idx in slots(k):
                    if kind == "item" and items:
                        if k == 0:
                            pe.wait_ge(loaded[(r + 2) % NBUF], p[0] * LOAD_INC + LOAD_INC * ((r + 2) // NBUF + 1))
                        item(*slot(p, idx), (r + 2) % NBUF, k)
                    if kind == "turn" and turns:
                        turn(*slot(p, idx), (r + 1) % 2)

            def score(p, i, f):
                r = p[1] % NBUF
                for hlf in range(2):
                    pe.wait_ge(edone[hlf], at(p, 32, 4 * i + f))
                    pe.matmul(eps[hlf][:], ks[r][:, f, i * P:(i + 1) * P], qs[r][:, f, hlf * BLK:(hlf + 1) * BLK],
                              start=True, stop=True).then_inc(escore[hlf], 1)

            def product(p, i, hlf):
                pe.wait_ge(edone[hlf], at(p, 32, 4 * i + 4))
                if i == 0:
                    pe.wait_ge(okept, at(p, 2))
                for f in range(4):
                    last = pe.matmul(ops[hlf][32 * f:32 * f + VW, :], vs[p[1] % NBUF][:, i, (f // 2) * VW:(f // 2 + 1) * VW],
                                     probs[i % 2][:, f, hlf * BLK:(hlf + 1) * BLK], start=(i == 0), stop=(i == ST - 1))
                last.then_inc(pv[i % 2][hlf], 1)

            def head(p, items=True, turns=True, before=None):
                pe.wait_ge(mplaced, at(p, 48, 48))
                for f in range(4):
                    score(p, 0, f)
                    max_step(p, f, items, turns)
                    if before and f % 2:
                        product(before, ST - 1, f // 2)

            def tail(p, items=True):
                for i in range(1, ST):
                    for f in range(4):
                        score(p, i, f)
                        max_step(p, 4 * i + f, items, False)
                        if f % 2:
                            product(p, i - 1, f // 2)

            pe.wait_ge(ones_set, NBUF)
            pe.wait_ge(loaded[0], LOAD_INC)
            for k in range(32):
                item(k % 2, k // 2, 0, k)
            for k in range(32):
                max_step((0, -1), k, True, True)
            head((0, 0))
            with pe.Fori(0, QUADS // 4 - 1) as it:
                for r in range(4):
                    tail((it, r))
                    head((it, r + 1), before=(it, r))
            for r in range(4):
                p = (QUADS // 4 - 1, r)
                tail(p, items=r < 2)
                if r < 3:
                    head(after(p), items=r < 1, turns=r < 2, before=p)
            for hlf in range(2):
                product(p, ST - 1, hlf)

        @block.vector
        def _(dve):
            def item(buf, uses, par, k):
                dve.wait_ge(mscore[buf], uses + 1)
                dve.tensor_reduce(negmax[par][:, k:k + 1], mps[buf][:], AX.X, ALU.max, negate=True).then_inc(mtaken[buf], 1)

            def turn(buf, uses, p):
                dve.wait_ge(mscore[buf], uses + 1)
                dve.tensor_copy(mrow[:], mps[buf][0:32, 0:P]).then_inc(mtaken[buf], 1)
                dve.wait_ge(mtaken[buf], uses + 1)
                dve.wait_ge(mplaced, at(p, 48, 48))
                dve.tensor_copy(mparts[:, 0, :], mrow[:]).then_inc(mstep, 1)
                dve.wait_ge(mstep, at(p, 3, 4))
                dve.tensor_tensor(mres[:], mrow[:], mparts[:, 0, :], ALU.subtract).then_inc(mstep, 1)
                dve.wait_ge(mstep, at(p, 3, 5))
                dve.tensor_copy(mparts[:, 1, :], mres[:]).then_inc(mstep, 1)
                dve.wait_ge(mstep, at(p, 3, 6))
                dve.tensor_tensor(mparts[:, 2, :], mres[:], mparts[:, 1, :], ALU.subtract).then_inc(msplit, 1)

            def steps(p, ks_, items=True, turns=True):
                for k in ks_:
                    for kind, k, idx in slots(k):
                        if kind == "item" and items:
                            item(*slot(p, idx), p[1] % 2, k)
                        if kind == "turn" and turns:
                            turn(*slot(p, idx), p)

            for k in range(32):
                item(k % 2, k // 2, 0, k)
            steps((0, -1), range(32))
            steps((0, 0), range(4))
            with dve.Fori(0, QUADS // 4 - 1) as it:
                for r in range(4):
                    steps((it, r), range(4, 32))
                    steps((it, r + 1), range(4))
            for r in range(4):
                p = (QUADS // 4 - 1, r)
                steps(p, range(4, 32), items=r < 2, turns=False)
                steps(after(p), range(4), items=r < 1, turns=r < 2)

        @block.scalar
        def _(act):
            def exps(p, i):
                for f in range(4):
                    for hlf in range(2):
                        act.wait_ge(escore[hlf], at(p, 32, 4 * i + f + 1))
                        if f == 0:
                            act.wait_ge(pv[i % 2][hlf], at(p, 4, i // 2))
                        act.activation(probs[i % 2][:, f, hlf * BLK:(hlf + 1) * BLK], eps[hlf][:], ACT.Exp).then_inc(edone[hlf], 1)

            def keep(p):
                act.wait_ge(ostored, at(p, 16))
                for hlf in range(2):
                    act.wait_ge(pv[1][hlf], at(p, 4, 4))
                    act.activation(oT[:, hlf * BLK:(hlf + 1) * BLK], ops[hlf][:], ACT.Copy).then_inc(okept, 1)

            exps((0, 0), 0)
            with act.Fori(0, QUADS // 4 - 1) as it:
                for r in range(4):
                    for i in range(1, ST):
                        exps((it, r), i)
                    exps((it, r + 1), 0)
                    keep((it, r))
            for r in range(4):
                p = (QUADS // 4 - 1, r)
                for i in range(1, ST):
                    exps(p, i)
                if r < 3:
                    exps(after(p), 0)
                keep(p)


def mix(nc, sb, pb, sem, g):
    with ExitStack() as c:
        os_ = sb(c, "m_o", [P, QB, BLK])
        xs = sb(c, "m_x", [P, TT, E])
        modb = sb(c, "m_modb", [P, 6, E])
        rec = sb(c, "m_rec", [P, 32])
        rl = sb(c, "m_rl", [P, 32])
        A = sb(c, "m_A", [P, 32, 16])
        D = sb(c, "m_D", [P, TT * HEADS, 16])
        tmp = sb(c, "m_tmp", [P, TT, E])
        ss = sb(c, "m_ss", [P, TT * HEADS])
        sse = sb(c, "m_sse", [P, TT * HEADS])
        rs0 = sb(c, "m_rs0", [P, TT * HEADS])
        rs = sb(c, "m_rs", [P, TT * HEADS])
        an = sb(c, "m_an", [P, TT, E])
        aT = sb(c, "m_aT", [P, CE, BLK])
        x1 = sb(c, "m_x1", [P, TT, E])
        stats = sb(c, "m_stats", [P, TT, 6])
        mv = sb(c, "m_mv", [P, TT, 2])
        vare = sb(c, "m_vare", [P, TT])
        rstd = sb(c, "m_rstd", [P, TT])
        carry = sb(c, "m_carry", [P, 1])
        xn = sb(c, "m_xn", [P, TT, E])
        h2 = sb(c, "m_h2", [P, TT, E])
        hT = sb(c, "m_hT", [P, CE, BLK])
        lg = sb(c, "m_lg", [P, TT, NEXP])
        top8 = sb(c, "m_top8", [P, TT, 8])
        idx8 = sb(c, "m_idx8", [P, TT, 8], U32)
        idxf = sb(c, "m_idxf", [P, TT, 2])
        diff = sb(c, "m_diff", [P, TT])
        ew = sb(c, "m_ew", [P, TT])
        den = sb(c, "m_den", [P, TT])
        wt = sb(c, "m_wt", [P, TT, 2])
        iota = sb(c, "m_iota", [P, NEXP])
        iotai = sb(c, "m_iotai", [P, NEXP], mybir.dt.int32)
        gate = [sb(c, f"m_gate{i}", [P, TT, NEXP]) for i in range(2)]
        rh = [sb(c, f"m_rh{i}", [P, BLK]) for i in range(2)]
        hs = [sb(c, f"m_hs{i}", [P, CH, BLK]) for i in range(2)]
        acc = sb(c, "m_acc", [P, TT, E])
        og = sb(c, "m_og", [P, TT, E])
        big = [pb(c, f"m_big{i}", [P, 1024]) for i in range(2)]
        gen = pb(c, "m_gen", [P, 1024])
        hp = [pb(c, f"m_hp{i}", [P, BLK]) for i in range(2)]
        names = ("o_in", "x_in", "modb_in", "out_stored", "turned", "ss_ready", "rs_ready", "an_ready", "aT_ps", "aT_ready",
                 "wo_ps", "var_ready", "rstd_ready", "h2_ready", "hT_ps", "hT_ready", "lg_ps", "diff_ready", "ew_ready",
                 "iota_ready", "wo_taken", "hid_ps", "relu_done", "sq_done", "y_ps", "y_taken", "out_ready", "lg_taken", "v_step", "g_step")
        S = {n: sem(c, f"m_{n}") for n in names}
        turn_taken = [sem(c, f"m_turn_taken{i}") for i in range(2)]
        block = c.enter_context(nc.Block())
        V_STEPS = 2 * V_BLOCK
        xv = g["x"].rearrange("b (u t p) e -> b u p t e", u=2, p=P)
        ov = g["out"].rearrange("b (u t p) e -> b u p t e", u=2, p=P)
        odv = g["od"].rearrange("(b q) p t -> b p q t", b=B)
        NH = NEXP * CH

        @block.sync
        def _(sp):
            with sp.Fori(0, B) as it:
                for r in range(2):
                    sp.wait_ge(S["turned"], TT * 2 * it + TT * r)
                    sp.dma_start(os_[:], odv[bass.ds(it, 1), :, :, r * BLK:(r + 1) * BLK].rearrange("a p q t -> (a p) q t")).then_inc(S["o_in"], 16)
                    if r == 0:
                        sp.wait_ge(S["out_ready"], 2 * it)
                        sp.dma_start(modb[:].rearrange("p k e -> p (k e)"), g["modd"][bass.ds(it, 1), :].broadcast_to((P, 6 * E))).then_inc(S["modb_in"], 16)
                    sp.wait_ge(S["wo_taken"], 2 * it + r)
                    sp.dma_start(xs[:], xv[bass.ds(it, 1), r].rearrange("a p t e -> (a p) t e")).then_inc(S["x_in"], 16)
                    sp.wait_ge(S["out_ready"], 2 * it + r + 1)
                    sp.dma_start(ov[bass.ds(it, 1), r].rearrange("a p t e -> (a p) t e"), og[:]).then_inc(S["out_stored"], 16)
            sp.wait_ge(S["out_stored"], 16 * 2 * B)

        @block.gpsimd
        def _(pool):
            pool.iota(iotai[:], [[1, NEXP]], base=0, channel_multiplier=0).then_inc(S["g_step"], 1)
            pool.wait_ge(S["g_step"], 1)
            pool.tensor_copy(iota[:], iotai[:]).then_inc(S["iota_ready"], 1)
            with pool.Fori(0, B) as it:
                for r in range(2):
                    pool.wait_ge(S["ss_ready"], 2 * it + r + 1)
                    pool.tensor_tensor(rs0[:], sse[:], g["neg_half"][:], ALU.pow).then_inc(S["rs_ready"], 1)
                    pool.wait_ge(S["var_ready"], 2 * it + r + 1)
                    pool.tensor_tensor(rstd[:], vare[:], g["neg_half"][:, 0:TT], ALU.pow).then_inc(S["rstd_ready"], 1)

        @block.tensor
        def _(pe):
            def turn_gen(src, ready, count, out_sem):
                pe.wait_ge(ready, count)
                gv = gen[:].rearrange("p (c t) -> p c t", c=CE)
                for ce in range(CE):
                    for t in range(TT):
                        last = pe.transpose(gv[:, ce, t * P:(t + 1) * P], src[:, t, ce * P:(ce + 1) * P], g["ident"][:])
                last.then_inc(out_sem, 1)

            pe.wait_ge(g["w_loaded"], 32 * NEXP)
            with pe.Fori(0, B) as it:
                for r in range(2):
                    n = 2 * it + r
                    pe.wait_ge(S["o_in"], 32 * it + 16 * (r + 1))
                    pe.wait_ge(S["y_taken"], n * (NEXP * TT))
                    for t in range(TT):
                        pe.wait_ge(turn_taken[t % 2], n * 2 + t // 2)
                        for q in range(QB):
                            last = pe.transpose(big[t % 2][:, q * P:(q + 1) * P], os_[:, q, t * P:(t + 1) * P], g["ident"][:])
                        last.then_inc(S["turned"], 1)
                    turn_gen(an, S["an_ready"], n + 1, S["aT_ps"])
                    pe.wait_ge(S["aT_ready"], n + 1)
                    gv = gen[:].rearrange("p (t e) -> p t e", t=TT)
                    for t in range(TT):
                        for ce in range(CE):
                            last = pe.matmul(gv[:, t, :], aT[:, ce, t * P:(t + 1) * P], g["wT"]["wo"][:, ce, :], start=(ce == 0), stop=(ce == CE - 1))
                    last.then_inc(S["wo_ps"], 1)
                    turn_gen(h2, S["h2_ready"], n + 1, S["hT_ps"])
                    pe.wait_ge(S["hT_ready"], n + 1)
                    for t in range(TT):
                        for ce in range(CE):
                            last = pe.matmul(gen[:, t * NEXP:(t + 1) * NEXP], hT[:, ce, t * P:(t + 1) * P], g["rT"][:, ce, :], start=(ce == 0), stop=(ce == CE - 1))
                    last.then_inc(S["lg_ps"], 1)

                    def hidden(e):
                        for m in range(CH):
                            k = e * CH + m
                            pe.wait_ge(S["relu_done"], n * NH + (k - 1) if k else n * NH)
                            for ce in range(CE):
                                last = pe.matmul(hp[m % 2][:], g["w1s"][:, e, ce, m * P:(m + 1) * P], hT[:, ce, :], start=(ce == 0), stop=(ce == CE - 1))
                            last.then_inc(S["hid_ps"], 1)

                    def outputs(e):
                        pe.wait_ge(S["sq_done"], n * NH + (e + 1) * CH)
                        if e >= 2:
                            pe.wait_ge(S["y_taken"], n * (NEXP * TT) + (e - 1) * TT)
                        for t in range(TT):
                            for m in range(CH):
                                last = pe.matmul(big[e % 2][:, t * E:(t + 1) * E], hs[e % 2][:, m, t * P:(t + 1) * P], g["w2s"][:, e, m, :],
                                                 start=(m == 0), stop=(m == CH - 1))
                            if t % 2:
                                last.then_inc(S["y_ps"], 1)

                    hidden(0)
                    for e in range(NEXP):
                        if e + 1 < NEXP:
                            hidden(e + 1)
                        outputs(e)

        @block.scalar
        def _(act):
            with act.Fori(0, B) as it:
                for r in range(2):
                    n = 2 * it + r
                    act.wait_ge(S["aT_ps"], n + 1)
                    act.activation(aT[:].rearrange("p c t -> p (c t)"), gen[:], ACT.Copy).then_inc(S["aT_ready"], 1)
                    act.wait_ge(S["hT_ps"], n + 1)
                    act.activation(hT[:].rearrange("p c t -> p (c t)"), gen[:], ACT.Copy).then_inc(S["hT_ready"], 1)
                    act.wait_ge(S["diff_ready"], n + 1)
                    act.activation(ew[:], diff[:], ACT.Exp).then_inc(S["ew_ready"], 1)
                    for k in range(NH):
                        act.wait_ge(S["hid_ps"], n * NH + k + 1)
                        act.wait_ge(S["sq_done"], n * NH + k - 1 if k else n * NH)
                        act.activation(rh[k % 2][:], hp[k % 2][:], ACT.Relu).then_inc(S["relu_done"], 1)

        @block.vector
        def _(dve):
            dve.wait_ge(S["iota_ready"], 1)
            with dve.Fori(0, B) as it:
                st = Steps(dve, S["v_step"], V_STEPS * it)
                for r in range(2):
                    n = 2 * it + r
                    for t in range(TT):
                        dve.wait_ge(S["turned"], n * TT + t + 1)
                        tv = big[t % 2][:].rearrange("p (f c) -> p f c", c=32)
                        st.done(dve.reciprocal(rec[:], tv[:, :, 16]))
                        st.done(dve.tensor_tensor(rl[:].rearrange("p (h a) -> p h a", a=2), rec[:].rearrange("p (h a) -> p h a", a=2),
                                                  g["lam_sign"][:].rearrange("p (o a) -> p o a", o=1).broadcast_to((P, HEADS, 2)), ALU.mult))
                        dve.tensor_tensor(A[:], tv[:, :, 0:16], rl[:].rearrange("p (f o) -> p f o", o=1).broadcast_to((P, 32, 16)), ALU.mult).then_inc(turn_taken[t % 2], 1)
                        dve.wait_ge(turn_taken[t % 2], n * 2 + t // 2 + 1)
                        av = A[:].rearrange("p (h a) c -> p h a c", a=2)
                        st.done(dve.tensor_tensor(D[:, t * HEADS:(t + 1) * HEADS, :], av[:, :, 0, :], av[:, :, 1, :], ALU.add))
                    tflat = tmp[:].rearrange("p t (h c) -> p (t h) c", c=16)
                    anf = an[:].rearrange("p t (h c) -> p (t h) c", c=16)
                    st.done(dve.tensor_scalar(tflat, D[:], 1.0 / 8, RANGE, ALU.mult, ALU.min))
                    st.done(dve.tensor_scalar(tflat, tflat, -RANGE, None, ALU.max))
                    st.done(dve.tensor_tensor(tflat, tflat, tflat, ALU.mult))
                    st.done(dve.reduce_sum(ss[:], tflat, axis=AX.X))
                    dve.tensor_scalar(sse[:], ss[:], EPS / 4, RANGE * RANGE, ALU.add, ALU.min).then_inc(S["ss_ready"], 1)
                    dve.wait_ge(S["rs_ready"], n + 1)
                    st.done(dve.scalar_tensor_tensor(rs[:], ss[:], RANGE * RANGE, rs0[:], ALU.is_lt, ALU.mult))
                    st.done(dve.tensor_tensor(tflat, D[:], rs[:].rearrange("p (f o) -> p f o", o=1).broadcast_to((P, TT * HEADS, 16)), ALU.mult))
                    dve.tensor_tensor(anf, tflat, g["subw"][:].rearrange("p (o c) -> p o c", o=1).broadcast_to((P, TT * HEADS, 16)), ALU.mult).then_inc(S["an_ready"], 1)
                    dve.wait_ge(S["wo_ps"], n + 1)
                    dve.wait_ge(S["modb_in"], 16 * (it + 1))
                    dve.wait_ge(S["x_in"], 32 * it + 16 * (r + 1))
                    st.done(dve.tensor_tensor(tmp[:], gen[:].rearrange("p (t e) -> p t e", t=TT), modb[:, 2:3, :].broadcast_to((P, TT, E)), ALU.mult))
                    dve.tensor_tensor(x1[:], tmp[:], xs[:], ALU.add).then_inc(S["wo_taken"], 1)
                    dve.wait_ge(S["wo_taken"], n + 1)
                    for t in range(TT):
                        ins = dve.bn_stats(stats[:, t, :], x1[:, t, :])
                    st.done(ins)
                    dve.memset(carry[:], 0.0)
                    for t in range(TT):
                        ins = dve.bn_aggr(mv[:, t, :], stats[:, t, :])
                    st.done(ins)
                    dve.tensor_scalar(vare[:], mv[:, :, 1], EPS, None, ALU.add).then_inc(S["var_ready"], 1)
                    dve.wait_ge(S["var_ready"], n + 1)
                    dve.wait_ge(S["rstd_ready"], n + 1)
                    for t in range(TT):
                        st.done(dve.tensor_scalar(xn[:, t, :], x1[:, t, :], mv[:, t, 0:1], rstd[:, t:t + 1], ALU.subtract, ALU.mult))
                    st.done(dve.tensor_tensor(tmp[:], xn[:], modb[:, 4:5, :].broadcast_to((P, TT, E)), ALU.mult))
                    dve.tensor_tensor(h2[:], tmp[:], modb[:, 3:4, :].broadcast_to((P, TT, E)), ALU.add).then_inc(S["h2_ready"], 1)
                    dve.wait_ge(S["lg_ps"], n + 1)
                    st.done(dve.tensor_copy(lg[:].rearrange("p t n -> p (t n)"), gen[:, 0:TT * NEXP]))
                    dve.memset(carry[:], 0.0)
                    for t in range(TT):
                        ins = dve.max(top8[:, t, :], lg[:, t, :])
                    st.done(ins)
                    dve.memset(carry[:], 0.0)
                    for t in range(TT):
                        ins = dve.max_index(idx8[:, t, :], top8[:, t, :], lg[:, t, :])
                    st.done(ins)
                    dve.tensor_tensor(diff[:], top8[:, :, 1], top8[:, :, 0], ALU.subtract).then_inc(S["diff_ready"], 1)
                    st.done(dve.tensor_copy(idxf[:], idx8[:, :, 0:2]))
                    dve.wait_ge(S["ew_ready"], n + 1)
                    st.done(dve.tensor_scalar(den[:], ew[:], 1.0, None, ALU.add))
                    st.done(dve.reciprocal(wt[:, :, 0], den[:]))
                    st.done(dve.tensor_tensor(wt[:, :, 1], ew[:], wt[:, :, 0], ALU.mult))
                    for t in range(TT):
                        for i in range(2):
                            st.done(dve.tensor_scalar(gate[i][:, t, :], iota[:], idxf[:, t, i:i + 1], wt[:, t, i:i + 1], ALU.is_equal, ALU.mult))
                    st.done(dve.tensor_tensor(gate[0][:], gate[0][:], gate[1][:], ALU.add))

                    def squares(e):
                        for m in range(CH):
                            k = e * CH + m
                            dve.wait_ge(S["relu_done"], n * NH + k + 1)
                            if m == 0 and e >= 2:
                                dve.wait_ge(S["y_ps"], n * (NEXP * 2) + (e - 1) * 2)
                            dve.tensor_tensor(hs[e % 2][:, m, :], rh[k % 2][:], rh[k % 2][:], ALU.mult).then_inc(S["sq_done"], 1)

                    def combine(e):
                        for t in range(TT):
                            dve.wait_ge(S["y_ps"], n * (NEXP * 2) + e * 2 + t // 2 + 1)
                            if e == 0:
                                ins = dve.tensor_scalar(acc[:, t, :], big[0][:, t * E:(t + 1) * E], gate[0][:, t, 0:1], None, ALU.mult)
                            else:
                                ins = dve.scalar_tensor_tensor(acc[:, t, :], big[e % 2][:, t * E:(t + 1) * E], gate[0][:, t, e:e + 1], acc[:, t, :], ALU.mult, ALU.add)
                            ins.then_inc(S["y_taken"], 1)

                    squares(0)
                    for e in range(NEXP):
                        if e:
                            dve.wait_ge(S["y_taken"], n * (NEXP * TT) + e * TT)
                        if e + 1 < NEXP:
                            squares(e + 1)
                        combine(e)
                    dve.wait_ge(S["y_taken"], (n + 1) * (NEXP * TT))
                    st.done(dve.tensor_tensor(tmp[:], acc[:], modb[:, 5:6, :].broadcast_to((P, TT, E)), ALU.mult))
                    dve.wait_ge(S["out_stored"], n * 16)
                    dve.tensor_tensor(og[:], tmp[:], x1[:], ALU.add).then_inc(S["out_ready"], 1)
                assert st.n == V_STEPS, st.n


V_BLOCK = 3 * TT + 5 + 1 + 1 + 2 + TT + 1 + 3 + 4 + 2 * TT + 1 + 1

_INS = ['L0_attn_query', 'L0_attn_Wq', 'L0_attn_Wk', 'L0_attn_Wv', 'L0_attn_Wo', 'L0_attn_lambda_q1', 'L0_attn_lambda_k1',
        'L0_attn_lambda_q2', 'L0_attn_lambda_k2', 'L0_attn_subln_w', 'L0_ffn_router_w', 'L0_ffn_w1', 'L0_ffn_w2', 'L0_c', 'L0_wmod']


def kernel(**inputs):
    import numpy as _np
    import concourse.bacc as _bacc
    from concourse import mybir as _mybir
    from concourse.bass_utils import run_bass_kernel_spmd as _run

    nc = _bacc.Bacc("TRN2", target_bir_lowering=False, num_devices=1)
    arrays, args = {}, []
    for name in _INS:
        a = _np.ascontiguousarray(inputs[name])
        arrays[f"in_{name}"] = a
        args.append(nc.dram_tensor(f"in_{name}", a.shape, _mybir.dt.from_np(a.dtype), kind="ExternalInput").ap())
    args.append(nc.dram_tensor("out_x", (B, T, E), _mybir.dt.float32, kind="ExternalOutput").ap())
    build(nc, *args)
    r = _run(nc, [arrays], core_ids=[0])
    return r.results[0]["out_x"]
```

```python
from contextlib import ExitStack

import numpy as np
import concourse.bass as bass
from concourse import mybir

FP32 = mybir.dt.float32
BF16 = mybir.dt.bfloat16
U32 = mybir.dt.uint32
I32 = mybir.dt.int32
ALU = mybir.AluOpType
ACT = mybir.ActivationFunctionType
AX = mybir.AxisListType

P = 128
B, T, E = 4, 1024, 256
HEADS, HD = 16, 8
NEXP, HID = 8, 512
LAMBDA_INIT = float(0.8 - 0.6 * np.exp(-0.3 * 12))
EPS = 1e-5
ROOT_SCALE = 2.0 ** -5
RANGE = 2.0 ** 61
CE = E // P
CH = HID // P
BLK = 512
TT = BLK // P
ST = T // P
QUADS = B * HEADS // 2
QB = HEADS // 2
CAP = B * T + P
ROWS = NEXP * CAP + P
NTILE = 2 * B * T // P + NEXP
NX = 4
NTAB = NTILE + NX
VW = 32
Q_PART = (0, 0, 0, 1, 1, 2)
K_PART = (0, 1, 2, 0, 1, 0)
SROWS = HD * len(Q_PART)
MROW = 64
NBUF = 4
LOAD_INC = 16 * 4


class Steps:

    def __init__(self, eng, sem, base=0):
        self.eng, self.sem, self.base, self.n = eng, sem, base, 0

    def done(self, ins):
        self.n += 1
        ins.then_inc(self.sem, 1)
        self.eng.wait_ge(self.sem, self.base + self.n)


def build(nc, x, wq, wk, wv, wo, lq1, lk1, lq2, lk2, subln, router, w1, w2, cond, wmod, out):
    top = ExitStack()
    with top:
        def sb(ctx, name, shape, dt=FP32):
            return ctx.enter_context(nc.sbuf_tensor(name, shape, dt))

        def pb(ctx, name, shape, dt=FP32):
            return ctx.enter_context(nc.psum_tensor(name, shape, dt))

        def sem(ctx, name):
            return ctx.enter_context(nc.semaphore(name))

        qd = nc.dram_tensor("q_stack", (QUADS, 4, SROWS, T), BF16, kind="Internal").ap()
        kd = nc.dram_tensor("k_stack", (QUADS, 4, SROWS, T), BF16, kind="Internal").ap()
        vd = nc.dram_tensor("v_quads", (QUADS, P, ST, 2 * VW), FP32, kind="Internal").ap()
        od = nc.dram_tensor("o_quads", (QUADS, P, T), FP32, kind="Internal").ap()
        modd = nc.dram_tensor("mod_rows", (B, 6 * E), FP32, kind="Internal").ap()

        ident = sb(top, "ident", [P, P])
        wT = {n: sb(top, f"{n}_T", [P, CE, E]) for n in ("wq", "wk", "wv", "wo")}
        rT = sb(top, "router_T", [P, CE, NEXP])
        lam_sign = sb(top, "lam_sign", [P, 2])
        neg_half = sb(top, "neg_half", [P, TT])
        w_loaded = sem(top, "w_loaded")
        xg = nc.dram_tensor("x_rows", (ROWS, E), FP32, kind="Internal").ap()
        yg = nc.dram_tensor("y_rows", (NTILE * P, E), FP32, kind="Internal").ap()
        x1d = nc.dram_tensor("x1_blocks", (2 * B, P, TT * E), FP32, kind="Internal").ap()
        chod = nc.dram_tensor("choices", (2 * B, P, 3 * 2 * TT), FP32, kind="Internal").ap()
        count = sb(top, "count", [P, NEXP])
        tail = sb(top, "tail", [P, NEXP], I32)
        close_up = sb(top, "close_up", [P, NEXP])
        iota = sb(top, "iota", [P, NEXP])
        first_row = sb(top, "first_row", [P, NEXP])
        row_of = sb(top, "row_of", [P, NTAB], I32)
        expert_of = sb(top, "expert_of", [P, NTAB], I32)
        w1s = sb(top, "w1s", [P, NEXP, CE, HID])
        with ExitStack() as stacks:
            qs = [sb(stacks, f"a_q{r}", [P, 4, T], BF16) for r in range(NBUF)]
            ks = [sb(stacks, f"a_k{r}", [P, 4, T], BF16) for r in range(NBUF)]
            setup(nc, top, sb, pb, sem, locals())
            project(nc, sb, pb, sem, locals())
            attend(nc, sb, pb, sem, locals())
        w2s = sb(top, "w2s", [P, NEXP, CH, E])
        route(nc, sb, pb, sem, locals())
        experts(nc, sb, pb, sem, locals())


def setup(nc, top, sb, pb, sem, g):
    with ExitStack() as c:
        wnat = {n: sb(c, f"{n}_nat", [P, CE, E]) for n in ("wq", "wk", "wv", "wo")}
        cT = sb(c, "cT", [P, CE, B])
        cexp = sb(c, "cexp", [P, CE, B])
        cden = sb(c, "cden", [P, CE, B])
        crec = sb(c, "crec", [P, CE, B])
        sT = sb(c, "sT", [P, CE, B])
        wm = sb(c, "wm", [P, CE, 6 * E])
        lv = sb(c, "lv", [P, 4, HD])
        lp = sb(c, "lp", [P, 2, HD])
        ls = sb(c, "ls", [P, 2])
        le = sb(c, "le", [P, 2])
        ld = sb(c, "ld", [P, 1])
        subn = sb(c, "subn", [P, 1])
        subw = sb(c, "subw", [P, 1])
        mod = sb(c, "mod", [B, 6 * E])
        gsign = sb(c, "gsign", [B, 2, E])
        gabs = sb(c, "gabs", [B, 2, E])
        wps = [pb(c, f"wps{i}", [P, CE, E]) for i in range(4)]
        mps = [pb(c, f"mps{i}", [P, 512]) for i in range(3)]
        w_in, c_in, s_id0, s_id = sem(c, "w_in"), sem(c, "c_in"), sem(c, "ident_zero"), sem(c, "ident_ready")
        mod_in, lam_in, small_in = sem(c, "mod_in"), sem(c, "lam_in"), sem(c, "small_in")
        w_turned, e_ready, s_ready = sem(c, "w_turned"), sem(c, "e_ready"), sem(c, "s_ready")
        l_sum, l_exp, mod_ps, mod_ready, mod_out = (sem(c, n) for n in ("l_sum", "l_exp", "mod_ps", "mod_ready", "mod_out"))
        v_step, cleared = sem(c, "setup_v_step"), sem(c, "stacks_cleared")
        block = c.enter_context(nc.Block())
        names = ("wq", "wk", "wv", "wo")

        @block.sync
        def _(sp):
            for ce in range(CE):
                sp.dma_start(cT[:, ce, :], g["cond"][:, ce * P:(ce + 1) * P].rearrange("b p -> p b"), allow_slow_non_contiguous=True).then_inc(c_in, 16)
            for n in names:
                sp.dma_start(wnat[n][:], g[n].rearrange("(c p) e -> p c e", p=P)).then_inc(w_in, 16)
            sp.dma_start(wm[:], g["wmod"].rearrange("(c p) n -> p c n", p=P)).then_inc(mod_in, 16)
            for i, v in enumerate(("lq1", "lk1", "lq2", "lk2")):
                sp.dma_start(lv[:, i, :], g[v].rearrange("(a n) -> a n", a=1).broadcast_to((P, HD))).then_inc(lam_in, 16)
            for h in range(P // 16):
                sp.dma_start(subn[h * 16:(h + 1) * 16, :], g["subln"].rearrange("(n a) -> n a", a=1)).then_inc(lam_in, 16)
            for ce in range(CE):
                sp.dma_start(g["rT"][:, ce, :], g["router"][:, ce * P:(ce + 1) * P].rearrange("n p -> p n"), allow_slow_non_contiguous=True).then_inc(small_in, 16)
            sp.wait_ge(mod_ready, 1)
            sp.dma_start(g["modd"], mod[:]).then_inc(mod_out, 16)
            sp.wait_ge(mod_out, 16)
            sp.wait_ge(small_in, 16 * CE)

        @block.gpsimd
        def _(pool):
            pool.memset(g["ident"][:], 0.0).then_inc(s_id0, 1)
            pool.memset(g["neg_half"][:], -0.5)
            pool.wait_ge(s_id0, 1)
            pool.affine_select(out=g["ident"][:], in_=g["ident"][:], compare_op=ALU.not_equal, fill=1.0,
                               base=0, pattern=[[-1, P]], channel_multiplier=1).then_inc(s_id, 1)
            for r in range(NBUF):
                for stack in (g["qs"][r], g["ks"][r]):
                    pool.memset(stack[:].rearrange("p f t -> p (f t)").bitcast(U32), 0).then_inc(cleared, 1)
            pool.wait_ge(cleared, 2 * NBUF)
            for r in range(NBUF):
                pool.memset(g["ks"][r][MROW:MROW + 3], 1.0)

        @block.tensor
        def _(pe):
            pe.wait_ge(s_id, 1)
            pe.wait_ge(w_in, 64)
            for i, n in enumerate(names):
                for ce in range(CE):
                    for cf in range(CE):
                        last = pe.transpose(wps[i][:, ce, cf * P:(cf + 1) * P], wnat[n][:, cf, ce * P:(ce + 1) * P], g["ident"][:])
                last.then_inc(w_turned, 1)
            pe.wait_ge(s_ready, 1)
            pe.wait_ge(mod_in, 16)
            for k in range(3):
                for ce in range(CE):
                    last = pe.matmul(mps[k][0:B, :], sT[:, ce, :], wm[:, ce, k * 512:(k + 1) * 512], start=(ce == 0), stop=(ce == CE - 1))
            last.then_inc(mod_ps, 1)

        @block.scalar
        def _(act):
            act.wait_ge(c_in, 16 * CE)
            act.activation(cexp[:], cT[:], ACT.Exp, scale=-1.0).then_inc(e_ready, 1)
            act.wait_ge(l_sum, 1)
            act.activation(le[:], ls[:], ACT.Exp).then_inc(l_exp, 1)

        @block.vector
        def _(dve):
            st = Steps(dve, v_step)
            dve.wait_ge(e_ready, 1)
            st.done(dve.tensor_scalar(cden[:], cexp[:], 1.0, None, ALU.add))
            st.done(dve.reciprocal(crec[:], cden[:]))
            dve.wait_ge(c_in, 16 * CE)
            dve.tensor_tensor(sT[:], cT[:], crec[:], ALU.mult).then_inc(s_ready, 1)
            dve.wait_ge(lam_in, 16 * (4 + P // 16))
            for i in range(2):
                st.done(dve.tensor_tensor(lp[:, i, :], lv[:, 2 * i, :], lv[:, 2 * i + 1, :], ALU.mult))
            dve.reduce_sum(ls[:], lp[:], axis=AX.X).then_inc(l_sum, 1)
            st.done(dve.tensor_scalar(subw[:], subn[:], 1.0 - LAMBDA_INIT, ROOT_SCALE, ALU.mult, ALU.mult))
            dve.memset(g["lam_sign"][:, 0:1], 1.0)
            dve.wait_ge(l_exp, 1)
            st.done(dve.tensor_tensor(ld[:], le[:, 1:2], le[:, 0:1], ALU.subtract))
            dve.tensor_scalar(g["lam_sign"][:, 1:2], ld[:], -LAMBDA_INIT, None, ALU.add)
            for i, n in enumerate(names):
                dve.wait_ge(w_turned, i + 1)
                if n == "wo":
                    dve.tensor_scalar(g["wT"][n][:], wps[i][:], subw[:, 0:1], None, ALU.mult)
                else:
                    dve.tensor_copy(g["wT"][n][:], wps[i][:])
            dve.wait_ge(mod_ps, 1)
            for k in range(3):
                st.done(dve.tensor_copy(mod[:, k * 512:(k + 1) * 512], mps[k][0:B, :]))
            m6 = mod[:].rearrange("b (a k e) -> b a k e", a=2, k=3)
            st.done(dve.tensor_scalar(m6[:, :, 1, :], m6[:, :, 1, :], 1.0, None, ALU.add))
            st.done(dve.tensor_scalar(gsign[:], m6[:, :, 2, :], 0.0, 2.0, ALU.is_ge, ALU.mult))
            st.done(dve.scalar_tensor_tensor(gabs[:], m6[:, :, 2, :], -1.0, m6[:, :, 2, :], ALU.mult, ALU.max))
            st.done(dve.tensor_scalar(gabs[:], gabs[:], 0.25, None, ALU.max))
            st.done(dve.tensor_scalar(gsign[:], gsign[:], -1.0, None, ALU.add))
            dve.tensor_tensor(m6[:, :, 2, :], gsign[:], gabs[:], ALU.mult).then_inc(mod_ready, 1)


def project(nc, sb, pb, sem, g):
    with ExitStack() as c:
        def two(name, shape, dt=FP32):
            return [sb(c, f"{name}{r}", shape, dt) for r in range(2)]

        xs = two("p_x", [P, TT, E])
        modb = sb(c, "p_modb", [P, 2, E])
        stats = sb(c, "p_stats", [P, TT, 6])
        mv = sb(c, "p_mv", [P, TT, 2])
        vare = sb(c, "p_vare", [P, TT])
        rstd = sb(c, "p_rstd", [P, TT])
        carry = sb(c, "p_carry", [P, 1])
        xn = sb(c, "p_xn", [P, TT, E])
        h = two("p_h", [P, TT, E])
        hT = two("p_hT", [P, CE, BLK])
        qf = sb(c, "p_qf", [P, 4, BLK])
        res = two("p_res", [P, BLK])
        parts = two("p_parts", [P, 4, 3, BLK], BF16)
        vaug = two("p_vaug", [P, TT, HEADS, VW])
        hps = pb(c, "p_hps", [P, CE, BLK])
        fps = [pb(c, f"p_fps{i}", [P, BLK]) for i in range(4)]
        vps = pb(c, "p_vps", [P, TT, E])
        x_in = [sem(c, f"p_x_in{r}") for r in range(2)]
        stored = [sem(c, f"p_stored{r}") for r in range(2)]
        modb_in, var_ready, rstd_ready, h_ready = (sem(c, f"p_{n}") for n in ("modb_in", "var_ready", "rstd_ready", "h_ready"))
        v_init, hps_ready, hT_ready, f_ready, v_ready = (sem(c, f"p_{n}") for n in ("v_init", "hps_ready", "hT_ready", "f_ready", "v_ready"))
        q1_ready, split_done, v_kept, v_step, g_step = (sem(c, f"p_{n}") for n in ("q1_ready", "split_done", "v_kept", "v_step", "g_step"))
        block = c.enter_context(nc.Block())
        NORM_STEPS, SPLIT_STEPS = 2 + TT + 1, 8
        STORES = 16 * (24 + TT)
        FREE = 1
        xv = g["x"].rearrange("b (u t p) e -> b u p t e", u=2, p=P)

        def batches(eng, body):
            with eng.Fori(0, B - 1) as it:
                for r in range(2):
                    body(it, r, True)
            for r in range(2):
                body(B - 1, r, r == 0)

        def pick(t, i):
            return t[i] if isinstance(i, int) else t[bass.ds(i, 1)].rearrange("a p t e -> (a p) t e")

        @block.sync
        def _(sp):
            def rows(b):
                m = g["modd"][b:b + 1, 0:2 * E] if isinstance(b, int) else g["modd"][bass.ds(b, 1), 0:2 * E]
                sp.dma_start(modb[:].rearrange("p k e -> p (k e)"), m.broadcast_to((P, 2 * E))).then_inc(modb_in, 16)

            for r in range(2):
                sp.dma_start(xs[r][:], xv[0, r]).then_inc(x_in[r], 16)
                if r == 0:
                    rows(0)

            def body(it, r, _):
                more = not isinstance(it, int)
                if more:
                    sp.wait_ge(h_ready, 2 * it + r + 1)
                    sp.dma_start(xs[r][:], pick(xv[:, r], it + 1)).then_inc(x_in[r], 16)
                    if r == 0:
                        sp.wait_ge(h_ready, 2 * it + 2)
                        rows(it + 1)
                for i in range(4):
                    dst = g["qd"] if i < 2 else g["kd"]
                    dv = dst.rearrange("(b q) f (g d) t -> b (q f) g d t", b=B, g=6)
                    sp.wait_ge(split_done, 8 * it + (4 * r + i + 1) + FREE)
                    for n, part in enumerate(Q_PART if i < 2 else K_PART):
                        to = dv[:, (i % 2) * 16:(i % 2) * 16 + 16, n, :, r * BLK:(r + 1) * BLK]
                        to = to[it] if isinstance(it, int) else to[bass.ds(it, 1)].rearrange("a f d t -> (a f) d t")
                        sp.dma_start(to, parts[r][:, i, part, :]).then_inc(stored[r], 16)
                sp.wait_ge(v_kept, 2 * it + (r + 1) + FREE)
                vv = g["vd"].rearrange("(b q) p s c -> b p q s c", b=B)
                for t in range(TT):
                    to = vv[:, :, :, r * TT + t, :]
                    to = to[it] if isinstance(it, int) else to[bass.ds(it, 1)].rearrange("a p q c -> (a p) q c")
                    sp.dma_start(to, vaug[r][:, t].rearrange("p (q h) c -> p q (h c)", h=2)).then_inc(stored[r], 16)

            batches(sp, body)
            for r in range(2):
                sp.wait_ge(stored[r], B * STORES + FREE)

        @block.gpsimd
        def _(pool):
            for s_ in (hps_ready, split_done, q1_ready, v_kept, v_ready, *stored):
                pool.sem_inc(s_, FREE)
            for r in range(2):
                pool.memset(vaug[r][:], 0.0).then_inc(g_step, 1)
            pool.wait_ge(g_step, 2)
            for r in range(2):
                pool.memset(vaug[r][:, :, :, 16:17], 1.0).then_inc(v_init, 1)
            with pool.Fori(0, 2 * B) as n:
                pool.wait_ge(var_ready, n + 1)
                pool.tensor_tensor(rstd[:], vare[:], g["neg_half"][:], ALU.pow).then_inc(rstd_ready, 1)

        @block.vector
        def _(dve):
            def norm(it, r, st):
                m = 2 * it + r
                dve.wait_ge(x_in[r], 16 * it + 16)
                for t in range(TT):
                    ins = dve.bn_stats(stats[:, t, :], xs[r][:, t, :])
                st.done(ins)
                dve.memset(carry[:], 0.0)
                for t in range(TT):
                    ins = dve.bn_aggr(mv[:, t, :], stats[:, t, :])
                st.done(ins)
                dve.tensor_scalar(vare[:], mv[:, :, 1], EPS, None, ALU.add).then_inc(var_ready, 1)
                dve.wait_ge(rstd_ready, m + 1)
                for t in range(TT):
                    st.done(dve.tensor_scalar(xn[:, t, :], xs[r][:, t, :], mv[:, t, 0:1], rstd[:, t:t + 1], ALU.subtract, ALU.mult))
                dve.wait_ge(modb_in, 16 * it + 16)
                st.done(dve.tensor_tensor(xn[:], xn[:], modb[:, 1:2, :].broadcast_to((P, TT, E)), ALU.mult))
                if not (isinstance(m, int) and m == 0):
                    dve.wait_ge(hps_ready, m - 1 + FREE)
                dve.tensor_tensor(h[r][:], xn[:], modb[:, 0:1, :].broadcast_to((P, TT, E)), ALU.add).then_inc(h_ready, 1)

            def body(it, r, ahead):
                st = Steps(dve, v_step, (NORM_STEPS + SPLIT_STEPS) * (2 * it + r) + NORM_STEPS)
                if ahead:
                    norm(it + r, 1 - r, st)
                    assert st.n == NORM_STEPS
                for i in range(4):
                    dve.wait_ge(q1_ready, 8 * it + (4 * r + i + 1) + FREE)
                    st.done(dve.tensor_tensor(res[i % 2][:], qf[:, i, :], parts[r][:, i, 0, :], ALU.subtract))
                    st.done(dve.tensor_copy(parts[r][:, i, 1, :], res[i % 2][:]))
                    dve.tensor_tensor(parts[r][:, i, 2, :], res[i % 2][:], parts[r][:, i, 1, :], ALU.subtract).then_inc(split_done, 1)

            norm(0, 0, Steps(dve, v_step))
            batches(dve, body)

        @block.tensor
        def _(pe):
            def turn(it, r):
                pe.wait_ge(h_ready, 2 * it + (r + 1))
                if not (isinstance(it, int) and it == 0 and r == 0):
                    pe.wait_ge(hT_ready, 2 * it + r)
                for ce in range(CE):
                    for t in range(TT):
                        last = pe.transpose(hps[:, ce, t * P:(t + 1) * P], h[r][:, t, ce * P:(ce + 1) * P], g["ident"][:])
                last.then_inc(hps_ready, 1)

            def body(it, r, ahead):
                pe.wait_ge(hT_ready, 2 * it + (r + 1))
                pe.wait_ge(q1_ready, 8 * it + 4 * r + FREE)
                for i in range(4):
                    w = g["wT"]["wq" if i < 2 else "wk"]
                    for ce in range(CE):
                        last = pe.matmul(fps[i][:], w[:, ce, (i % 2) * P:(i % 2 + 1) * P], hT[r][:, ce, :], start=(ce == 0), stop=(ce == CE - 1))
                    last.then_inc(f_ready, 1)
                if ahead:
                    turn(it + r, 1 - r)
                pe.wait_ge(v_kept, 2 * it + r + FREE)
                for t in range(TT):
                    for ce in range(CE):
                        last = pe.matmul(vps[:, t, :], hT[r][:, ce, t * P:(t + 1) * P], g["wT"]["wv"][:, ce, :], start=(ce == 0), stop=(ce == CE - 1))
                last.then_inc(v_ready, 1)

            turn(0, 0)
            batches(pe, body)

        @block.scalar
        def _(act):
            def keep(it, r):
                act.wait_ge(hps_ready, 2 * it + (r + 1) + FREE)
                if not (isinstance(it, int) and it == 0 and r == 0):
                    act.wait_ge(v_ready, 2 * it + r - 1 + FREE)
                act.activation(hT[r][:], hps[:], ACT.Copy).then_inc(hT_ready, 1)

            def body(it, r, ahead):
                act.wait_ge(stored[r], STORES * it + FREE)
                act.wait_ge(split_done, 8 * it + 4 * r + FREE)
                for i in range(4):
                    act.wait_ge(f_ready, 8 * it + (4 * r + i + 1))
                    scale = HD ** -0.5 if i < 2 else 1.0
                    act.activation(qf[:, i, :], fps[i][:], ACT.Copy, scale=scale)
                    act.activation(parts[r][:, i, 0, :], fps[i][:], ACT.Copy, scale=scale).then_inc(q1_ready, 1)
                if ahead:
                    keep(it + r, 1 - r)
                act.wait_ge(v_ready, 2 * it + (r + 1) + FREE)
                act.activation(vaug[r][:, :, :, 0:16], vps[:].rearrange("p t (h c) -> p t h c", c=16), ACT.Copy).then_inc(v_kept, 1)

            act.wait_ge(v_init, 2)
            keep(0, 0)
            batches(act, body)


def attend(nc, sb, pb, sem, g):
    with ExitStack() as c:
        qs, ks = g["qs"], g["ks"]
        vs = [sb(c, f"a_v{r}", [P, ST, 2 * VW]) for r in range(NBUF)]
        probs = [sb(c, f"a_p{r}", [P, 4, T]) for r in range(2)]
        zrow = sb(c, "a_zrow", [3, T], BF16)
        negmax = [sb(c, f"a_negmax{r}", [P, 32]) for r in range(2)]
        mrow = sb(c, "a_mrow", [32, P])
        mres = sb(c, "a_mres", [32, P])
        mparts = sb(c, "a_mparts", [32, 3, P], BF16)
        oT = sb(c, "a_oT", [P, T])
        mps = [pb(c, f"a_mps{r}", [P, T]) for r in range(2)]
        eps = [pb(c, f"a_eps{r}", [P, BLK]) for r in range(2)]
        ops = [pb(c, f"a_ops{r}", [P, BLK]) for r in range(2)]
        loaded = [sem(c, f"a_loaded{r}") for r in range(NBUF)]
        zeroed = sem(c, "a_zeroed")
        mscore = [sem(c, f"a_mscore{r}") for r in range(2)]
        mtaken = [sem(c, f"a_mtaken{r}") for r in range(2)]
        mstep, msplit, mplaced = sem(c, "a_mstep"), sem(c, "a_msplit"), sem(c, "a_mplaced")
        escore = [sem(c, f"a_escore{r}") for r in range(2)]
        edone = [sem(c, f"a_edone{r}") for r in range(2)]
        pv = [[sem(c, f"a_pv{s}{r}") for r in range(2)] for s in range(2)]
        okept, ostored = sem(c, "a_okept"), sem(c, "a_ostored")
        block = c.enter_context(nc.Block())
        FREE = 1

        def at(p, a, k=0):
            it, r = p
            return it * (4 * a) + (r * a + k)

        def after(p, n=1):
            return p[0], p[1] + n

        def slot(p, idx):
            it, r = p
            k = 65 + 33 * r + idx
            return k % 2, it * 66 + k // 2

        def slots(k):
            return [("item", 0, 0), ("turn", 0, 1)] if k == 0 else [("item", k, k + 1)]

        @block.sync
        def _(sp):
            def load(r, p):
                q4 = g["qd"][p].rearrange("a f s t -> s (a f) t") if not isinstance(p, int) else g["qd"][p].rearrange("f s t -> s f t")
                k4 = g["kd"][p].rearrange("a f s t -> s (a f) t") if not isinstance(p, int) else g["kd"][p].rearrange("f s t -> s f t")
                v4 = g["vd"][p].rearrange("a p s c -> (a p) s c") if not isinstance(p, int) else g["vd"][p]
                sp.dma_start(ks[r][0:SROWS], k4).then_inc(loaded[r], 16)
                sp.dma_start(qs[r][0:SROWS], q4).then_inc(loaded[r], 16)
                sp.dma_start(qs[r][MROW:MROW + 3], zrow[:].rearrange("p (a t) -> p a t", a=1).broadcast_to((3, 4, T))).then_inc(loaded[r], 16)
                sp.dma_start(vs[r][:], v4).then_inc(loaded[r], 16)

            def place(r, count):
                sp.wait_ge(msplit, count)
                for j in range(3):
                    sp.dma_start(qs[r][MROW + j:MROW + j + 1].rearrange("a f (t c) -> a (f t) c", c=P), mparts[:, j, :]).then_inc(mplaced, 16)

            def store(p, index):
                sp.wait_ge(okept, at(p, 2, 2) + FREE)
                sp.dma_start(g["od"][index].rearrange("a p t -> (a p) t") if not isinstance(index, int) else g["od"][index], oT[:]).then_inc(ostored, 16)

            sp.wait_ge(zeroed, 1)
            for q in range(3):
                load(q, q)
            for n in range(NEXP):
                sp.dma_start(g["w1s"][:, n], g["w1"][n].rearrange("(c p) h -> p c h", p=P)).then_inc(g["w_loaded"], 16)
            place(0, 1)
            place(1, 2)
            load(3, 3)

            def period(p, quad, places, loads):
                it, r = p
                if places:
                    place((r + 2) % NBUF, at(p, 1, 3))
                store(p, quad(0))
                if loads:
                    sp.wait_ge(pv[1][1], at(p, 4, 4) + FREE)
                    load(r, quad(4))

            with sp.Fori(0, QUADS // 4 - 1) as it:
                for r in range(4):
                    period((it, r), lambda n: bass.ds(it * 4 + (r + n), 1), True, True)
            for r in range(4):
                period((QUADS // 4 - 1, r), lambda n: QUADS - 4 + r + n, r < 2, False)
            sp.wait_ge(ostored, 16 * QUADS + FREE)

        @block.gpsimd
        def _(pool):
            pool.memset(zrow[:], 0.0).then_inc(zeroed, 1)
            for s_ in (okept, ostored, *pv[0], *pv[1]):
                pool.sem_inc(s_, FREE)

        @block.tensor
        def _(pe):
            def item(buf, uses, r, k, halves=(0, 1)):
                f, t = k // ST, k % ST
                if 0 in halves and not (isinstance(uses, int) and uses == 0):
                    pe.wait_ge(mtaken[buf], uses)
                for hlf in halves:
                    last = pe.matmul(mps[buf][:, hlf * BLK:(hlf + 1) * BLK], qs[r][:, f, t * P:(t + 1) * P],
                                     ks[r][:, f, hlf * BLK:(hlf + 1) * BLK], start=True, stop=True)
                if 1 in halves:
                    last.then_inc(mscore[buf], 1)

            def turn(buf, uses, par):
                pe.wait_ge(mtaken[buf], uses)
                pe.matmul(mps[buf][0:32, 0:P], negmax[par][:], g["ident"][:], start=True, stop=True).then_inc(mscore[buf], 1)

            def max_step(p, k, items, turns, halves=(0, 1)):
                r = p[1]
                for kind, k, idx in slots(k):
                    if kind == "item" and items:
                        if k == 0 and 0 in halves:
                            pe.wait_ge(loaded[(r + 2) % NBUF], p[0] * LOAD_INC + LOAD_INC * ((r + 2) // NBUF + 1))
                        item(*slot(p, idx), (r + 2) % NBUF, k, halves)
                    if kind == "turn" and turns and 1 in halves:
                        turn(*slot(p, idx), (r + 1) % 2)

            def score(p, i, f, hlf):
                r = p[1] % NBUF
                if i or f or not (isinstance(p[0], int) and p == (0, 0)):
                    pe.wait_ge(edone[hlf], at(p, 32, 4 * i + f))
                pe.matmul(eps[hlf][:], ks[r][:, f, i * P:(i + 1) * P], qs[r][:, f, hlf * BLK:(hlf + 1) * BLK],
                          start=True, stop=True).then_inc(escore[hlf], 1)

            def product(p, i, hlf):
                pe.wait_ge(edone[hlf], at(p, 32, 4 * i + 4))
                if i == 0:
                    pe.wait_ge(okept, at(p, 2) + FREE)
                for f in range(4):
                    last = pe.matmul(ops[hlf][32 * f:32 * f + VW, :], vs[p[1] % NBUF][:, i, (f // 2) * VW:(f // 2 + 1) * VW],
                                     probs[i % 2][:, f, hlf * BLK:(hlf + 1) * BLK], start=(i == 0), stop=(i == ST - 1))
                last.then_inc(pv[i % 2][hlf], 1)

            def key_tile(p, i, items, turns, before):
                for f in range(0, 4, 2):
                    k = 4 * i + f
                    score(p, i, f, 0)
                    max_step(p, k, items, turns)
                    max_step(p, k + 1, items, turns, halves=(0,))
                    score(p, i, f, 1)
                    max_step(p, k + 1, items, turns, halves=(1,))
                    score(p, i, f + 1, 0)
                    if before:
                        product(*before, f // 2)
                    score(p, i, f + 1, 1)

            def head(p, items=True, turns=True, before=None):
                pe.wait_ge(mplaced, at(p, 48, 48))
                key_tile(p, 0, items, turns, before and (before, ST - 1))

            def tail(p, items=True):
                for i in range(1, ST):
                    key_tile(p, i, items, False, (p, i - 1))

            pe.wait_ge(loaded[0], LOAD_INC)
            for k in range(32):
                item(k % 2, k // 2, 0, k)
            for k in range(32):
                max_step((0, -1), k, True, True)
            head((0, 0))
            with pe.Fori(0, QUADS // 4 - 1) as it:
                for r in range(4):
                    tail((it, r))
                    head((it, r + 1), before=(it, r))
            for r in range(4):
                p = (QUADS // 4 - 1, r)
                tail(p, items=r < 2)
                if r < 3:
                    head(after(p), items=r < 1, turns=r < 2, before=p)
            for hlf in range(2):
                product(p, ST - 1, hlf)

        @block.vector
        def _(dve):
            def item(buf, uses, par, k):
                dve.wait_ge(mscore[buf], uses + 1)
                dve.tensor_reduce(negmax[par][:, k:k + 1], mps[buf][:], AX.X, ALU.max, negate=True).then_inc(mtaken[buf], 1)

            def turn(buf, uses, p):
                dve.wait_ge(mscore[buf], uses + 1)
                dve.tensor_copy(mrow[:], mps[buf][0:32, 0:P]).then_inc(mtaken[buf], 1)
                dve.wait_ge(mtaken[buf], uses + 1)
                if p[1] != -1:
                    dve.wait_ge(mplaced, at(p, 48, 48))
                dve.tensor_copy(mparts[:, 0, :], mrow[:]).then_inc(mstep, 1)
                dve.wait_ge(mstep, at(p, 3, 4))
                dve.tensor_tensor(mres[:], mrow[:], mparts[:, 0, :], ALU.subtract).then_inc(mstep, 1)
                dve.wait_ge(mstep, at(p, 3, 5))
                dve.tensor_copy(mparts[:, 1, :], mres[:]).then_inc(mstep, 1)
                dve.wait_ge(mstep, at(p, 3, 6))
                dve.tensor_tensor(mparts[:, 2, :], mres[:], mparts[:, 1, :], ALU.subtract).then_inc(msplit, 1)

            def steps(p, ks_, items=True, turns=True):
                for k in ks_:
                    for kind, k, idx in slots(k):
                        if kind == "item" and items:
                            item(*slot(p, idx), p[1] % 2, k)
                        if kind == "turn" and turns:
                            turn(*slot(p, idx), p)

            for k in range(32):
                item(k % 2, k // 2, 0, k)
            steps((0, -1), range(32))
            steps((0, 0), range(4))
            with dve.Fori(0, QUADS // 4 - 1) as it:
                for r in range(4):
                    steps((it, r), range(4, 32))
                    steps((it, r + 1), range(4))
            for r in range(4):
                p = (QUADS // 4 - 1, r)
                steps(p, range(4, 32), items=r < 2, turns=False)
                steps(after(p), range(4), items=r < 1, turns=r < 2)

        @block.scalar
        def _(act):
            def exps(p, i):
                for f in range(4):
                    for hlf in range(2):
                        act.wait_ge(escore[hlf], at(p, 32, 4 * i + f + 1))
                        if f == 0:
                            act.wait_ge(pv[i % 2][hlf], at(p, 4, i // 2) + FREE)
                        act.activation(probs[i % 2][:, f, hlf * BLK:(hlf + 1) * BLK], eps[hlf][:], ACT.Exp).then_inc(edone[hlf], 1)

            def keep(p):
                act.wait_ge(ostored, at(p, 16) + FREE)
                for hlf in range(2):
                    act.wait_ge(pv[1][hlf], at(p, 4, 4) + FREE)
                    act.activation(oT[:, hlf * BLK:(hlf + 1) * BLK], ops[hlf][:], ACT.Copy).then_inc(okept, 1)

            exps((0, 0), 0)
            with act.Fori(0, QUADS // 4 - 1) as it:
                for r in range(4):
                    for i in range(1, ST):
                        exps((it, r), i)
                    exps((it, r + 1), 0)
                    keep((it, r))
            for r in range(4):
                p = (QUADS // 4 - 1, r)
                for i in range(1, ST):
                    exps(p, i)
                if r < 3:
                    exps(after(p), 0)
                keep(p)


def route(nc, sb, pb, sem, g):
    with ExitStack() as c:
        def two(name, shape, dt=FP32):
            return [sb(c, f"{name}{r}", shape, dt) for r in range(2)]

        os_ = two("m_o", [P, QB, BLK])
        xs = two("m_x", [P, TT, E])
        modb = sb(c, "m_modb", [P, 3, E])
        wog = sb(c, "m_wog", [P, CE, E])
        rec = sb(c, "m_rec", [P, 32])
        rl = sb(c, "m_rl", [P, 32])
        A = sb(c, "m_A", [P, 32, 16])
        D = two("m_D", [P, TT * HEADS, 16])
        tmp = two("m_tmp", [P, TT, E])
        ss = two("m_ss", [P, TT * HEADS])
        sse = two("m_sse", [P, TT * HEADS])
        root = two("m_root", [P, TT * HEADS])
        rs = two("m_rs", [P, TT * HEADS])
        nt = sb(c, "m_newton", [P, TT * HEADS])
        an = two("m_an", [P, TT, E])
        aT = two("m_aT", [P, CE, BLK])
        x1 = two("m_x1", [P, TT, E])
        stats = sb(c, "m_stats", [P, TT, 6])
        mv = two("m_mv", [P, TT, 2])
        vare = two("m_vare", [P, TT])
        rstd = two("m_rstd", [P, TT])
        carry = sb(c, "m_carry", [P, 1])
        pcarry = sb(c, "m_pcarry", [P, 2])
        h2 = two("m_h2", [P, TT, E])
        hT = two("m_hT", [P, CE, BLK])
        lg = sb(c, "m_lg", [P, TT, NEXP])
        top8 = sb(c, "m_top8", [P, TT, 8])
        idx8 = sb(c, "m_idx8", [P, TT, 8], U32)
        cho = two("m_cho", [P, 3, 2, TT])
        hot = two("m_hot", [P, 2, TT, NEXP])
        both = two("m_both", [P, TT, NEXP])
        msum = sb(c, "m_msum", [P, NEXP])
        seen = two("m_seen", [P, NEXP])
        slotr = sb(c, "m_slotr", [P, TT, NEXP])
        prod = sb(c, "m_prod", [P, 2, TT, NEXP])
        pos = two("m_pos", [P, 2 * TT], U32)
        tri = sb(c, "m_tri", [P, P])
        ones = sb(c, "m_ones", [P, P])
        iotai = sb(c, "m_iotai", [P, NTAB], I32)
        big = [pb(c, f"m_big{i}", [P, 1024]) for i in range(2)]
        gen = [pb(c, f"m_gen{i}", [P, 1024]) for i in range(2)]
        names = ("modb_in", "turned", "cl_ready", "sq_ready", "sse_ready", "root_ready", "aT_ready", "wog_ready",
                 "var_ready", "rstd_ready", "h2_ready", "hT_ready", "iota_ready", "tri_ready", "x_added", "both_ready",
                 "rank_ps", "rank_taken", "pos_ready", "an_ready", "aT_ps", "wo_ps", "hT_ps", "lg_ps", "v_step", "g_step",
                 "count_ps", "h2_free", "carried", "tables_step")
        S = {n: sem(c, f"m_{n}") for n in names}
        turn_taken = [sem(c, f"m_turn_taken{i}") for i in range(2)]
        o_in = [sem(c, f"m_o_in{i}") for i in range(2)]
        x_in = [sem(c, f"m_x_in{i}") for i in range(2)]
        x1_kept = [sem(c, f"m_x1_kept{i}") for i in range(2)]
        cho_kept = [sem(c, f"m_cho_kept{i}") for i in range(2)]
        sent = [sem(c, f"m_sent{i}") for i in range(2)]
        block = c.enter_context(nc.Block())
        FREE = 1
        V_STEPS = 2 * (3 * TT + 1 + 1 + 6 + 2 + TT + 1 + 8 + 3)
        xv = g["x"].rearrange("b (u t p) e -> b u p t e", u=2, p=P)
        odv = g["od"].rearrange("(b q) p t -> b p q t", b=B)
        SENT = 16 * 2 * TT
        flat = lambda v: v[:].rearrange("p t e -> p (t e)")

        @block.sync
        def _(sp):
            def load(b):
                one = isinstance(b, int)
                for r in range(2):
                    o = odv[:, :, :, r * BLK:(r + 1) * BLK]
                    sp.dma_start(os_[r][:], o[b] if one else o[bass.ds(b, 1)].rearrange("a p q t -> (a p) q t")).then_inc(o_in[r], 16)
                for r in range(2):
                    sp.dma_start(xs[r][:], xv[b, r] if one else xv[bass.ds(b, 1), r].rearrange("a p t e -> (a p) t e")).then_inc(x_in[r], 16)

            def rows(b):
                m = g["modd"][b:b + 1, 2 * E:5 * E] if isinstance(b, int) else g["modd"][bass.ds(b, 1), 2 * E:5 * E]
                sp.dma_start(modb[:].rearrange("p k e -> p (k e)"), m.broadcast_to((P, 3 * E))).then_inc(S["modb_in"], 16)

            def store(it, n, ready, src, dst, done, shift=0):
                for r in range(2):
                    sp.wait_ge(ready, 2 * it + (r + 1) + shift)
                    to = dst[it * 2 + r] if isinstance(it, int) else dst[bass.ds(2 * it + r, 1)].rearrange("a p n -> (a p) n")
                    sp.dma_start(to, src[r]).then_inc(done[r], 16)

            def body(it, more):
                if more:
                    sp.wait_ge(S["x_added"], 2 * it + 2)
                    load(it + 1)
                store(it, 0, S["h2_ready"], [flat(x1[r]) for r in range(2)], g["x1d"], x1_kept)
                if more:
                    rows(it + 1)
                store(it, 1, S["pos_ready"], [cho[r][:].rearrange("p a k t -> p (a k t)") for r in range(2)], g["chod"], cho_kept)

            rows(0)
            load(0)
            for n in range(NEXP):
                sp.dma_start(g["w2s"][:, n], g["w2"][n].rearrange("(c p) e -> p c e", p=P)).then_inc(g["w_loaded"], 16)
            with sp.Fori(0, B - 1) as it:
                body(it, True)
            body(B - 1, False)
            for r in range(2):
                sp.wait_ge(x1_kept[r], 16 * B + FREE)
                sp.wait_ge(cho_kept[r], 16 * B + FREE)

        @block.gpsimd
        def _(pool):
            for s_ in (*x1_kept, *cho_kept, *turn_taken, S["h2_free"], S["rank_taken"], S["rank_ps"], S["wo_ps"]):
                pool.sem_inc(s_, FREE)
            pool.iota(iotai[:], [[1, NTAB]], base=0, channel_multiplier=0).then_inc(S["g_step"], 1)
            pool.memset(ones[:], 1.0).then_inc(S["g_step"], 1)
            pool.wait_ge(S["g_step"], 2)
            pool.tensor_copy(g["iota"][:], iotai[:, 0:NEXP]).then_inc(S["iota_ready"], 1)
            pool.affine_select(out=tri[:], in_=ones[:], compare_op=ALU.is_gt, fill=0.0, base=0, pattern=[[1, P]], channel_multiplier=-1).then_inc(S["tri_ready"], 1)
            with pool.Fori(0, B) as it:
                for r in range(2):
                    pool.wait_ge(S["var_ready"], 2 * it + r + 1)
                    pool.tensor_tensor(rstd[r][:], vare[r][:], g["neg_half"][:], ALU.pow).then_inc(S["rstd_ready"], 1)
                for r in range(2):
                    pool.wait_ge(S["pos_ready"], 2 * it + r + 1)
                    pool.tensor_tensor(pcarry[:, r:r + 1], g["neg_half"][:, 0:1], g["neg_half"][:, 0:1], ALU.mult).then_inc(S["carried"], 1)
                    for k in range(2):
                        for t in range(TT):
                            pool.indirect_dma_start(out=g["xg"], out_offset=bass.IndirectOffsetOnAxis(ap=pos[r][:, k * TT + t:k * TT + t + 1], axis=0),
                                                    in_=h2[r][:, t, :], in_offset=None).then_inc(sent[r], 16)
                for r in range(2):
                    pool.wait_ge(sent[r], SENT * (it + 1))
                pool.wait_ge(S["carried"], 2 * it + 2)
                pool.sem_inc(S["h2_free"], 1)

        @block.tensor
        def _(pe):
            def turn(src, dst, out_sem):
                dv = dst[:].rearrange("p (c t) -> p c t", c=CE)
                for ce in range(CE):
                    for t in range(TT):
                        last = pe.transpose(dv[:, ce, t * P:(t + 1) * P], src[:, t, ce * P:(ce + 1) * P], g["ident"][:])
                last.then_inc(out_sem, 1)

            pe.wait_ge(S["tri_ready"], 1)
            with pe.Fori(0, B) as it:
                for r in range(2):
                    n = 2 * it + r
                    pe.wait_ge(o_in[r], 16 * it + 16)
                    for t in range(TT):
                        pe.wait_ge(turn_taken[t % 2], n * 2 + t // 2 + FREE)
                        for q in range(QB):
                            last = pe.transpose(big[t % 2][:, q * P:(q + 1) * P], os_[r][:, q, t * P:(t + 1) * P], g["ident"][:])
                        last.then_inc(S["turned"], 1)
                pe.wait_ge(S["rank_taken"], 2 * it + FREE)
                for r in range(2):
                    n = 2 * it + r
                    pe.wait_ge(S["an_ready"], n + 1)
                    turn(an[r], gen[r], S["aT_ps"])
                pe.wait_ge(S["wog_ready"], it + 1)
                for r in range(2):
                    n = 2 * it + r
                    pe.wait_ge(S["aT_ready"], n + 1)
                    gv = gen[r][:].rearrange("p (t e) -> p t e", t=TT)
                    for t in range(TT):
                        for ce in range(CE):
                            last = pe.matmul(gv[:, t, :], aT[r][:, ce, t * P:(t + 1) * P], wog[:, ce, :], start=(ce == 0), stop=(ce == CE - 1))
                    last.then_inc(S["wo_ps"], 1)
                for r in range(2):
                    pe.wait_ge(S["h2_ready"], 2 * it + r + 1)
                    turn(h2[r], gen[r], S["hT_ps"])
                for r in range(2):
                    pe.wait_ge(S["hT_ready"], 2 * it + r + 1)
                    for t in range(TT):
                        for ce in range(CE):
                            last = pe.matmul(gen[r][:, t * NEXP:(t + 1) * NEXP], hT[r][:, ce, t * P:(t + 1) * P], g["rT"][:, ce, :], start=(ce == 0), stop=(ce == CE - 1))
                    last.then_inc(S["lg_ps"], 1)
                for r in range(2):
                    pe.wait_ge(S["both_ready"], 2 * it + r + 1)
                    rk = gen[r][:, BLK:BLK + TT * NEXP].rearrange("p (t n) -> p t n", t=TT)
                    pe.matmul(rk, tri[:], both[r][:], start=True, stop=False)
                    for t in range(TT - 1):
                        pe.matmul(rk[:, t + 1:TT, :], ones[:], both[r][:, t:t + 1, :].broadcast_to((P, TT - 1 - t, NEXP)), start=False, stop=False)
                    pe.matmul(rk, ones[:], seen[r][:].rearrange("p (o n) -> p o n", o=1).broadcast_to((P, TT, NEXP)), start=False, stop=True).then_inc(S["rank_ps"], 1)
            pe.wait_ge(S["pos_ready"], 2 * B)
            pe.matmul(big[0][:, 0:NEXP], ones[:], seen[0][:], start=True, stop=True).then_inc(S["count_ps"], 1)

        @block.scalar
        def _(act):
            with act.Fori(0, B) as it:
                for r in range(2):
                    act.wait_ge(S["cl_ready"], 2 * it + r + 1)
                    act.activation(flat(tmp[r]), flat(tmp[r]), ACT.Square).then_inc(S["sq_ready"], 1)
                for r in range(2):
                    act.wait_ge(S["sse_ready"], 2 * it + r + 1)
                    act.activation(root[r][:], sse[r][:], ACT.Sqrt, scale=ROOT_SCALE * ROOT_SCALE * 4).then_inc(S["root_ready"], 1)
                for r in range(2):
                    act.wait_ge(S["aT_ps"], 2 * it + r + 1)
                    act.activation(aT[r][:].rearrange("p c t -> p (c t)"), gen[r][:], ACT.Copy).then_inc(S["aT_ready"], 1)
                for r in range(2):
                    act.wait_ge(S["hT_ps"], 2 * it + r + 1)
                    act.activation(hT[r][:].rearrange("p c t -> p (c t)"), gen[r][:], ACT.Copy).then_inc(S["hT_ready"], 1)

        @block.vector
        def _(dve):
            wide = (P, TT, E)
            heads = (P, TT * HEADS, 16)
            first_row, iota, count = g["first_row"], g["iota"], g["count"]
            dve.wait_ge(S["iota_ready"], 1)
            dve.tensor_scalar(first_row[:], iota[:], float(CAP), None, ALU.mult)
            init = Steps(dve, S["tables_step"])
            init.done(dve.memset(seen[0][:], 0.0))
            with dve.Fori(0, B) as it:
                st = Steps(dve, S["v_step"], V_STEPS * it)
                dve.wait_ge(S["modb_in"], 16 * it + 16)
                dve.wait_ge(S["wo_ps"], 2 * it + FREE)
                dve.tensor_tensor(wog[:], g["wT"]["wo"][:], modb[:, 0:1, :].broadcast_to((P, CE, E)), ALU.mult).then_inc(S["wog_ready"], 1)
                for r in range(2):
                    n = 2 * it + r
                    for t in range(TT):
                        dve.wait_ge(S["turned"], n * TT + t + 1)
                        tv = big[t % 2][:].rearrange("p (f c) -> p f c", c=32)
                        st.done(dve.reciprocal(rec[:], tv[:, :, 16]))
                        st.done(dve.tensor_tensor(rl[:].rearrange("p (h a) -> p h a", a=2), rec[:].rearrange("p (h a) -> p h a", a=2),
                                                  g["lam_sign"][:].rearrange("p (o a) -> p o a", o=1).broadcast_to((P, HEADS, 2)), ALU.mult))
                        dve.tensor_tensor(A[:], tv[:, :, 0:16], rl[:].rearrange("p (f o) -> p f o", o=1).broadcast_to((P, 32, 16)), ALU.mult).then_inc(turn_taken[t % 2], 1)
                        dve.wait_ge(turn_taken[t % 2], n * 2 + (t // 2 + 1) + FREE)
                        av = A[:].rearrange("p (h a) c -> p h a c", a=2)
                        st.done(dve.tensor_tensor(D[r][:, t * HEADS:(t + 1) * HEADS, :], av[:, :, 0, :], av[:, :, 1, :], ALU.add))
                    tflat = tmp[r][:].rearrange("p t (h c) -> p (t h) c", c=16)
                    st.done(dve.tensor_scalar(tflat, D[r][:], 1.0 / 8, RANGE, ALU.mult, ALU.min))
                    dve.tensor_scalar(tflat, tflat, -RANGE, None, ALU.max).then_inc(S["cl_ready"], 1)
                for r in range(2):
                    tflat = tmp[r][:].rearrange("p t (h c) -> p (t h) c", c=16)
                    dve.wait_ge(S["sq_ready"], 2 * it + r + 1)
                    st.done(dve.reduce_sum(ss[r][:], tflat, axis=AX.X))
                    dve.tensor_scalar(sse[r][:], ss[r][:], EPS / 4, RANGE * RANGE, ALU.add, ALU.min).then_inc(S["sse_ready"], 1)
                for r in range(2):
                    anf = an[r][:].rearrange("p t (h c) -> p (t h) c", c=16)
                    dve.wait_ge(S["root_ready"], 2 * it + r + 1)
                    st.done(dve.reciprocal(rs[r][:], root[r][:]))
                    st.done(dve.tensor_tensor(nt[:], sse[r][:], rs[r][:], ALU.mult))
                    st.done(dve.tensor_tensor(nt[:], nt[:], rs[r][:], ALU.mult))
                    st.done(dve.tensor_scalar(nt[:], nt[:], -2.0 * ROOT_SCALE * ROOT_SCALE, 1.5, ALU.mult, ALU.add))
                    st.done(dve.tensor_tensor(rs[r][:], rs[r][:], nt[:], ALU.mult))
                    st.done(dve.scalar_tensor_tensor(rs[r][:], ss[r][:], RANGE * RANGE, rs[r][:], ALU.is_lt, ALU.mult))
                    dve.tensor_tensor(anf, D[r][:], rs[r][:].rearrange("p (f o) -> p f o", o=1).broadcast_to(heads), ALU.mult).then_inc(S["an_ready"], 1)
                for r in range(2):
                    n = 2 * it + r
                    dve.wait_ge(S["wo_ps"], n + 1 + FREE)
                    dve.wait_ge(x_in[r], 16 * it + 16)
                    dve.wait_ge(x1_kept[r], 16 * it + FREE)
                    dve.tensor_tensor(x1[r][:], gen[r][:].rearrange("p (t e) -> p t e", t=TT), xs[r][:], ALU.add).then_inc(S["x_added"], 1)
                    dve.wait_ge(S["x_added"], n + 1)
                    for t in range(TT):
                        ins = dve.bn_stats(stats[:, t, :], x1[r][:, t, :])
                    st.done(ins)
                    dve.memset(carry[:], 0.0)
                    for t in range(TT):
                        ins = dve.bn_aggr(mv[r][:, t, :], stats[:, t, :])
                    st.done(ins)
                    dve.tensor_scalar(vare[r][:], mv[r][:, :, 1], EPS, None, ALU.add).then_inc(S["var_ready"], 1)
                for r in range(2):
                    n = 2 * it + r
                    dve.wait_ge(S["rstd_ready"], n + 1)
                    for t in range(TT):
                        ins = dve.tensor_scalar(tmp[r][:, t, :], x1[r][:, t, :], mv[r][:, t, 0:1], rstd[r][:, t:t + 1], ALU.subtract, ALU.mult)
                        st.done(ins)
                    st.done(dve.tensor_tensor(tmp[r][:], tmp[r][:], modb[:, 2:3, :].broadcast_to(wide), ALU.mult))
                    dve.wait_ge(S["h2_free"], it + FREE)
                    dve.tensor_tensor(h2[r][:], tmp[r][:], modb[:, 1:2, :].broadcast_to(wide), ALU.add).then_inc(S["h2_ready"], 1)
                for r in range(2):
                    n = 2 * it + r
                    dve.wait_ge(S["lg_ps"], n + 1)
                    st.done(dve.tensor_copy(lg[:].rearrange("p t n -> p (t n)"), gen[r][:, 0:TT * NEXP]))
                    dve.memset(carry[:], 0.0)
                    for t in range(TT):
                        ins = dve.max(top8[:, t, :], lg[:, t, :])
                    st.done(ins)
                    dve.memset(carry[:], 0.0)
                    for t in range(TT):
                        ins = dve.max_index(idx8[:, t, :], top8[:, t, :], lg[:, t, :])
                    st.done(ins)
                    dve.wait_ge(cho_kept[r], 16 * it + FREE)
                    dve.tensor_copy(cho[r][:, 2], top8[:, :, 0:2].rearrange("p t k -> p k t"))
                    st.done(dve.tensor_copy(cho[r][:, 1], idx8[:, :, 0:2].rearrange("p t k -> p k t")))
                    for k in range(2):
                        ins = dve.tensor_tensor(hot[r][:, k], iota[:].rearrange("p (o n) -> p o n", o=1).broadcast_to((P, TT, NEXP)),
                                                cho[r][:, 1, k, :].rearrange("p (t o) -> p t o", o=1).broadcast_to((P, TT, NEXP)), ALU.is_equal)
                    st.done(ins)
                    dve.tensor_tensor(both[r][:], hot[r][:, 0], hot[r][:, 1], ALU.add).then_inc(S["both_ready"], 1)
                    dve.wait_ge(S["both_ready"], n + 1)
                    st.done(dve.reduce_sum(msum[:], both[r][:].rearrange("p t n -> p n t"), axis=AX.X))
                    dve.wait_ge(S["rank_ps"], n + FREE)
                    st.done(dve.tensor_tensor(seen[1 - r][:], seen[r][:], msum[:], ALU.add))
                    st.done(dve.memset(carry[:], 0.0))
                for r in range(2):
                    n = 2 * it + r
                    dve.wait_ge(S["rank_ps"], n + 1 + FREE)
                    rk = gen[r][:, BLK:BLK + TT * NEXP].rearrange("p (t n) -> p t n", t=TT)
                    dve.tensor_tensor(slotr[:], rk, first_row[:].rearrange("p (o n) -> p o n", o=1).broadcast_to((P, TT, NEXP)), ALU.add).then_inc(S["rank_taken"], 1)
                    dve.wait_ge(S["rank_taken"], n + 1 + FREE)
                    for k in range(2):
                        ins = dve.tensor_tensor(prod[:, k], hot[r][:, k], slotr[:], ALU.mult)
                    st.done(ins)
                    st.done(dve.reduce_sum(cho[r][:, 0], prod[:], axis=AX.X))
                    dve.tensor_copy(pos[r][:], cho[r][:, 0].rearrange("p k t -> p (k t)")).then_inc(S["pos_ready"], 1)
                    st.done(dve.memset(carry[:], 0.0))
                assert st.n == V_STEPS, (st.n, V_STEPS)

            tailf, ntile, ncum, ef, mf, jf = (sb(c, f"m_{n}", [P, k]) for n, k in
                                              (("tailf", NEXP), ("ntile", NEXP), ("ncum", NEXP), ("ef", NTAB), ("mf", NTAB), ("jf", NTAB)))
            ntilei = sb(c, "m_ntilei", [P, NEXP], I32)
            ge, gc = sb(c, "m_ge", [P, NTAB, NEXP]), sb(c, "m_gc", [P, NTAB, NEXP])
            e = init
            dve.wait_ge(S["count_ps"], 1)
            e.done(dve.tensor_copy(count[:], big[0][:, 0:NEXP]))
            e.done(dve.tensor_tensor(tailf[:], count[:], first_row[:], ALU.add))
            e.done(dve.tensor_copy(g["tail"][:], tailf[:]))
            e.done(dve.tensor_scalar(ntile[:], count[:], float(P - 1), None, ALU.add))
            e.done(dve.tensor_copy(ntilei[:], ntile[:]))
            e.done(dve.tensor_scalar(ntilei[:], ntilei[:], P.bit_length() - 1, None, ALU.arith_shift_right))
            e.done(dve.tensor_copy(ntile[:], ntilei[:]))
            e.done(dve.tensor_copy(ncum[:], ntile[:]))
            for n in range(1, NEXP):
                e.done(dve.tensor_tensor(ncum[:, n:n + 1], ncum[:, n:n + 1], ncum[:, n - 1:n], ALU.add))
            e.done(dve.tensor_tensor(ntile[:], ncum[:], ntile[:], ALU.subtract))
            e.done(dve.scalar_tensor_tensor(g["close_up"][:], ntile[:], float(P), first_row[:], ALU.mult, ALU.subtract))
            e.done(dve.tensor_copy(jf[:], iotai[:]))
            nb = ncum[:].rearrange("p (o n) -> p o n", o=1).broadcast_to((P, NTAB, NEXP))
            jb = jf[:].rearrange("p (j o) -> p j o", o=1).broadcast_to((P, NTAB, NEXP))
            e.done(dve.tensor_tensor(ge[:], jb, nb, ALU.is_ge))
            e.done(dve.reduce_sum(ef[:], ge[:], axis=AX.X))
            e.done(dve.tensor_tensor(gc[:], ge[:], nb, ALU.mult))
            e.done(dve.reduce_max(mf[:], gc[:], AX.X))
            e.done(dve.tensor_tensor(mf[:], jf[:], mf[:], ALU.subtract))
            e.done(dve.tensor_scalar(mf[:], mf[:], float(P), None, ALU.mult))
            e.done(dve.scalar_tensor_tensor(mf[:], ef[:], float(CAP), mf[:], ALU.mult, ALU.add))
            e.done(dve.tensor_scalar(mf[:], mf[:], float(NEXP * CAP), None, ALU.min))
            e.done(dve.tensor_scalar(ef[:], ef[:], float(NEXP - 1), None, ALU.min))
            e.done(dve.tensor_copy(g["row_of"][:], mf[:]))
            e.done(dve.tensor_copy(g["expert_of"][:], ef[:]))


def experts(nc, sb, pb, sem, g):
    with ExitStack() as c:
        def many(make, name, shape, n=2, dt=FP32):
            return [make(c, f"{name}{r}", shape, dt) for r in range(n)]

        zrows = sb(c, "e_zrows", [P, E])
        xt = many(sb, "e_x", [P, E], NX)
        xT = many(sb, "e_xT", [P, CE, P])
        w1t = many(sb, "e_w1", [P, CE, HID])
        rl = many(sb, "e_relu", [P, CH, P])
        hT = many(sb, "e_hT", [P, CH, P])
        ys = many(sb, "e_y", [P, E], NX)
        cho = sb(c, "c_cho", [P, 2 * B, 3, 2 * TT])
        hot = sb(c, "c_hot", [P, 2 * TT, NEXP])
        shift = sb(c, "c_shift", [P, 2 * B, 2 * TT])
        posall = sb(c, "c_posall", [P, 2 * B, 2 * TT], U32)
        wt = sb(c, "c_wt", [P, 2 * B, 2, TT])
        ediff = sb(c, "c_ediff", [P, 2 * B, TT])
        pos = many(sb, "c_pos", [P, 2 * TT], dt=U32)
        wcur = many(sb, "c_wcur", [P, 2, TT])
        x1 = many(sb, "c_x1", [P, TT, E])
        yk = many(sb, "c_yk", [P, 2, TT, E])
        modb = many(sb, "c_gb", [P, E])
        z = sb(c, "c_z", [P, TT, E])
        og = many(sb, "c_out", [P, TT, E])
        pcarry = sb(c, "c_pcarry", [P, 2])
        xps = many(pb, "e_xps", [P, 512])
        hps = many(pb, "e_hps", [P, HID])
        yps = many(pb, "e_yps", [P, 512])

        def sems(name, n=2):
            return [sem(c, f"e_{name}{r}") for r in range(n)]

        x_in, y_stored = sems("x_in", NX), sems("y_stored", NX)
        x_turned, xT_ready, w1_ready, hid_ps, relu_done, hT_ready, y_ps, y_ready = (
            sems(n) for n in ("x_turned", "xT_ready", "w1_ready", "hid_ps", "relu_done", "hT_ready", "y_ps", "y_ready"))
        z_ready, z_stored, cho_in, d_step, diff_ready, exp_ready, rows_written = (
            sem(c, f"e_{n}") for n in ("z_ready", "z_stored", "cho_in", "d_step", "diff_ready", "exp_ready", "rows_written"))
        in_, fetched, out_ready, stored = (sems(n) for n in ("in", "fetched", "out_ready", "stored"))
        picked, carried, v_step = sem(c, "e_picked"), sem(c, "e_carried"), sem(c, "e_v_step")
        block = c.enter_context(nc.Block())
        rows_of = lambda t, v: t[bass.ds(v, P), :]
        ov = g["out"].rearrange("b (u t p) e -> b u p t e", u=2, p=P)
        FREE = 1
        ROUNDS = NTILE // NX
        V_STEPS = 2 * (2 * TT + 1)

        @block.gpsimd
        def _(pool):
            pool.memset(zrows[:], 0.0).then_inc(z_ready, 1)
            for s_ in (*x_turned, *xT_ready, *hid_ps, *relu_done, *hT_ready, *y_ps, *y_ready, *y_stored, *out_ready, *stored):
                pool.sem_inc(s_, FREE)
            pool.wait_ge(rows_written, 1)
            with pool.Fori(0, B) as it:
                for r in range(2):
                    pool.wait_ge(picked, 2 * it + r + 1)
                    pool.wait_ge(out_ready[r], it + FREE)
                    pool.tensor_tensor(pcarry[:, r:r + 1], g["neg_half"][:, 0:1], g["neg_half"][:, 0:1], ALU.mult).then_inc(carried, 1)
                    for k in range(2):
                        for t in range(TT):
                            pool.indirect_dma_start(out=yk[r][:, k, t, :], out_offset=None, in_=g["yg"],
                                                    in_offset=bass.IndirectOffsetOnAxis(ap=pos[r][:, k * TT + t:k * TT + t + 1], axis=0)).then_inc(fetched[r], 16)
                pool.wait_ge(carried, 2 * it + 2)

        @block.sync
        def _(sp):
            def load(s, j, n):
                row = sp.value_load(g["row_of"][0:1, j:j + 1] if isinstance(j, int) else g["row_of"][0:1, bass.ds(j, 1)], min_val=0, max_val=NEXP * CAP)
                if not (isinstance(n, int) and n == 0):
                    sp.wait_ge(x_turned[s % 2], (NX // 2) * (n - 1) + (s // 2 + 1) + FREE)
                sp.dma_start(xt[s][:], rows_of(g["xg"], row)).then_inc(x_in[s], 16)

            sp.wait_ge(z_ready, 1)
            for n in range(NEXP):
                tail = sp.value_load(g["tail"][0:1, n:n + 1], min_val=n * CAP, max_val=n * CAP + B * T)
                sp.dma_start(rows_of(g["xg"], tail), zrows[:]).then_inc(z_stored, 16)
            sp.dma_start(g["xg"][NEXP * CAP:NEXP * CAP + P, :], zrows[:]).then_inc(z_stored, 16)
            sp.dma_start(cho[:].rearrange("p b a k -> p b (a k)"), g["chod"].rearrange("b p n -> p b n")).then_inc(cho_in, 16)
            sp.wait_ge(z_stored, 16 * (NEXP + 1))
            for s in range(NX):
                load(s, s, 0)
            with sp.Fori(0, ROUNDS) as it:
                for s in range(NX):
                    load(s, NX * it + (s + NX), it + 1)
                    sp.wait_ge(y_ready[s % 2], (NX // 2) * it + (s // 2 + 1) + FREE)
                    sp.dma_start(rows_of(g["yg"], it * (NX * P) + s * P), ys[s][:]).then_inc(y_stored[s], 16)
            for s in range(NX):
                sp.wait_ge(y_stored[s], 16 * ROUNDS + FREE)
            sp.sem_inc(rows_written, 1)
            with sp.Fori(0, B) as it:
                for r in range(2):
                    sp.wait_ge(out_ready[r], it + FREE)
                    sp.dma_start(x1[r][:].rearrange("p t e -> p (t e)"), g["x1d"][bass.ds(2 * it + r, 1)].rearrange("a p n -> (a p) n")).then_inc(in_[r], 16)
                    sp.dma_start(modb[r][:], g["modd"][bass.ds(it, 1), 5 * E:6 * E].broadcast_to((P, E))).then_inc(in_[r], 16)

        @block.tensor
        def _(pe):
            def expert(j):
                return pe.value_load(g["expert_of"][0:1, bass.ds(j, 1)], min_val=0, max_val=NEXP - 1)

            def turn_x(s, rounds):
                q = s % 2
                pe.wait_ge(x_in[s], 16 * rounds + 16)
                if not (isinstance(rounds, int) and rounds == 0 and s < 2):
                    pe.wait_ge(xT_ready[q], (NX // 2) * rounds + s // 2 + FREE)
                for ce in range(CE):
                    last = pe.transpose(xps[q][:, ce * P:(ce + 1) * P], xt[s][:, ce * P:(ce + 1) * P], g["ident"][:])
                last.then_inc(x_turned[q], 1)

            def hidden(s, rounds):
                q, n = s % 2, (NX // 2) * rounds + s // 2
                pe.wait_ge(w1_ready[q], n + 1)
                pe.wait_ge(xT_ready[q], n + 1 + FREE)
                pe.wait_ge(relu_done[q], n + FREE)
                for m in range(CH):
                    for ce in range(CE):
                        last = pe.matmul(hps[q][:, m * P:(m + 1) * P], w1t[q][:, ce, m * P:(m + 1) * P],
                                         xT[q][:, ce, :], start=(ce == 0), stop=(ce == CE - 1))
                last.then_inc(hid_ps[q], 1)

            def outputs(s, rounds, e):
                q, n = s % 2, (NX // 2) * rounds + s // 2
                pe.wait_ge(hT_ready[q], n + 1 + FREE)
                pe.wait_ge(y_ready[q], n + FREE)
                for m in range(CH):
                    last = pe.matmul(yps[q][:, 0:E], hT[q][:, m, :], g["w2s"][:, bass.ds(e, 1), m, :].rearrange("p a e -> p (a e)"), start=(m == 0), stop=(m == CH - 1))
                last.then_inc(y_ps[q], 1)

            pe.wait_ge(g["w_loaded"], 32 * NEXP)
            turn_x(0, 0)
            hidden(0, 0)
            turn_x(1, 0)
            with pe.Fori(0, ROUNDS) as it:
                es = [expert(NX * it + s) for s in range(NX)]
                for s in range(NX):
                    hidden((s + 1) % NX, it + (s + 1) // NX)
                    turn_x((s + 2) % NX, it + (s + 2) // NX)
                    outputs(s, it, es[s])

        @block.scalar
        def _(act):
            def keep_x(s, rounds):
                q, n = s % 2, (NX // 2) * rounds + s // 2
                act.wait_ge(x_turned[q], n + 1 + FREE)
                act.wait_ge(hid_ps[q], n + FREE)
                act.activation(xT[q][:].rearrange("p c t -> p (c t)"), xps[q][:, 0:E], ACT.Copy).then_inc(xT_ready[q], 1)

            def weights(s, rounds, e):
                q, n = s % 2, (NX // 2) * rounds + s // 2
                act.wait_ge(hid_ps[q], n + FREE)
                act.activation(w1t[q][:].rearrange("p c h -> p (c h)"), g["w1s"][:, bass.ds(e, 1)].rearrange("p a c h -> p (a c h)"), ACT.Copy).then_inc(w1_ready[q], 1)

            def expert(j):
                at = g["expert_of"][0:1, j:j + 1] if isinstance(j, int) else g["expert_of"][0:1, bass.ds(j, 1)]
                return act.value_load(at, min_val=0, max_val=NEXP - 1)

            act.wait_ge(g["w_loaded"], 32 * NEXP)
            weights(0, 0, expert(0))
            weights(1, 0, expert(1))
            keep_x(0, 0)
            keep_x(1, 0)
            act.wait_ge(diff_ready, 1)
            act.activation(ediff[:], ediff[:], ACT.Exp).then_inc(exp_ready, 1)
            with act.Fori(0, ROUNDS) as it:
                es = [expert(NX * it + (s + 2)) for s in range(NX)]
                for s in range(NX):
                    q, n = s % 2, (NX // 2) * it + s // 2
                    act.wait_ge(relu_done[q], n + 1 + FREE)
                    act.wait_ge(y_ps[q], n + FREE)
                    act.activation(hT[q][:].rearrange("p c t -> p (c t)"), rl[q][:].rearrange("p c t -> p (c t)"), ACT.Square).then_inc(hT_ready[q], 1)
                    keep_x((s + 2) % NX, it + (s + 2) // NX)
                    weights((s + 2) % NX, it + (s + 2) // NX, es[s])
            with act.Fori(0, B) as it:
                for r in range(2):
                    act.wait_ge(out_ready[r], it + 1 + FREE)
                    act.dma_start(ov[bass.ds(it, 1), r].rearrange("a p t e -> (a p) t e"), og[r][:]).then_inc(stored[r], 16)
            for r in range(2):
                act.wait_ge(stored[r], 16 * B + FREE)

        @block.vector
        def _(dve):
            def relu(s, rounds):
                q, n = s % 2, (NX // 2) * rounds + s // 2
                dve.wait_ge(hid_ps[q], n + 1 + FREE)
                dve.wait_ge(hT_ready[q], n + FREE)
                dve.tensor_scalar(rl[q][:].rearrange("p c t -> p (c t)"), hps[q][:], 0.0, None, ALU.max).then_inc(relu_done[q], 1)

            relu(0, 0)
            d = Steps(dve, d_step)
            dve.wait_ge(cho_in, 16)
            lgt = cho[:, :, 2, :].rearrange("p b (k t) -> p b k t", k=2)
            dve.tensor_tensor(ediff[:], lgt[:, :, 1, :], lgt[:, :, 0, :], ALU.subtract).then_inc(diff_ready, 1)
            row = lambda v: v[:].rearrange("p (o n) -> p o n", o=1).broadcast_to((P, 2 * TT, NEXP))
            for b in range(2 * B):
                d.done(dve.tensor_tensor(hot[:], row(g["iota"]), cho[:, b, 1, :].rearrange("p (m o) -> p m o", o=1).broadcast_to((P, 2 * TT, NEXP)), ALU.is_equal))
                d.done(dve.tensor_tensor(hot[:], hot[:], row(g["close_up"]), ALU.mult))
                d.done(dve.reduce_sum(shift[:, b, :], hot[:], axis=AX.X))
            d.done(dve.tensor_tensor(posall[:], cho[:, :, 0, :], shift[:], ALU.add))
            dve.wait_ge(exp_ready, 1)
            d.done(dve.tensor_scalar(shift[:, :, 0:TT], ediff[:], 1.0, None, ALU.add))
            d.done(dve.reciprocal(wt[:, :, 0, :], shift[:, :, 0:TT]))
            d.done(dve.tensor_tensor(wt[:, :, 1, :], ediff[:], wt[:, :, 0, :], ALU.mult))
            with dve.Fori(0, ROUNDS) as it:
                for s in range(NX):
                    q, n = s % 2, (NX // 2) * it + s // 2
                    relu((s + 1) % NX, it + (s + 1) // NX)
                    dve.wait_ge(y_ps[q], n + 1 + FREE)
                    dve.wait_ge(y_stored[s], 16 * it + FREE)
                    dve.tensor_copy(ys[s][:], yps[q][:, 0:E]).then_inc(y_ready[q], 1)

            def pick(it, r):
                blk = (lambda v: v[:, it * 2 + r]) if isinstance(it, int) else (lambda v: v[:, bass.ds(2 * it + r, 1)])
                dve.tensor_copy(wcur[r][:].rearrange("p k t -> p (k t)"), blk(wt[:].rearrange("p b k t -> p b (k t)")))
                dve.tensor_copy(pos[r][:], blk(posall)).then_inc(picked, 1)

            for r in range(2):
                pick(0, r)

            def weigh(it, r, st):
                dve.wait_ge(picked, 2 * it + (r + 1))
                dve.wait_ge(in_[r], 32 * it + 32)
                dve.wait_ge(fetched[r], 16 * 2 * TT * (it + 1))
                for t in range(TT):
                    st.done(dve.tensor_scalar(z[:, t, :], yk[r][:, 0, t, :], wcur[r][:, 0, t:t + 1], None, ALU.mult))
                for t in range(TT):
                    st.done(dve.scalar_tensor_tensor(z[:, t, :], yk[r][:, 1, t, :], wcur[r][:, 1, t:t + 1], z[:, t, :], ALU.mult, ALU.add))
                st.done(dve.tensor_tensor(z[:], z[:], modb[r][:].rearrange("p (o e) -> p o e", o=1).broadcast_to((P, TT, E)), ALU.mult))
                dve.wait_ge(stored[r], 16 * it + FREE)
                dve.tensor_tensor(og[r][:], z[:], x1[r][:], ALU.add).then_inc(out_ready[r], 1)
                dve.wait_ge(out_ready[r], it + 1 + FREE)

            with dve.Fori(0, B - 1) as it:
                st = Steps(dve, v_step, V_STEPS * it)
                for r in range(2):
                    weigh(it, r, st)
                    pick(it + 1, r)
                assert st.n == V_STEPS, st.n
            st = Steps(dve, v_step, V_STEPS * (B - 1))
            for r in range(2):
                weigh(B - 1, r, st)


_INS = ['L0_attn_query', 'L0_attn_Wq', 'L0_attn_Wk', 'L0_attn_Wv', 'L0_attn_Wo', 'L0_attn_lambda_q1', 'L0_attn_lambda_k1',
        'L0_attn_lambda_q2', 'L0_attn_lambda_k2', 'L0_attn_subln_w', 'L0_ffn_router_w', 'L0_ffn_w1', 'L0_ffn_w2', 'L0_c', 'L0_wmod']


def kernel(**inputs):
    import numpy as _np
    import concourse.bacc as _bacc
    from concourse import mybir as _mybir
    from concourse.bass_utils import run_bass_kernel_spmd as _run

    nc = _bacc.Bacc("TRN2", target_bir_lowering=False, num_devices=1)
    arrays, args = {}, []
    for name in _INS:
        a = _np.ascontiguousarray(inputs[name])
        arrays[f"in_{name}"] = a
        args.append(nc.dram_tensor(f"in_{name}", a.shape, _mybir.dt.from_np(a.dtype), kind="ExternalInput").ap())
    args.append(nc.dram_tensor("out_x", (B, T, E), _mybir.dt.float32, kind="ExternalOutput").ap())
    build(nc, *args)
    r = _run(nc, [arrays], core_ids=[0])
    return r.results[0]["out_x"]
```

```python
from contextlib import ExitStack

import numpy as np
import concourse.bass as bass
from concourse import mybir

FP32 = mybir.dt.float32
BF16 = mybir.dt.bfloat16
U32 = mybir.dt.uint32
I32 = mybir.dt.int32
ALU = mybir.AluOpType
ACT = mybir.ActivationFunctionType
AX = mybir.AxisListType

P = 128
B, T, E = 4, 1024, 256
HEADS, HD = 16, 8
NEXP, HID = 8, 512
LAMBDA_INIT = float(0.8 - 0.6 * np.exp(-0.3 * 12))
EPS = 1e-5
ROOT_SCALE = 2.0 ** -5
RANGE = 2.0 ** 61
CE = E // P
CH = HID // P
BLK = 512
TT = BLK // P
ST = T // P
QUADS = B * HEADS // 2
QB = HEADS // 2
CAP = B * T + P
ROWS = NEXP * CAP + P
NTILE = 2 * B * T // P + NEXP
NX = 4
NTAB = NTILE + NX
VW = 32
Q_PART = (0, 0, 0, 1, 1, 2)
K_PART = (0, 1, 2, 0, 1, 0)
MROW = 64
ITEMS = 4 * ST
AHEAD = 8
NBUF = 4
LOAD_INC = 16 * (len(Q_PART) + len(K_PART) + 2)


class Steps:

    def __init__(self, eng, sem, base=0):
        self.eng, self.sem, self.base, self.n = eng, sem, base, 0

    def done(self, ins):
        self.n += 1
        ins.then_inc(self.sem, 1)
        self.eng.wait_ge(self.sem, self.base + self.n)


def build(nc, x, wq, wk, wv, wo, lq1, lk1, lq2, lk2, subln, router, w1, w2, cond, wmod, out):
    top = ExitStack()
    with top:
        def sb(ctx, name, shape, dt=FP32):
            return ctx.enter_context(nc.sbuf_tensor(name, shape, dt))

        def pb(ctx, name, shape, dt=FP32):
            return ctx.enter_context(nc.psum_tensor(name, shape, dt))

        def sem(ctx, name):
            return ctx.enter_context(nc.semaphore(name))

        qd = nc.dram_tensor("q_parts", (3, QUADS, 4, HD, T), BF16, kind="Internal").ap()
        kd = nc.dram_tensor("k_parts", (3, QUADS, 4, HD, T), BF16, kind="Internal").ap()
        vd = nc.dram_tensor("v_quads", (QUADS, P, ST, 2 * VW), FP32, kind="Internal").ap()
        od = nc.dram_tensor("o_quads", (QUADS, P, T), FP32, kind="Internal").ap()
        modd = nc.dram_tensor("mod_rows", (B, 6 * E), FP32, kind="Internal").ap()

        ident = sb(top, "ident", [P, P])
        wT = {n: sb(top, f"{n}_T", [P, CE, E]) for n in ("wq", "wk", "wv", "wo")}
        rT = sb(top, "router_T", [P, CE, NEXP])
        lam_sign = sb(top, "lam_sign", [P, 2])
        neg_half = sb(top, "neg_half", [P, TT])
        w_loaded = sem(top, "w_loaded")
        xg = nc.dram_tensor("x_rows", (ROWS, E), FP32, kind="Internal").ap()
        yg = nc.dram_tensor("y_rows", (NTILE * P, E), FP32, kind="Internal").ap()
        x1d = nc.dram_tensor("x1_blocks", (2 * B, P, TT * E), FP32, kind="Internal").ap()
        chod = nc.dram_tensor("choices", (2 * B, P, 3 * 2 * TT), FP32, kind="Internal").ap()
        count = sb(top, "count", [P, NEXP])
        tail = sb(top, "tail", [P, NEXP], I32)
        close_up = sb(top, "close_up", [P, NEXP])
        iota = sb(top, "iota", [P, NEXP])
        first_row = sb(top, "first_row", [P, NEXP])
        row_of = sb(top, "row_of", [P, NTAB], I32)
        expert_of = sb(top, "expert_of", [P, NTAB], I32)
        w1s = sb(top, "w1s", [P, NEXP, CE, HID])
        with ExitStack() as stacks:
            qs = [sb(stacks, f"a_q{r}", [P, 4, T], BF16) for r in range(NBUF)]
            ks = [sb(stacks, f"a_k{r}", [P, 4, T], BF16) for r in range(NBUF)]
            vs = [sb(stacks, f"a_v{r}", [P, ST, 2 * VW]) for r in range(NBUF)]
            zrow = sb(stacks, "a_zrow", [3, T], BF16)
            loaded = [sem(stacks, f"a_loaded{r}") for r in range(NBUF)]
            xs = [sb(stacks, f"p_x{r}", [P, TT, E]) for r in range(2)]
            x_in = [sem(stacks, f"p_x_in{r}") for r in range(2)]
            xv = x.rearrange("b (u t p) e -> b u p t e", u=2, p=P)
            setup(nc, top, sb, pb, sem, locals())
            project(nc, sb, pb, sem, locals())
            attend(nc, sb, pb, sem, locals())
        w2s = sb(top, "w2s", [P, NEXP, CH, E])
        tails, first_rows = [], []
        route(nc, sb, pb, sem, locals())
        experts(nc, sb, pb, sem, locals())


def load_quad(sp, g, r, p):
    one = isinstance(p, int)
    v = g["vd"][p] if one else g["vd"][p].rearrange("a p s c -> (a p) s c")
    for stack, parts, order in ((g["qs"][r], g["qd"], Q_PART), (g["ks"][r], g["kd"], K_PART)):
        for n, part in enumerate(order):
            rows = parts[part, p].rearrange("f d t -> d f t") if one else parts[part, p].rearrange("a f d t -> d (a f) t")
            sp.dma_start(stack[n * HD:(n + 1) * HD], rows).then_inc(g["loaded"][r], 16)
    sp.dma_start(g["qs"][r][MROW:MROW + 3], g["zrow"][:].rearrange("p (a t) -> p a t", a=1).broadcast_to((3, 4, T))).then_inc(g["loaded"][r], 16)
    sp.dma_start(g["vs"][r][:], v).then_inc(g["loaded"][r], 16)


def setup(nc, top, sb, pb, sem, g):
    with ExitStack() as c:
        wnat = {n: sb(c, f"{n}_nat", [P, CE, E]) for n in ("wq", "wk", "wv", "wo")}
        cT = sb(c, "cT", [P, CE, B])
        cexp = sb(c, "cexp", [P, CE, B])
        cden = sb(c, "cden", [P, CE, B])
        crec = sb(c, "crec", [P, CE, B])
        sT = sb(c, "sT", [P, CE, B])
        wm = sb(c, "wm", [P, CE, 6 * E])
        lv = sb(c, "lv", [P, 4, HD])
        lp = sb(c, "lp", [P, 2, HD])
        ls = sb(c, "ls", [P, 2])
        le = sb(c, "le", [P, 2])
        ld = sb(c, "ld", [P, 1])
        subn = sb(c, "subn", [P, 1])
        subw = sb(c, "subw", [P, 1])
        mod = sb(c, "mod", [B, 6 * E])
        gsign = sb(c, "gsign", [B, 2, E])
        gabs = sb(c, "gabs", [B, 2, E])
        wps = [pb(c, f"wps{i}", [P, CE, E]) for i in range(4)]
        mps = [pb(c, f"mps{i}", [P, 512]) for i in range(3)]
        w_in, c_in, s_id0, s_id = sem(c, "w_in"), sem(c, "c_in"), sem(c, "ident_zero"), sem(c, "ident_ready")
        mod_in, lam_in, small_in = sem(c, "mod_in"), sem(c, "lam_in"), sem(c, "small_in")
        w_turned, e_ready, s_ready = sem(c, "w_turned"), sem(c, "e_ready"), sem(c, "s_ready")
        l_sum, l_exp, mod_ps, mod_ready, mod_out = (sem(c, n) for n in ("l_sum", "l_exp", "mod_ps", "mod_ready", "mod_out"))
        v_step, cleared = sem(c, "setup_v_step"), sem(c, "stacks_cleared")
        block = c.enter_context(nc.Block())
        names = ("wq", "wk", "wv", "wo")

        @block.sync
        def _(sp):
            for ce in range(CE):
                sp.dma_start(cT[:, ce, :], g["cond"][:, ce * P:(ce + 1) * P].rearrange("b p -> p b"), allow_slow_non_contiguous=True).then_inc(c_in, 16)
            for n in names:
                sp.dma_start(wnat[n][:], g[n].rearrange("(c p) e -> p c e", p=P)).then_inc(w_in, 16)
            sp.dma_start(g["xs"][0][:], g["xv"][0, 0]).then_inc(g["x_in"][0], 16)
            sp.dma_start(wm[:], g["wmod"].rearrange("(c p) n -> p c n", p=P)).then_inc(mod_in, 16)
            for i, v in enumerate(("lq1", "lk1", "lq2", "lk2")):
                sp.dma_start(lv[:, i, :], g[v].rearrange("(a n) -> a n", a=1).broadcast_to((P, HD))).then_inc(lam_in, 16)
            for h in range(P // 16):
                sp.dma_start(subn[h * 16:(h + 1) * 16, :], g["subln"].rearrange("(n a) -> n a", a=1)).then_inc(lam_in, 16)
            for ce in range(CE):
                sp.dma_start(g["rT"][:, ce, :], g["router"][:, ce * P:(ce + 1) * P].rearrange("n p -> p n"), allow_slow_non_contiguous=True).then_inc(small_in, 16)
            sp.dma_start(g["xs"][1][:], g["xv"][0, 1]).then_inc(g["x_in"][1], 16)
            sp.wait_ge(mod_ready, 1)
            sp.dma_start(g["modd"], mod[:]).then_inc(mod_out, 16)
            sp.wait_ge(mod_out, 16)
            sp.wait_ge(small_in, 16 * CE)

        @block.gpsimd
        def _(pool):
            pool.memset(g["ident"][:], 0.0).then_inc(s_id0, 1)
            pool.memset(g["neg_half"][:], -0.5)
            pool.wait_ge(s_id0, 1)
            pool.affine_select(out=g["ident"][:], in_=g["ident"][:], compare_op=ALU.not_equal, fill=1.0,
                               base=0, pattern=[[-1, P]], channel_multiplier=1).then_inc(s_id, 1)
            pool.memset(g["zrow"][:], 0.0)
            for r in range(NBUF):
                for stack in (g["qs"][r], g["ks"][r]):
                    pool.memset(stack[:].rearrange("p f t -> p (f t)").bitcast(U32), 0).then_inc(cleared, 1)
            pool.wait_ge(cleared, 2 * NBUF)
            for r in range(NBUF):
                pool.memset(g["ks"][r][MROW:MROW + 3], 1.0)

        @block.tensor
        def _(pe):
            pe.wait_ge(s_id, 1)
            pe.wait_ge(w_in, 64)
            for i, n in enumerate(names):
                for ce in range(CE):
                    for cf in range(CE):
                        last = pe.transpose(wps[i][:, ce, cf * P:(cf + 1) * P], wnat[n][:, cf, ce * P:(ce + 1) * P], g["ident"][:])
                last.then_inc(w_turned, 1)
            pe.wait_ge(s_ready, 1)
            pe.wait_ge(mod_in, 16)
            for k in range(3):
                for ce in range(CE):
                    last = pe.matmul(mps[k][0:B, :], sT[:, ce, :], wm[:, ce, k * 512:(k + 1) * 512], start=(ce == 0), stop=(ce == CE - 1))
            last.then_inc(mod_ps, 1)

        @block.scalar
        def _(act):
            act.wait_ge(c_in, 16 * CE)
            act.activation(cexp[:], cT[:], ACT.Exp, scale=-1.0).then_inc(e_ready, 1)
            act.wait_ge(l_sum, 1)
            act.activation(le[:], ls[:], ACT.Exp).then_inc(l_exp, 1)

        @block.vector
        def _(dve):
            st = Steps(dve, v_step)
            dve.wait_ge(e_ready, 1)
            st.done(dve.tensor_scalar(cden[:], cexp[:], 1.0, None, ALU.add))
            st.done(dve.reciprocal(crec[:], cden[:]))
            dve.wait_ge(c_in, 16 * CE)
            dve.tensor_tensor(sT[:], cT[:], crec[:], ALU.mult).then_inc(s_ready, 1)
            dve.wait_ge(lam_in, 16 * (4 + P // 16))
            for i in range(2):
                st.done(dve.tensor_tensor(lp[:, i, :], lv[:, 2 * i, :], lv[:, 2 * i + 1, :], ALU.mult))
            dve.reduce_sum(ls[:], lp[:], axis=AX.X).then_inc(l_sum, 1)
            st.done(dve.tensor_scalar(subw[:], subn[:], 1.0 - LAMBDA_INIT, ROOT_SCALE, ALU.mult, ALU.mult))
            dve.memset(g["lam_sign"][:, 0:1], 1.0)
            dve.wait_ge(l_exp, 1)
            st.done(dve.tensor_tensor(ld[:], le[:, 1:2], le[:, 0:1], ALU.subtract))
            dve.tensor_scalar(g["lam_sign"][:, 1:2], ld[:], -LAMBDA_INIT, None, ALU.add)
            for i, n in enumerate(names):
                dve.wait_ge(w_turned, i + 1)
                if n == "wo":
                    dve.tensor_scalar(g["wT"][n][:], wps[i][:], subw[:, 0:1], None, ALU.mult)
                else:
                    dve.tensor_copy(g["wT"][n][:], wps[i][:])
            dve.wait_ge(mod_ps, 1)
            for k in range(3):
                st.done(dve.tensor_copy(mod[:, k * 512:(k + 1) * 512], mps[k][0:B, :]))
            m6 = mod[:].rearrange("b (a k e) -> b a k e", a=2, k=3)
            st.done(dve.tensor_scalar(m6[:, :, 1, :], m6[:, :, 1, :], 1.0, None, ALU.add))
            st.done(dve.tensor_scalar(gsign[:], m6[:, :, 2, :], 0.0, 2.0, ALU.is_ge, ALU.mult))
            st.done(dve.scalar_tensor_tensor(gabs[:], m6[:, :, 2, :], -1.0, m6[:, :, 2, :], ALU.mult, ALU.max))
            st.done(dve.tensor_scalar(gabs[:], gabs[:], 0.25, None, ALU.max))
            st.done(dve.tensor_scalar(gsign[:], gsign[:], -1.0, None, ALU.add))
            dve.tensor_tensor(m6[:, :, 2, :], gsign[:], gabs[:], ALU.mult).then_inc(mod_ready, 1)


def project(nc, sb, pb, sem, g):
    with ExitStack() as c:
        def two(name, shape, dt=FP32):
            return [sb(c, f"{name}{r}", shape, dt) for r in range(2)]

        xs, x_in, xv = g["xs"], g["x_in"], g["xv"]
        modb = sb(c, "p_modb", [P, 2, E])
        stats = sb(c, "p_stats", [P, TT, 6])
        mv = sb(c, "p_mv", [P, TT, 2])
        vare = sb(c, "p_vare", [P, TT])
        rstd = sb(c, "p_rstd", [P, TT])
        carry = sb(c, "p_carry", [P, 1])
        xn = sb(c, "p_xn", [P, TT, E])
        h = two("p_h", [P, TT, E])
        hT = two("p_hT", [P, CE, BLK])
        qf = sb(c, "p_qf", [P, 4, BLK])
        res = two("p_res", [P, BLK])
        parts = two("p_parts", [P, 4, 3, BLK], BF16)
        vaug = two("p_vaug", [P, QB, TT, 2 * VW])
        hps = pb(c, "p_hps", [P, CE, BLK])
        fps = [pb(c, f"p_fps{i}", [P, BLK]) for i in range(4)]
        vps = pb(c, "p_vps", [P, TT, E])
        stored = [sem(c, f"p_stored{r}") for r in range(2)]
        modb_in, var_ready, rstd_ready, h_ready = (sem(c, f"p_{n}") for n in ("modb_in", "var_ready", "rstd_ready", "h_ready"))
        v_init, hps_ready, hT_ready, f_ready, v_ready = (sem(c, f"p_{n}") for n in ("v_init", "hps_ready", "hT_ready", "f_ready", "v_ready"))
        two_split = sem(c, "p_two_split")
        q1_ready, split_done, v_kept, v_step, g_step = (sem(c, f"p_{n}") for n in ("q1_ready", "split_done", "v_kept", "v_step", "g_step"))
        block = c.enter_context(nc.Block())
        NORM_STEPS, SPLIT_STEPS = 2 + TT + 1, 4
        STORES = 16 * (4 + 1)
        FREE = 1

        def batches(eng, body):
            with eng.Fori(0, B - 1) as it:
                for r in range(2):
                    body(it, r, True)
            for r in range(2):
                body(B - 1, r, r == 0)

        def pick(t, i):
            return t[i] if isinstance(i, int) else t[bass.ds(i, 1)].rearrange("a p t e -> (a p) t e")

        @block.sync
        def _(sp):
            def rows(b):
                m = g["modd"][b:b + 1, 0:2 * E] if isinstance(b, int) else g["modd"][bass.ds(b, 1), 0:2 * E]
                sp.dma_start(modb[:].rearrange("p k e -> p (k e)"), m.broadcast_to((P, 2 * E))).then_inc(modb_in, 16)

            rows(0)

            def load_x(b, r):
                sp.dma_start(xs[r][:], pick(xv[:, r], b)).then_inc(x_in[r], 16)

            def body(it, r):
                last = isinstance(it, int) and it == B - 1
                cols = slice(r * BLK, (r + 1) * BLK)
                if last and r == 0:
                    for u in range(2):
                        sp.wait_ge(stored[u], STORES + FREE)
                    load_quad(sp, g, 0, 0)
                if not last:
                    sp.wait_ge(h_ready, 2 * it + (r + 2))
                    if r == 0:
                        load_x(it + 1, 1)
                        rows(it + 1)
                    elif not isinstance(it, int):
                        load_x(it + 2, 0)
                for i in range(4):
                    dst = (g["qd"] if i < 2 else g["kd"]).rearrange("g (b i q) f d t -> b i (q f d) g t", b=B, i=2)
                    to = dst[it, i % 2, :, :, cols] if isinstance(it, int) else dst[bass.ds(it, 1), i % 2, :, :, cols].rearrange("a p g t -> (a p) g t")
                    sp.wait_ge(split_done, 8 * it + (4 * r + i + 1) + FREE)
                    sp.dma_start(to, parts[r][:, i]).then_inc(stored[r], 16)
                sp.wait_ge(v_kept, 2 * it + (r + 1) + FREE)
                vv = g["vd"].rearrange("(b q) p (u t) c -> b u p q (t c)", b=B, u=2)
                to = vv[it, r] if isinstance(it, int) else vv[bass.ds(it, 1), r].rearrange("a p q c -> (a p) q c")
                sp.dma_start(to, vaug[r][:].rearrange("p q t c -> p q (t c)")).then_inc(stored[r], 16)

            sp.wait_ge(h_ready, 1)
            load_x(1, 0)
            with sp.Fori(0, B - 2) as it:
                for r in range(2):
                    body(it, r)
            for b in range(B - 2, B):
                for r in range(2):
                    body(b, r)
            for r in range(2):
                sp.wait_ge(stored[r], B * STORES + FREE)

        @block.gpsimd
        def _(pool):
            for s_ in (hps_ready, split_done, q1_ready, v_kept, v_ready, *stored):
                pool.sem_inc(s_, FREE)
            for r in range(2):
                pool.memset(vaug[r][:], 0.0).then_inc(g_step, 1)
            pool.wait_ge(g_step, 2)
            for r in range(2):
                pool.memset(vaug[r][:].rearrange("p q t (h c) -> p (q t h) c", h=2)[:, :, 16:17], 1.0).then_inc(v_init, 1)

            def root(n):
                pool.wait_ge(var_ready, n + 1)
                pool.tensor_tensor(rstd[:], vare[:], g["neg_half"][:], ALU.pow).then_inc(rstd_ready, 1)

            def body(it, r, ahead):
                if ahead:
                    root(2 * it + (r + 1))
                for i in range(4):
                    pool.wait_ge(two_split, 8 * it + (4 * r + i + 1))
                    pool.tensor_tensor(parts[r][:, i, 2, :], res[i % 2][:], parts[r][:, i, 1, :], ALU.subtract).then_inc(split_done, 1)

            root(0)
            batches(pool, body)

        @block.vector
        def _(dve):
            def norm(it, r, st):
                m = 2 * it + r
                dve.wait_ge(x_in[r], 16 * it + 16)
                for t in range(TT):
                    ins = dve.bn_stats(stats[:, t, :], xs[r][:, t, :])
                st.done(ins)
                dve.memset(carry[:], 0.0)
                for t in range(TT):
                    ins = dve.bn_aggr(mv[:, t, :], stats[:, t, :])
                st.done(ins)
                dve.tensor_scalar(vare[:], mv[:, :, 1], EPS, None, ALU.add).then_inc(var_ready, 1)
                dve.wait_ge(rstd_ready, m + 1)
                for t in range(TT):
                    st.done(dve.tensor_scalar(xn[:, t, :], xs[r][:, t, :], mv[:, t, 0:1], rstd[:, t:t + 1], ALU.subtract, ALU.mult))
                dve.wait_ge(modb_in, 16 * it + 16)
                st.done(dve.tensor_tensor(xn[:], xn[:], modb[:, 1:2, :].broadcast_to((P, TT, E)), ALU.mult))
                if not (isinstance(m, int) and m == 0):
                    dve.wait_ge(hps_ready, m - 1 + FREE)
                dve.tensor_tensor(h[r][:], xn[:], modb[:, 0:1, :].broadcast_to((P, TT, E)), ALU.add).then_inc(h_ready, 1)

            def body(it, r, ahead):
                st = Steps(dve, v_step, (NORM_STEPS + SPLIT_STEPS) * (2 * it + r) + NORM_STEPS)
                if ahead:
                    norm(it + r, 1 - r, st)
                    assert st.n == NORM_STEPS
                for i in range(4):
                    dve.wait_ge(q1_ready, 8 * it + (4 * r + i + 1) + FREE)
                    if not (isinstance(it, int) and it == 0 and r == 0):
                        dve.wait_ge(split_done, 8 * it + (4 * r + i - 1) + FREE)
                    st.done(dve.tensor_tensor(res[i % 2][:], qf[:, i, :], parts[r][:, i, 0, :], ALU.subtract))
                    dve.tensor_copy(parts[r][:, i, 1, :], res[i % 2][:]).then_inc(two_split, 1)

            norm(0, 0, Steps(dve, v_step))
            batches(dve, body)

        @block.tensor
        def _(pe):
            def turn(it, r):
                pe.wait_ge(h_ready, 2 * it + (r + 1))
                if not (isinstance(it, int) and it == 0 and r == 0):
                    pe.wait_ge(hT_ready, 2 * it + r)
                for ce in range(CE):
                    for t in range(TT):
                        last = pe.transpose(hps[:, ce, t * P:(t + 1) * P], h[r][:, t, ce * P:(ce + 1) * P], g["ident"][:])
                last.then_inc(hps_ready, 1)

            def body(it, r, ahead):
                pe.wait_ge(hT_ready, 2 * it + (r + 1))
                pe.wait_ge(q1_ready, 8 * it + 4 * r + FREE)
                for i in range(4):
                    w = g["wT"]["wq" if i < 2 else "wk"]
                    for ce in range(CE):
                        last = pe.matmul(fps[i][:], w[:, ce, (i % 2) * P:(i % 2 + 1) * P], hT[r][:, ce, :], start=(ce == 0), stop=(ce == CE - 1))
                    last.then_inc(f_ready, 1)
                if ahead:
                    turn(it + r, 1 - r)
                pe.wait_ge(v_kept, 2 * it + r + FREE)
                for t in range(TT):
                    for ce in range(CE):
                        last = pe.matmul(vps[:, t, :], hT[r][:, ce, t * P:(t + 1) * P], g["wT"]["wv"][:, ce, :], start=(ce == 0), stop=(ce == CE - 1))
                last.then_inc(v_ready, 1)

            turn(0, 0)
            batches(pe, body)

        @block.scalar
        def _(act):
            def keep(it, r):
                act.wait_ge(hps_ready, 2 * it + (r + 1) + FREE)
                if not (isinstance(it, int) and it == 0 and r == 0):
                    act.wait_ge(v_ready, 2 * it + r - 1 + FREE)
                act.activation(hT[r][:], hps[:], ACT.Copy).then_inc(hT_ready, 1)

            def body(it, r, ahead):
                act.wait_ge(stored[r], STORES * it + FREE)
                act.wait_ge(split_done, 8 * it + 4 * r + FREE)
                for i in range(4):
                    act.wait_ge(f_ready, 8 * it + (4 * r + i + 1))
                    scale = HD ** -0.5 if i < 2 else 1.0
                    act.activation(qf[:, i, :], fps[i][:], ACT.Copy, scale=scale)
                    act.activation(parts[r][:, i, 0, :], fps[i][:], ACT.Copy, scale=scale).then_inc(q1_ready, 1)
                if ahead:
                    keep(it + r, 1 - r)
                act.wait_ge(v_ready, 2 * it + (r + 1) + FREE)
                for t in range(TT):
                    last = act.activation(vaug[r][:, :, t, :].rearrange("p q (h c) -> p q h c", h=2)[:, :, :, 0:16],
                                          vps[:, t, :].rearrange("p (q h c) -> p q h c", q=QB, h=2), ACT.Copy)
                last.then_inc(v_kept, 1)

            act.wait_ge(v_init, 2)
            keep(0, 0)
            batches(act, body)


def attend(nc, sb, pb, sem, g):
    with ExitStack() as c:
        qs, ks, vs, loaded = g["qs"], g["ks"], g["vs"], g["loaded"]
        probs = [sb(c, f"a_p{r}", [P, 4, T]) for r in range(2)]
        negmax = [sb(c, f"a_negmax{r}", [P, 32]) for r in range(2)]
        mrow = sb(c, "a_mrow", [32, P])
        mres = sb(c, "a_mres", [32, P])
        mparts = sb(c, "a_mparts", [32, 3, P], BF16)
        oT = sb(c, "a_oT", [P, T])
        mps = [pb(c, f"a_mps{r}", [P, T]) for r in range(2)]
        eps = [pb(c, f"a_eps{r}", [P, BLK]) for r in range(2)]
        ops = [pb(c, f"a_ops{r}", [P, BLK]) for r in range(2)]
        mscore = [sem(c, f"a_mscore{r}") for r in range(2)]
        mtaken = [sem(c, f"a_mtaken{r}") for r in range(2)]
        mstep, msplit, mplaced = sem(c, "a_mstep"), sem(c, "a_msplit"), sem(c, "a_mplaced")
        escore = [sem(c, f"a_escore{r}") for r in range(2)]
        edone = [sem(c, f"a_edone{r}") for r in range(2)]
        pv = [[sem(c, f"a_pv{s}{r}") for r in range(2)] for s in range(2)]
        okept, ostored = sem(c, "a_okept"), sem(c, "a_ostored")
        block = c.enter_context(nc.Block())
        FREE = 1

        def at(p, a, k=0):
            it, r = p
            return it * (4 * a) + (r * a + k)

        def after(p, n=1):
            return p[0], p[1] + n

        def slot(p, idx):
            it, r = p
            k = ITEMS + AHEAD + 1 + (ITEMS + 1) * r + idx
            return k % 2, it * (2 * (ITEMS + 1)) + k // 2

        def steps_of(p, k):
            def exists(off):
                return not isinstance(p[0], int) or 4 * p[0] + p[1] + off < QUADS

            turns = k == ITEMS - AHEAD
            off = 1 if k < ITEMS - AHEAD else 2
            item = ((k + AHEAD) % ITEMS, off, slot(p, k + (k > ITEMS - AHEAD))) if exists(off) else None
            return item, slot(p, k + 1) if turns and exists(1) else None

        @block.sync
        def _(sp):
            def place(r, count):
                sp.wait_ge(msplit, count)
                for j in range(3):
                    sp.dma_start(qs[r][MROW + j:MROW + j + 1].rearrange("a f (t c) -> a (f t) c", c=P), mparts[:, j, :]).then_inc(mplaced, 16)

            def store(p, index):
                sp.wait_ge(okept, at(p, 2, 2) + FREE)
                sp.dma_start(g["od"][index].rearrange("a p t -> (a p) t") if not isinstance(index, int) else g["od"][index], oT[:]).then_inc(ostored, 16)

            for q in range(1, 3):
                load_quad(sp, g, q, q)
            for n in range(NEXP):
                sp.dma_start(g["w1s"][:, n], g["w1"][n].rearrange("(c p) h -> p c h", p=P)).then_inc(g["w_loaded"], 16)
            place(0, 1)
            load_quad(sp, g, 3, 3)

            def period(p, quad, places, loads):
                it, r = p
                if places:
                    place((r + 1) % NBUF, at(p, 1, 2))
                store(p, quad(0))
                if loads:
                    sp.wait_ge(pv[1][1], at(p, 4, 4) + FREE)
                    load_quad(sp, g, r, quad(4))

            with sp.Fori(0, QUADS // 4 - 1) as it:
                for r in range(4):
                    period((it, r), lambda n: bass.ds(it * 4 + (r + n), 1), True, True)
            for r in range(4):
                period((QUADS // 4 - 1, r), lambda n: QUADS - 4 + r + n, r < 3, False)
            sp.wait_ge(ostored, 16 * QUADS + FREE)

        @block.gpsimd
        def _(pool):
            for s_ in (okept, ostored, *pv[0], *pv[1]):
                pool.sem_inc(s_, FREE)

        @block.tensor
        def _(pe):
            def item(buf, uses, r, k, halves=(0, 1)):
                f, t = k // ST, k % ST
                if 0 in halves and not (isinstance(uses, int) and uses == 0):
                    pe.wait_ge(mtaken[buf], uses)
                for hlf in halves:
                    last = pe.matmul(mps[buf][:, hlf * BLK:(hlf + 1) * BLK], qs[r][:, f, t * P:(t + 1) * P],
                                     ks[r][:, f, hlf * BLK:(hlf + 1) * BLK], start=True, stop=True)
                if 1 in halves:
                    last.then_inc(mscore[buf], 1)

            def turn(buf, uses, par):
                pe.wait_ge(mtaken[buf], uses)
                pe.matmul(mps[buf][0:32, 0:P], negmax[par][:], g["ident"][:], start=True, stop=True).then_inc(mscore[buf], 1)

            def max_step(p, k, halves=(0, 1)):
                r = p[1]
                tile, turned = steps_of(p, k)
                if tile:
                    k, off, where = tile
                    if k == 0:
                        pe.wait_ge(loaded[(r + 2) % NBUF], p[0] * LOAD_INC + LOAD_INC * ((r + 2) // NBUF + 1))
                    item(*where, (r + off) % NBUF, k, halves)
                if turned:
                    turn(*turned, (r + 1) % 2)

            def score(p, i, f, hlf):
                r = p[1] % NBUF
                if i or f or not (isinstance(p[0], int) and p == (0, 0)):
                    pe.wait_ge(edone[hlf], at(p, 32, 4 * i + f))
                pe.matmul(eps[hlf][:], ks[r][:, f, i * P:(i + 1) * P], qs[r][:, f, hlf * BLK:(hlf + 1) * BLK],
                          start=True, stop=True).then_inc(escore[hlf], 1)

            def product(p, i, hlf):
                pe.wait_ge(edone[hlf], at(p, 32, 4 * i + 4))
                if i == 0:
                    pe.wait_ge(okept, at(p, 2) + FREE)
                for f in range(4):
                    last = pe.matmul(ops[hlf][32 * f:32 * f + VW, :], vs[p[1] % NBUF][:, i, (f // 2) * VW:(f // 2 + 1) * VW],
                                     probs[i % 2][:, f, hlf * BLK:(hlf + 1) * BLK], start=(i == 0), stop=(i == ST - 1))
                last.then_inc(pv[i % 2][hlf], 1)

            def key_tile(p, i, before):
                for f in range(0, 4, 2):
                    k = 4 * i + f
                    score(p, i, f, 0)
                    max_step(p, k)
                    max_step(p, k + 1, halves=(0,))
                    score(p, i, f, 1)
                    max_step(p, k + 1, halves=(1,))
                    score(p, i, f + 1, 0)
                    if before:
                        product(*before, f // 2)
                    score(p, i, f + 1, 1)

            def head(p, before=None):
                pe.wait_ge(mplaced, at(p, 48, 48))
                key_tile(p, 0, before and (before, ST - 1))

            def tail(p):
                for i in range(1, ST):
                    key_tile(p, i, (p, i - 1))

            pe.wait_ge(loaded[0], LOAD_INC)
            for k in range(ITEMS):
                item(k % 2, k // 2, 0, k)
            for k in range(ITEMS - AHEAD, ITEMS):
                max_step((0, -1), k)
            head((0, 0))
            with pe.Fori(0, QUADS // 4 - 1) as it:
                for r in range(4):
                    tail((it, r))
                    head((it, r + 1), before=(it, r))
            for r in range(4):
                p = (QUADS // 4 - 1, r)
                tail(p)
                if r < 3:
                    head(after(p), before=p)
            for hlf in range(2):
                product(p, ST - 1, hlf)

        @block.vector
        def _(dve):
            def item(buf, uses, par, k):
                dve.wait_ge(mscore[buf], uses + 1)
                dve.tensor_reduce(negmax[par][:, k:k + 1], mps[buf][:], AX.X, ALU.max, negate=True).then_inc(mtaken[buf], 1)

            def turn(buf, uses, p):
                dve.wait_ge(mscore[buf], uses + 1)
                dve.tensor_copy(mrow[:], mps[buf][0:32, 0:P]).then_inc(mtaken[buf], 1)
                dve.wait_ge(mtaken[buf], uses + 1)
                if p[1] != -1:
                    dve.wait_ge(mplaced, at(p, 48, 48))
                dve.tensor_copy(mparts[:, 0, :], mrow[:]).then_inc(mstep, 1)
                dve.wait_ge(mstep, at(p, 3, 4))
                dve.tensor_tensor(mres[:], mrow[:], mparts[:, 0, :], ALU.subtract).then_inc(mstep, 1)
                dve.wait_ge(mstep, at(p, 3, 5))
                dve.tensor_copy(mparts[:, 1, :], mres[:]).then_inc(mstep, 1)
                dve.wait_ge(mstep, at(p, 3, 6))
                dve.tensor_tensor(mparts[:, 2, :], mres[:], mparts[:, 1, :], ALU.subtract).then_inc(msplit, 1)

            def steps(p, ks_):
                for k in ks_:
                    tile, turned = steps_of(p, k)
                    if tile:
                        k, off, where = tile
                        item(*where, (p[1] + off) % 2, k)
                    if turned:
                        turn(*turned, p)

            for k in range(ITEMS):
                item(k % 2, k // 2, 0, k)
            steps((0, -1), range(ITEMS - AHEAD, ITEMS))
            steps((0, 0), range(4))
            with dve.Fori(0, QUADS // 4 - 1) as it:
                for r in range(4):
                    steps((it, r), range(4, ITEMS))
                    steps((it, r + 1), range(4))
            for r in range(4):
                p = (QUADS // 4 - 1, r)
                steps(p, range(4, ITEMS))
                if r < 3:
                    steps(after(p), range(4))

        @block.scalar
        def _(act):
            def exps(p, i):
                for f in range(4):
                    for hlf in range(2):
                        act.wait_ge(escore[hlf], at(p, 32, 4 * i + f + 1))
                        if f == 0:
                            act.wait_ge(pv[i % 2][hlf], at(p, 4, i // 2) + FREE)
                        act.activation(probs[i % 2][:, f, hlf * BLK:(hlf + 1) * BLK], eps[hlf][:], ACT.Exp).then_inc(edone[hlf], 1)

            def keep(p):
                act.wait_ge(ostored, at(p, 16) + FREE)
                for hlf in range(2):
                    act.wait_ge(pv[1][hlf], at(p, 4, 4) + FREE)
                    act.activation(oT[:, hlf * BLK:(hlf + 1) * BLK], ops[hlf][:], ACT.Copy).then_inc(okept, 1)

            exps((0, 0), 0)
            with act.Fori(0, QUADS // 4 - 1) as it:
                for r in range(4):
                    for i in range(1, ST):
                        exps((it, r), i)
                    exps((it, r + 1), 0)
                    keep((it, r))
            for r in range(4):
                p = (QUADS // 4 - 1, r)
                for i in range(1, ST):
                    exps(p, i)
                if r < 3:
                    exps(after(p), 0)
                keep(p)


def route(nc, sb, pb, sem, g):
    with ExitStack() as c:
        def two(name, shape, dt=FP32):
            return [sb(c, f"{name}{r}", shape, dt) for r in range(2)]

        os_ = two("m_o", [P, QB, BLK])
        xs = two("m_x", [P, TT, E])
        modb = sb(c, "m_modb", [P, 3, E])
        wog = sb(c, "m_wog", [P, CE, E])
        rec = sb(c, "m_rec", [P, 32])
        rl = sb(c, "m_rl", [P, 32])
        A = sb(c, "m_A", [P, 32, 16])
        D = two("m_D", [P, TT * HEADS, 16])
        tmp = two("m_tmp", [P, TT, E])
        ss = two("m_ss", [P, TT * HEADS])
        sse = two("m_sse", [P, TT * HEADS])
        root = two("m_root", [P, TT * HEADS])
        rs = two("m_rs", [P, TT * HEADS])
        nt = sb(c, "m_newton", [P, TT * HEADS])
        an = two("m_an", [P, TT, E])
        aT = two("m_aT", [P, CE, BLK])
        x1 = two("m_x1", [P, TT, E])
        stats = sb(c, "m_stats", [P, TT, 6])
        mv = two("m_mv", [P, TT, 2])
        vare = two("m_vare", [P, TT])
        rstd = two("m_rstd", [P, TT])
        shift = two("m_shift", [P, TT])
        carry = sb(c, "m_carry", [P, 1])
        pcarry = sb(c, "m_pcarry", [P, 2])
        h2 = two("m_h2", [P, TT, E])
        hT = two("m_hT", [P, CE, BLK])
        lg = sb(c, "m_lg", [P, TT, NEXP])
        top8 = sb(c, "m_top8", [P, TT, 8])
        idx8 = sb(c, "m_idx8", [P, TT, 8], U32)
        cho = two("m_cho", [P, 3, 2, TT])
        hot = two("m_hot", [P, 2, TT, NEXP])
        both = two("m_both", [P, TT, NEXP])
        msum = sb(c, "m_msum", [P, NEXP])
        seen = two("m_seen", [P, NEXP])
        slotr = sb(c, "m_slotr", [P, TT, NEXP])
        prod = sb(c, "m_prod", [P, 2, TT, NEXP])
        pos = two("m_pos", [P, 2 * TT], U32)
        tri = sb(c, "m_tri", [P, P])
        ones = sb(c, "m_ones", [P, P])
        iotai = sb(c, "m_iotai", [P, NTAB], I32)
        big = [pb(c, f"m_big{i}", [P, 1024]) for i in range(2)]
        gen = [pb(c, f"m_gen{i}", [P, 1024]) for i in range(2)]
        names = ("modb_in", "turned", "cl_ready", "sq_ready", "sse_ready", "root_ready", "aT_ready", "wog_ready",
                 "var_ready", "rstd_ready", "h2_ready", "hT_ready", "iota_ready", "tri_ready", "x_added", "both_ready",
                 "rank_ps", "rank_taken", "pos_ready", "an_ready", "aT_ps", "wo_ps", "hT_ps", "lg_ps", "v_step", "g_step",
                 "count_ps", "h2_free", "carried", "tables_step", "tables_ready", "shift_ready", "xn_ready")
        S = {n: sem(c, f"m_{n}") for n in names}
        turn_taken = [sem(c, f"m_turn_taken{i}") for i in range(2)]
        o_in = [sem(c, f"m_o_in{i}") for i in range(2)]
        x_in = [sem(c, f"m_x_in{i}") for i in range(2)]
        x1_kept = [sem(c, f"m_x1_kept{i}") for i in range(2)]
        cho_kept = [sem(c, f"m_cho_kept{i}") for i in range(2)]
        sent = [sem(c, f"m_sent{i}") for i in range(2)]
        block = c.enter_context(nc.Block())
        FREE = 1
        JOIN_STEPS = 3 * TT * 2
        V_STEPS = JOIN_STEPS + 2 * (1 + 1 + 6 + 2 + 1 + 8 + 3)
        xv = g["x"].rearrange("b (u t p) e -> b u p t e", u=2, p=P)
        odv = g["od"].rearrange("(b q) p t -> b p q t", b=B)
        SENT = 16 * 2 * TT
        flat = lambda v: v[:].rearrange("p t e -> p (t e)")

        @block.sync
        def _(sp):
            def load_o(b, r):
                o = odv[:, :, :, r * BLK:(r + 1) * BLK]
                sp.dma_start(os_[r][:], o[b] if isinstance(b, int) else o[bass.ds(b, 1)].rearrange("a p q t -> (a p) q t")).then_inc(o_in[r], 16)

            def load_x(b):
                for r in range(2):
                    sp.dma_start(xs[r][:], xv[b, r] if isinstance(b, int) else xv[bass.ds(b, 1), r].rearrange("a p t e -> (a p) t e")).then_inc(x_in[r], 16)

            def rows(b):
                m = g["modd"][b:b + 1, 2 * E:5 * E] if isinstance(b, int) else g["modd"][bass.ds(b, 1), 2 * E:5 * E]
                sp.dma_start(modb[:].rearrange("p k e -> p (k e)"), m.broadcast_to((P, 3 * E))).then_inc(S["modb_in"], 16)

            def store(it, r, ready, src, dst, done):
                sp.wait_ge(ready, 2 * it + (r + 1))
                to = dst[it * 2 + r] if isinstance(it, int) else dst[bass.ds(2 * it + r, 1)].rearrange("a p n -> (a p) n")
                sp.dma_start(to, src).then_inc(done[r], 16)

            def body(it, more, more_o):
                if more:
                    sp.wait_ge(S["x_added"], 2 * it + 2)
                    load_x(it + 1)
                for r in range(2):
                    store(it, r, S["h2_ready"], flat(x1[r]), g["x1d"], x1_kept)
                if more:
                    rows(it + 1)
                for r in range(2):
                    if more_o:
                        sp.wait_ge(S["turned"], TT * (2 * it) + TT * (3 + r))
                        load_o(it + 2, r)
                    store(it, r, S["pos_ready"], cho[r][:].rearrange("p a k t -> p (a k t)"), g["chod"], cho_kept)

            rows(0)
            for r in range(2):
                load_o(0, r)
            load_x(0)
            for r in range(2):
                sp.wait_ge(S["turned"], TT * (1 + r))
                load_o(1, r)
            for n in range(NEXP):
                sp.dma_start(g["w2s"][:, n], g["w2"][n].rearrange("(c p) e -> p c e", p=P)).then_inc(g["w_loaded"], 16)
            with sp.Fori(0, B - 2) as it:
                body(it, True, True)
            body(B - 2, True, False)
            body(B - 1, False, False)
            sp.wait_ge(S["tables_ready"], 1)
            for n in range(NEXP):
                g["tails"].append(sp.value_load(g["tail"][0:1, n:n + 1], min_val=n * CAP, max_val=n * CAP + B * T))
            for j in range(NX):
                g["first_rows"].append(sp.value_load(g["row_of"][0:1, j:j + 1], min_val=0, max_val=NEXP * CAP))
            for r in range(2):
                sp.wait_ge(x1_kept[r], 16 * B + FREE)
                sp.wait_ge(cho_kept[r], 16 * B + FREE)

        @block.gpsimd
        def _(pool):
            for s_ in (*x1_kept, *cho_kept, *turn_taken, S["h2_free"], S["rank_taken"], S["rank_ps"], S["wo_ps"]):
                pool.sem_inc(s_, FREE)
            pool.iota(iotai[:], [[1, NTAB]], base=0, channel_multiplier=0).then_inc(S["g_step"], 1)
            pool.memset(ones[:], 1.0).then_inc(S["g_step"], 1)
            pool.wait_ge(S["g_step"], 2)
            pool.tensor_copy(g["iota"][:], iotai[:, 0:NEXP]).then_inc(S["iota_ready"], 1)
            pool.affine_select(out=tri[:], in_=ones[:], compare_op=ALU.is_gt, fill=0.0, base=0, pattern=[[1, P]], channel_multiplier=-1).then_inc(S["tri_ready"], 1)
            with pool.Fori(0, B) as it:
                for r in range(2):
                    pool.wait_ge(S["var_ready"], 2 * it + r + 1)
                    pool.tensor_tensor(rstd[r][:], vare[r][:], g["neg_half"][:], ALU.pow).then_inc(S["rstd_ready"], 1)
                for r in range(2):
                    pool.wait_ge(S["pos_ready"], 2 * it + r + 1)
                    pool.tensor_tensor(pcarry[:, r:r + 1], g["neg_half"][:, 0:1], g["neg_half"][:, 0:1], ALU.mult).then_inc(S["carried"], 1)
                    for k in range(2):
                        for t in range(TT):
                            pool.indirect_dma_start(out=g["xg"], out_offset=bass.IndirectOffsetOnAxis(ap=pos[r][:, k * TT + t:k * TT + t + 1], axis=0),
                                                    in_=h2[r][:, t, :], in_offset=None).then_inc(sent[r], 16)
                for r in range(2):
                    pool.wait_ge(sent[r], SENT * (it + 1))
                pool.wait_ge(S["carried"], 2 * it + 2)
                pool.sem_inc(S["h2_free"], 1)

        @block.tensor
        def _(pe):
            def turn(src, dst, out_sem):
                dv = dst[:].rearrange("p (c t) -> p c t", c=CE)
                for ce in range(CE):
                    for t in range(TT):
                        last = pe.transpose(dv[:, ce, t * P:(t + 1) * P], src[:, t, ce * P:(ce + 1) * P], g["ident"][:])
                last.then_inc(out_sem, 1)

            def turn_o(it, r, tiles):
                pe.wait_ge(o_in[r], 16 * it + 16)
                for t in tiles:
                    pe.wait_ge(turn_taken[t % 2], 4 * it + (2 * r + t // 2) + FREE)
                    for q in range(QB):
                        last = pe.transpose(big[t % 2][:, q * P:(q + 1) * P], os_[r][:, q, t * P:(t + 1) * P], g["ident"][:])
                    last.then_inc(S["turned"], 1)

            def wo(it, r):
                pe.wait_ge(S["aT_ready"], 2 * it + (r + 1))
                gv = gen[r][:].rearrange("p (t e) -> p t e", t=TT)
                for t in range(TT):
                    for ce in range(CE):
                        last = pe.matmul(gv[:, t, :], aT[r][:, ce, t * P:(t + 1) * P], wog[:, ce, :], start=(ce == 0), stop=(ce == CE - 1))
                last.then_inc(S["wo_ps"], 1)

            def logits(it, r):
                pe.wait_ge(S["hT_ready"], 2 * it + (r + 1))
                for t in range(TT):
                    for ce in range(CE):
                        last = pe.matmul(gen[r][:, t * NEXP:(t + 1) * NEXP], hT[r][:, ce, t * P:(t + 1) * P], g["rT"][:, ce, :], start=(ce == 0), stop=(ce == CE - 1))
                last.then_inc(S["lg_ps"], 1)

            def rank(it, r):
                pe.wait_ge(S["both_ready"], 2 * it + (r + 1))
                rk = gen[r][:, BLK:BLK + TT * NEXP].rearrange("p (t n) -> p t n", t=TT)
                pe.matmul(rk, tri[:], both[r][:], start=True, stop=False)
                for t in range(TT - 1):
                    pe.matmul(rk[:, t + 1:TT, :], ones[:], both[r][:, t:t + 1, :].broadcast_to((P, TT - 1 - t, NEXP)), start=False, stop=False)
                pe.matmul(rk, ones[:], seen[r][:].rearrange("p (o n) -> p o n", o=1).broadcast_to((P, TT, NEXP)), start=False, stop=True).then_inc(S["rank_ps"], 1)

            def body(it, more):
                if more:
                    turn_o(it + 1, 0, (0, 1))
                pe.wait_ge(S["rank_taken"], 2 * it + FREE)
                for r in range(2):
                    pe.wait_ge(S["an_ready"], 2 * it + (r + 1))
                    turn(an[r], gen[r], S["aT_ps"])
                    if r == 0:
                        pe.wait_ge(S["wog_ready"], it + 1)
                    elif more:
                        turn_o(it + 1, 0, (2, 3))
                    wo(it, r)
                if more:
                    turn_o(it + 1, 1, (0, 1))
                for r in range(2):
                    pe.wait_ge(S["h2_ready"], 2 * it + (r + 1))
                    turn(h2[r], gen[r], S["hT_ps"])
                    if more and r == 0:
                        turn_o(it + 1, 1, (2,))
                logits(it, 0)
                if more:
                    turn_o(it + 1, 1, (3,))
                logits(it, 1)
                for r in range(2):
                    rank(it, r)

            pe.wait_ge(S["tri_ready"], 1)
            for r in range(2):
                turn_o(0, r, range(TT))
            with pe.Fori(0, B - 1) as it:
                body(it, True)
            body(B - 1, False)
            pe.wait_ge(S["pos_ready"], 2 * B)
            pe.matmul(big[0][:, 0:NEXP], ones[:], seen[0][:], start=True, stop=True).then_inc(S["count_ps"], 1)

        @block.scalar
        def _(act):
            with act.Fori(0, B) as it:
                for r in range(2):
                    act.wait_ge(S["cl_ready"], 2 * it + r + 1)
                    act.activation(flat(tmp[r]), flat(tmp[r]), ACT.Square).then_inc(S["sq_ready"], 1)
                for r in range(2):
                    act.wait_ge(S["sse_ready"], 2 * it + r + 1)
                    act.activation(root[r][:], sse[r][:], ACT.Sqrt, scale=ROOT_SCALE * ROOT_SCALE * 4).then_inc(S["root_ready"], 1)
                for r in range(2):
                    act.wait_ge(S["aT_ps"], 2 * it + r + 1)
                    act.activation(aT[r][:].rearrange("p c t -> p (c t)"), gen[r][:], ACT.Copy).then_inc(S["aT_ready"], 1)
                for r in range(2):
                    act.wait_ge(S["shift_ready"], 2 * it + r + 1)
                    for t in range(TT):
                        last = act.activation(tmp[r][:, t, :], x1[r][:, t, :], ACT.Identity, bias=shift[r][:, t:t + 1], scale=rstd[r][:, t:t + 1])
                    last.then_inc(S["xn_ready"], 1)
                for r in range(2):
                    act.wait_ge(S["hT_ps"], 2 * it + r + 1)
                    act.activation(hT[r][:].rearrange("p c t -> p (c t)"), gen[r][:], ACT.Copy).then_inc(S["hT_ready"], 1)

        @block.vector
        def _(dve):
            wide = (P, TT, E)
            heads = (P, TT * HEADS, 16)
            first_row, iota, count = g["first_row"], g["iota"], g["count"]
            dve.wait_ge(S["iota_ready"], 1)
            dve.tensor_scalar(first_row[:], iota[:], float(CAP), None, ALU.mult)
            init = Steps(dve, S["tables_step"])
            init.done(dve.memset(seen[0][:], 0.0))
            def join(it, r, tiles, st):
                n = 2 * it + r
                for t in tiles:
                    dve.wait_ge(S["turned"], 2 * TT * it + (r * TT + t + 1))
                    tv = big[t % 2][:].rearrange("p (f c) -> p f c", c=32)
                    st.done(dve.reciprocal(rec[:], tv[:, :, 16]))
                    st.done(dve.tensor_tensor(rl[:].rearrange("p (h a) -> p h a", a=2), rec[:].rearrange("p (h a) -> p h a", a=2),
                                              g["lam_sign"][:].rearrange("p (o a) -> p o a", o=1).broadcast_to((P, HEADS, 2)), ALU.mult))
                    dve.tensor_tensor(A[:], tv[:, :, 0:16], rl[:].rearrange("p (f o) -> p f o", o=1).broadcast_to((P, 32, 16)), ALU.mult).then_inc(turn_taken[t % 2], 1)
                    dve.wait_ge(turn_taken[t % 2], 4 * it + (2 * r + t // 2 + 1) + FREE)
                    av = A[:].rearrange("p (h a) c -> p h a c", a=2)
                    st.done(dve.tensor_tensor(D[r][:, t * HEADS:(t + 1) * HEADS, :], av[:, :, 0, :], av[:, :, 1, :], ALU.add))

            def add(it, r, st):
                n = 2 * it + r
                dve.wait_ge(S["wo_ps"], n + 1 + FREE)
                dve.wait_ge(x_in[r], 16 * it + 16)
                dve.wait_ge(x1_kept[r], 16 * it + FREE)
                dve.tensor_tensor(x1[r][:], gen[r][:].rearrange("p (t e) -> p t e", t=TT), xs[r][:], ALU.add).then_inc(S["x_added"], 1)
                dve.wait_ge(S["x_added"], n + 1)
                for t in range(TT):
                    ins = dve.bn_stats(stats[:, t, :], x1[r][:, t, :])
                st.done(ins)
                dve.memset(carry[:], 0.0)
                for t in range(TT):
                    ins = dve.bn_aggr(mv[r][:, t, :], stats[:, t, :])
                st.done(ins)
                dve.tensor_scalar(vare[r][:], mv[r][:, :, 1], EPS, None, ALU.add).then_inc(S["var_ready"], 1)

            def choose(it, r, st):
                n = 2 * it + r
                dve.wait_ge(S["lg_ps"], n + 1)
                st.done(dve.tensor_copy(lg[:].rearrange("p t n -> p (t n)"), gen[r][:, 0:TT * NEXP]))
                dve.memset(carry[:], 0.0)
                for t in range(TT):
                    ins = dve.max(top8[:, t, :], lg[:, t, :])
                st.done(ins)
                dve.memset(carry[:], 0.0)
                for t in range(TT):
                    ins = dve.max_index(idx8[:, t, :], top8[:, t, :], lg[:, t, :])
                st.done(ins)
                dve.wait_ge(cho_kept[r], 16 * it + FREE)
                dve.tensor_copy(cho[r][:, 2], top8[:, :, 0:2].rearrange("p t k -> p k t"))
                st.done(dve.tensor_copy(cho[r][:, 1], idx8[:, :, 0:2].rearrange("p t k -> p k t")))
                for k in range(2):
                    ins = dve.tensor_tensor(hot[r][:, k], iota[:].rearrange("p (o n) -> p o n", o=1).broadcast_to((P, TT, NEXP)),
                                            cho[r][:, 1, k, :].rearrange("p (t o) -> p t o", o=1).broadcast_to((P, TT, NEXP)), ALU.is_equal)
                st.done(ins)
                dve.tensor_tensor(both[r][:], hot[r][:, 0], hot[r][:, 1], ALU.add).then_inc(S["both_ready"], 1)
                dve.wait_ge(S["both_ready"], n + 1)
                st.done(dve.reduce_sum(msum[:], both[r][:].rearrange("p t n -> p n t"), axis=AX.X))
                dve.wait_ge(S["rank_ps"], n + FREE)
                st.done(dve.tensor_tensor(seen[1 - r][:], seen[r][:], msum[:], ALU.add))
                st.done(dve.memset(carry[:], 0.0))

            def body(it, more, st):
                dve.wait_ge(S["modb_in"], 16 * it + 16)
                dve.wait_ge(S["wo_ps"], 2 * it + FREE)
                dve.tensor_tensor(wog[:], g["wT"]["wo"][:], modb[:, 0:1, :].broadcast_to((P, CE, E)), ALU.mult).then_inc(S["wog_ready"], 1)
                for r in range(2):
                    tflat = tmp[r][:].rearrange("p t (h c) -> p (t h) c", c=16)
                    st.done(dve.tensor_scalar(tflat, D[r][:], 1.0 / 8, RANGE, ALU.mult, ALU.min))
                    dve.tensor_scalar(tflat, tflat, -RANGE, None, ALU.max).then_inc(S["cl_ready"], 1)
                for r in range(2):
                    tflat = tmp[r][:].rearrange("p t (h c) -> p (t h) c", c=16)
                    dve.wait_ge(S["sq_ready"], 2 * it + r + 1)
                    st.done(dve.reduce_sum(ss[r][:], tflat, axis=AX.X))
                    dve.tensor_scalar(sse[r][:], ss[r][:], EPS / 4, RANGE * RANGE, ALU.add, ALU.min).then_inc(S["sse_ready"], 1)
                for r in range(2):
                    anf = an[r][:].rearrange("p t (h c) -> p (t h) c", c=16)
                    dve.wait_ge(S["root_ready"], 2 * it + r + 1)
                    st.done(dve.reciprocal(rs[r][:], root[r][:]))
                    st.done(dve.tensor_tensor(nt[:], sse[r][:], rs[r][:], ALU.mult))
                    st.done(dve.tensor_tensor(nt[:], nt[:], rs[r][:], ALU.mult))
                    st.done(dve.tensor_scalar(nt[:], nt[:], -2.0 * ROOT_SCALE * ROOT_SCALE, 1.5, ALU.mult, ALU.add))
                    st.done(dve.tensor_tensor(rs[r][:], rs[r][:], nt[:], ALU.mult))
                    st.done(dve.scalar_tensor_tensor(rs[r][:], ss[r][:], RANGE * RANGE, rs[r][:], ALU.is_lt, ALU.mult))
                    dve.tensor_tensor(anf, D[r][:], rs[r][:].rearrange("p (f o) -> p f o", o=1).broadcast_to(heads), ALU.mult).then_inc(S["an_ready"], 1)
                if more:
                    join(it + 1, 0, (0, 1), st)
                add(it, 0, st)
                if more:
                    join(it + 1, 0, (2, 3), st)
                add(it, 1, st)
                for r in range(2):
                    n = 2 * it + r
                    dve.wait_ge(S["rstd_ready"], n + 1)
                    dve.scalar_tensor_tensor(shift[r][:], mv[r][:, :, 0], -1.0, rstd[r][:], ALU.mult, ALU.mult).then_inc(S["shift_ready"], 1)
                if more:
                    join(it + 1, 1, (0,), st)
                for r in range(2):
                    n = 2 * it + r
                    dve.wait_ge(S["xn_ready"], n + 1)
                    st.done(dve.tensor_tensor(tmp[r][:], tmp[r][:], modb[:, 2:3, :].broadcast_to(wide), ALU.mult))
                    dve.wait_ge(S["h2_free"], it + FREE)
                    dve.tensor_tensor(h2[r][:], tmp[r][:], modb[:, 1:2, :].broadcast_to(wide), ALU.add).then_inc(S["h2_ready"], 1)
                if more:
                    join(it + 1, 1, (1, 2), st)
                choose(it, 0, st)
                if more:
                    join(it + 1, 1, (3,), st)
                choose(it, 1, st)
                for r in range(2):
                    n = 2 * it + r
                    dve.wait_ge(S["rank_ps"], n + 1 + FREE)
                    rk = gen[r][:, BLK:BLK + TT * NEXP].rearrange("p (t n) -> p t n", t=TT)
                    dve.tensor_tensor(slotr[:], rk, first_row[:].rearrange("p (o n) -> p o n", o=1).broadcast_to((P, TT, NEXP)), ALU.add).then_inc(S["rank_taken"], 1)
                    dve.wait_ge(S["rank_taken"], n + 1 + FREE)
                    for k in range(2):
                        ins = dve.tensor_tensor(prod[:, k], hot[r][:, k], slotr[:], ALU.mult)
                    st.done(ins)
                    st.done(dve.reduce_sum(cho[r][:, 0], prod[:], axis=AX.X))
                    dve.tensor_copy(pos[r][:], cho[r][:, 0].rearrange("p k t -> p (k t)")).then_inc(S["pos_ready"], 1)
                    st.done(dve.memset(carry[:], 0.0))

            first = Steps(dve, S["v_step"])
            for r in range(2):
                join(0, r, range(TT), first)
            assert first.n == JOIN_STEPS
            with dve.Fori(0, B - 1) as it:
                st = Steps(dve, S["v_step"], V_STEPS * it + JOIN_STEPS)
                body(it, True, st)
                assert st.n == V_STEPS, (st.n, V_STEPS)
            body(B - 1, False, Steps(dve, S["v_step"], V_STEPS * (B - 1) + JOIN_STEPS))

            tailf, ntile, ncum, ef, mf, jf = (sb(c, f"m_{n}", [P, k]) for n, k in
                                              (("tailf", NEXP), ("ntile", NEXP), ("ncum", NEXP), ("ef", NTAB), ("mf", NTAB), ("jf", NTAB)))
            ntilei = sb(c, "m_ntilei", [P, NEXP], I32)
            ge, gc = sb(c, "m_ge", [P, NTAB, NEXP]), sb(c, "m_gc", [P, NTAB, NEXP])
            e = init
            dve.wait_ge(S["count_ps"], 1)
            e.done(dve.tensor_copy(count[:], big[0][:, 0:NEXP]))
            e.done(dve.tensor_tensor(tailf[:], count[:], first_row[:], ALU.add))
            e.done(dve.tensor_copy(g["tail"][:], tailf[:]))
            e.done(dve.tensor_scalar(ntile[:], count[:], float(P - 1), None, ALU.add))
            e.done(dve.tensor_copy(ntilei[:], ntile[:]))
            e.done(dve.tensor_scalar(ntilei[:], ntilei[:], P.bit_length() - 1, None, ALU.arith_shift_right))
            e.done(dve.tensor_copy(ntile[:], ntilei[:]))
            e.done(dve.tensor_copy(ncum[:], ntile[:]))
            for n in range(1, NEXP):
                e.done(dve.tensor_tensor(ncum[:, n:n + 1], ncum[:, n:n + 1], ncum[:, n - 1:n], ALU.add))
            e.done(dve.tensor_tensor(ntile[:], ncum[:], ntile[:], ALU.subtract))
            e.done(dve.scalar_tensor_tensor(g["close_up"][:], ntile[:], float(P), first_row[:], ALU.mult, ALU.subtract))
            e.done(dve.tensor_copy(jf[:], iotai[:]))
            nb = ncum[:].rearrange("p (o n) -> p o n", o=1).broadcast_to((P, NTAB, NEXP))
            jb = jf[:].rearrange("p (j o) -> p j o", o=1).broadcast_to((P, NTAB, NEXP))
            e.done(dve.tensor_tensor(ge[:], jb, nb, ALU.is_ge))
            e.done(dve.reduce_sum(ef[:], ge[:], axis=AX.X))
            e.done(dve.tensor_tensor(gc[:], ge[:], nb, ALU.mult))
            e.done(dve.reduce_max(mf[:], gc[:], AX.X))
            e.done(dve.tensor_tensor(mf[:], jf[:], mf[:], ALU.subtract))
            e.done(dve.tensor_scalar(mf[:], mf[:], float(P), None, ALU.mult))
            e.done(dve.scalar_tensor_tensor(mf[:], ef[:], float(CAP), mf[:], ALU.mult, ALU.add))
            e.done(dve.tensor_scalar(mf[:], mf[:], float(NEXP * CAP), None, ALU.min))
            e.done(dve.tensor_scalar(ef[:], ef[:], float(NEXP - 1), None, ALU.min))
            dve.tensor_copy(g["row_of"][:], mf[:])
            dve.tensor_copy(g["expert_of"][:], ef[:]).then_inc(S["tables_ready"], 1)


def experts(nc, sb, pb, sem, g):
    with ExitStack() as c:
        def many(make, name, shape, n=2, dt=FP32):
            return [make(c, f"{name}{r}", shape, dt) for r in range(n)]

        zrows = sb(c, "e_zrows", [P, E])
        xt = many(sb, "e_x", [P, E], NX)
        xT = many(sb, "e_xT", [P, CE, P])
        w1t = many(sb, "e_w1", [P, CE, HID])
        rl = many(sb, "e_relu", [P, CH, P])
        hT = many(sb, "e_hT", [P, CH, P])
        ys = many(sb, "e_y", [P, E], NX)
        cho = sb(c, "c_cho", [P, 2 * B, 3, 2 * TT])
        hot = sb(c, "c_hot", [P, 2 * TT, NEXP])
        shift = sb(c, "c_shift", [P, 2 * B, 2 * TT])
        posall = sb(c, "c_posall", [P, 2 * B, 2 * TT], U32)
        wt = sb(c, "c_wt", [P, 2 * B, 2, TT])
        ediff = sb(c, "c_ediff", [P, 2 * B, TT])
        pos = many(sb, "c_pos", [P, 2 * TT], dt=U32)
        wcur = many(sb, "c_wcur", [P, 2, TT])
        x1 = many(sb, "c_x1", [P, TT, E])
        yk = many(sb, "c_yk", [P, 2, TT, E])
        modb = many(sb, "c_gb", [P, E])
        z = sb(c, "c_z", [P, TT, E])
        og = many(sb, "c_out", [P, TT, E])
        pcarry = sb(c, "c_pcarry", [P, 2])
        xps = many(pb, "e_xps", [P, 512])
        hps = many(pb, "e_hps", [P, HID])
        yps = many(pb, "e_yps", [P, 512])

        def sems(name, n=2):
            return [sem(c, f"e_{name}{r}") for r in range(n)]

        x_in, y_stored = sems("x_in", NX), sems("y_stored", NX)
        x_turned, xT_ready, w1_ready, hid_ps, relu_done, hT_ready, y_ps, y_ready = (
            sems(n) for n in ("x_turned", "xT_ready", "w1_ready", "hid_ps", "relu_done", "hT_ready", "y_ps", "y_ready"))
        z_ready, z_stored, cho_in, d_step, diff_ready, exp_ready, rows_written = (
            sem(c, f"e_{n}") for n in ("z_ready", "z_stored", "cho_in", "d_step", "diff_ready", "exp_ready", "rows_written"))
        in_, fetched, out_ready, stored = (sems(n) for n in ("in", "fetched", "out_ready", "stored"))
        picked, carried, v_step = sem(c, "e_picked"), sem(c, "e_carried"), sem(c, "e_v_step")
        block = c.enter_context(nc.Block())
        rows_of = lambda t, v: t[bass.ds(v, P), :]
        ov = g["out"].rearrange("b (u t p) e -> b u p t e", u=2, p=P)
        FREE = 1
        ROUNDS = NTILE // NX
        V_STEPS = 2 * (2 * TT + 1)

        @block.gpsimd
        def _(pool):
            pool.memset(zrows[:], 0.0).then_inc(z_ready, 1)
            for s_ in (*x_turned, *xT_ready, *hid_ps, *relu_done, *hT_ready, *y_ps, *y_ready, *y_stored, *out_ready, *stored):
                pool.sem_inc(s_, FREE)
            pool.wait_ge(rows_written, 1)
            with pool.Fori(0, B) as it:
                for r in range(2):
                    pool.wait_ge(picked, 2 * it + r + 1)
                    pool.wait_ge(out_ready[r], it + FREE)
                    pool.tensor_tensor(pcarry[:, r:r + 1], g["neg_half"][:, 0:1], g["neg_half"][:, 0:1], ALU.mult).then_inc(carried, 1)
                    for k in range(2):
                        for t in range(TT):
                            pool.indirect_dma_start(out=yk[r][:, k, t, :], out_offset=None, in_=g["yg"],
                                                    in_offset=bass.IndirectOffsetOnAxis(ap=pos[r][:, k * TT + t:k * TT + t + 1], axis=0)).then_inc(fetched[r], 16)
                pool.wait_ge(carried, 2 * it + 2)

        @block.sync
        def _(sp):
            def load(s, j, n):
                row = g["first_rows"][j] if isinstance(j, int) else sp.value_load(g["row_of"][0:1, bass.ds(j, 1)], min_val=0, max_val=NEXP * CAP)
                if not (isinstance(n, int) and n == 0):
                    sp.wait_ge(x_turned[s % 2], (NX // 2) * (n - 1) + (s // 2 + 1) + FREE)
                sp.dma_start(xt[s][:], rows_of(g["xg"], row)).then_inc(x_in[s], 16)

            sp.wait_ge(z_ready, 1)
            for n in range(NEXP):
                sp.dma_start(rows_of(g["xg"], g["tails"][n]), zrows[:]).then_inc(z_stored, 16)
            sp.dma_start(g["xg"][NEXP * CAP:NEXP * CAP + P, :], zrows[:]).then_inc(z_stored, 16)
            sp.dma_start(cho[:].rearrange("p b a k -> p b (a k)"), g["chod"].rearrange("b p n -> p b n")).then_inc(cho_in, 16)
            sp.wait_ge(z_stored, 16 * (NEXP + 1))
            for s in range(NX):
                load(s, s, 0)
            with sp.Fori(0, ROUNDS) as it:
                for s in range(NX):
                    load(s, NX * it + (s + NX), it + 1)
                    sp.wait_ge(y_ready[s % 2], (NX // 2) * it + (s // 2 + 1) + FREE)
                    sp.dma_start(rows_of(g["yg"], it * (NX * P) + s * P), ys[s][:]).then_inc(y_stored[s], 16)
            for s in range(NX):
                sp.wait_ge(y_stored[s], 16 * ROUNDS + FREE)
            sp.sem_inc(rows_written, 1)
            with sp.Fori(0, B) as it:
                for r in range(2):
                    sp.wait_ge(out_ready[r], it + FREE)
                    sp.dma_start(x1[r][:].rearrange("p t e -> p (t e)"), g["x1d"][bass.ds(2 * it + r, 1)].rearrange("a p n -> (a p) n")).then_inc(in_[r], 16)
                    sp.dma_start(modb[r][:], g["modd"][bass.ds(it, 1), 5 * E:6 * E].broadcast_to((P, E))).then_inc(in_[r], 16)

        @block.tensor
        def _(pe):
            def expert(j):
                return pe.value_load(g["expert_of"][0:1, bass.ds(j, 1)], min_val=0, max_val=NEXP - 1)

            def turn_x(s, rounds):
                q = s % 2
                pe.wait_ge(x_in[s], 16 * rounds + 16)
                if not (isinstance(rounds, int) and rounds == 0 and s < 2):
                    pe.wait_ge(xT_ready[q], (NX // 2) * rounds + s // 2 + FREE)
                for ce in range(CE):
                    last = pe.transpose(xps[q][:, ce * P:(ce + 1) * P], xt[s][:, ce * P:(ce + 1) * P], g["ident"][:])
                last.then_inc(x_turned[q], 1)

            def hidden(s, rounds):
                q, n = s % 2, (NX // 2) * rounds + s // 2
                pe.wait_ge(w1_ready[q], n + 1)
                pe.wait_ge(xT_ready[q], n + 1 + FREE)
                pe.wait_ge(relu_done[q], n + FREE)
                for m in range(CH):
                    for ce in range(CE):
                        last = pe.matmul(hps[q][:, m * P:(m + 1) * P], w1t[q][:, ce, m * P:(m + 1) * P],
                                         xT[q][:, ce, :], start=(ce == 0), stop=(ce == CE - 1))
                last.then_inc(hid_ps[q], 1)

            def outputs(s, rounds, e):
                q, n = s % 2, (NX // 2) * rounds + s // 2
                pe.wait_ge(hT_ready[q], n + 1 + FREE)
                pe.wait_ge(y_ready[q], n + FREE)
                for m in range(CH):
                    last = pe.matmul(yps[q][:, 0:E], hT[q][:, m, :], g["w2s"][:, bass.ds(e, 1), m, :].rearrange("p a e -> p (a e)"), start=(m == 0), stop=(m == CH - 1))
                last.then_inc(y_ps[q], 1)

            pe.wait_ge(g["w_loaded"], 32 * NEXP)
            turn_x(0, 0)
            hidden(0, 0)
            turn_x(1, 0)
            with pe.Fori(0, ROUNDS) as it:
                es = [expert(NX * it + s) for s in range(NX)]
                for s in range(NX):
                    hidden((s + 1) % NX, it + (s + 1) // NX)
                    turn_x((s + 2) % NX, it + (s + 2) // NX)
                    outputs(s, it, es[s])

        @block.scalar
        def _(act):
            def keep_x(s, rounds):
                q, n = s % 2, (NX // 2) * rounds + s // 2
                act.wait_ge(x_turned[q], n + 1 + FREE)
                act.wait_ge(hid_ps[q], n + FREE)
                act.activation(xT[q][:].rearrange("p c t -> p (c t)"), xps[q][:, 0:E], ACT.Copy).then_inc(xT_ready[q], 1)

            def weights(s, rounds, e):
                q, n = s % 2, (NX // 2) * rounds + s // 2
                act.wait_ge(hid_ps[q], n + FREE)
                act.activation(w1t[q][:].rearrange("p c h -> p (c h)"), g["w1s"][:, bass.ds(e, 1)].rearrange("p a c h -> p (a c h)"), ACT.Copy).then_inc(w1_ready[q], 1)

            def expert(j):
                at = g["expert_of"][0:1, j:j + 1] if isinstance(j, int) else g["expert_of"][0:1, bass.ds(j, 1)]
                return act.value_load(at, min_val=0, max_val=NEXP - 1)

            act.wait_ge(g["w_loaded"], 32 * NEXP)
            weights(0, 0, expert(0))
            weights(1, 0, expert(1))
            keep_x(0, 0)
            keep_x(1, 0)
            act.wait_ge(diff_ready, 1)
            act.activation(ediff[:], ediff[:], ACT.Exp).then_inc(exp_ready, 1)
            with act.Fori(0, ROUNDS) as it:
                es = [expert(NX * it + (s + 2)) for s in range(NX)]
                for s in range(NX):
                    q, n = s % 2, (NX // 2) * it + s // 2
                    act.wait_ge(relu_done[q], n + 1 + FREE)
                    act.wait_ge(y_ps[q], n + FREE)
                    act.activation(hT[q][:].rearrange("p c t -> p (c t)"), rl[q][:].rearrange("p c t -> p (c t)"), ACT.Square).then_inc(hT_ready[q], 1)
                    keep_x((s + 2) % NX, it + (s + 2) // NX)
                    weights((s + 2) % NX, it + (s + 2) // NX, es[s])
            with act.Fori(0, B) as it:
                for r in range(2):
                    act.wait_ge(out_ready[r], it + 1 + FREE)
                    act.dma_start(ov[bass.ds(it, 1), r].rearrange("a p t e -> (a p) t e"), og[r][:]).then_inc(stored[r], 16)
            for r in range(2):
                act.wait_ge(stored[r], 16 * B + FREE)

        @block.vector
        def _(dve):
            def relu(s, rounds):
                q, n = s % 2, (NX // 2) * rounds + s // 2
                dve.wait_ge(hid_ps[q], n + 1 + FREE)
                dve.wait_ge(hT_ready[q], n + FREE)
                dve.tensor_scalar(rl[q][:].rearrange("p c t -> p (c t)"), hps[q][:], 0.0, None, ALU.max).then_inc(relu_done[q], 1)

            relu(0, 0)
            d = Steps(dve, d_step)
            dve.wait_ge(cho_in, 16)
            lgt = cho[:, :, 2, :].rearrange("p b (k t) -> p b k t", k=2)
            dve.tensor_tensor(ediff[:], lgt[:, :, 1, :], lgt[:, :, 0, :], ALU.subtract).then_inc(diff_ready, 1)
            row = lambda v: v[:].rearrange("p (o n) -> p o n", o=1).broadcast_to((P, 2 * TT, NEXP))
            for b in range(2 * B):
                d.done(dve.tensor_tensor(hot[:], row(g["iota"]), cho[:, b, 1, :].rearrange("p (m o) -> p m o", o=1).broadcast_to((P, 2 * TT, NEXP)), ALU.is_equal))
                d.done(dve.tensor_tensor(hot[:], hot[:], row(g["close_up"]), ALU.mult))
                d.done(dve.reduce_sum(shift[:, b, :], hot[:], axis=AX.X))
            d.done(dve.tensor_tensor(posall[:], cho[:, :, 0, :], shift[:], ALU.add))
            dve.wait_ge(exp_ready, 1)
            d.done(dve.tensor_scalar(shift[:, :, 0:TT], ediff[:], 1.0, None, ALU.add))
            d.done(dve.reciprocal(wt[:, :, 0, :], shift[:, :, 0:TT]))
            d.done(dve.tensor_tensor(wt[:, :, 1, :], ediff[:], wt[:, :, 0, :], ALU.mult))
            with dve.Fori(0, ROUNDS) as it:
                for s in range(NX):
                    q, n = s % 2, (NX // 2) * it + s // 2
                    relu((s + 1) % NX, it + (s + 1) // NX)
                    dve.wait_ge(y_ps[q], n + 1 + FREE)
                    dve.wait_ge(y_stored[s], 16 * it + FREE)
                    dve.tensor_copy(ys[s][:], yps[q][:, 0:E]).then_inc(y_ready[q], 1)

            def pick(it, r):
                blk = (lambda v: v[:, it * 2 + r]) if isinstance(it, int) else (lambda v: v[:, bass.ds(2 * it + r, 1)])
                dve.tensor_copy(wcur[r][:].rearrange("p k t -> p (k t)"), blk(wt[:].rearrange("p b k t -> p b (k t)")))
                dve.tensor_copy(pos[r][:], blk(posall)).then_inc(picked, 1)

            for r in range(2):
                pick(0, r)

            def weigh(it, r, st):
                dve.wait_ge(picked, 2 * it + (r + 1))
                dve.wait_ge(in_[r], 32 * it + 32)
                dve.wait_ge(fetched[r], 16 * 2 * TT * (it + 1))
                for t in range(TT):
                    st.done(dve.tensor_scalar(z[:, t, :], yk[r][:, 0, t, :], wcur[r][:, 0, t:t + 1], None, ALU.mult))
                for t in range(TT):
                    st.done(dve.scalar_tensor_tensor(z[:, t, :], yk[r][:, 1, t, :], wcur[r][:, 1, t:t + 1], z[:, t, :], ALU.mult, ALU.add))
                st.done(dve.tensor_tensor(z[:], z[:], modb[r][:].rearrange("p (o e) -> p o e", o=1).broadcast_to((P, TT, E)), ALU.mult))
                dve.wait_ge(stored[r], 16 * it + FREE)
                dve.tensor_tensor(og[r][:], z[:], x1[r][:], ALU.add).then_inc(out_ready[r], 1)
                dve.wait_ge(out_ready[r], it + 1 + FREE)

            with dve.Fori(0, B - 1) as it:
                st = Steps(dve, v_step, V_STEPS * it)
                for r in range(2):
                    weigh(it, r, st)
                    pick(it + 1, r)
                assert st.n == V_STEPS, st.n
            st = Steps(dve, v_step, V_STEPS * (B - 1))
            for r in range(2):
                weigh(B - 1, r, st)


_INS = ['L0_attn_query', 'L0_attn_Wq', 'L0_attn_Wk', 'L0_attn_Wv', 'L0_attn_Wo', 'L0_attn_lambda_q1', 'L0_attn_lambda_k1',
        'L0_attn_lambda_q2', 'L0_attn_lambda_k2', 'L0_attn_subln_w', 'L0_ffn_router_w', 'L0_ffn_w1', 'L0_ffn_w2', 'L0_c', 'L0_wmod']


def kernel(**inputs):
    import numpy as _np
    import concourse.bacc as _bacc
    from concourse import mybir as _mybir
    from concourse.bass_utils import run_bass_kernel_spmd as _run

    nc = _bacc.Bacc("TRN2", target_bir_lowering=False, num_devices=1)
    arrays, args = {}, []
    for name in _INS:
        a = _np.ascontiguousarray(inputs[name])
        arrays[f"in_{name}"] = a
        args.append(nc.dram_tensor(f"in_{name}", a.shape, _mybir.dt.from_np(a.dtype), kind="ExternalInput").ap())
    args.append(nc.dram_tensor("out_x", (B, T, E), _mybir.dt.float32, kind="ExternalOutput").ap())
    build(nc, *args)
    r = _run(nc, [arrays], core_ids=[0])
    return r.results[0]["out_x"]
```
